# Optimizing a Trainium2 kernel written in Bass

```python
import numpy as np
import jax
import jax.numpy as jnp

def _softmax(x, axis=-1):
    return jax.nn.softmax(x, axis=axis)

def _gelu(x):
    return jax.nn.gelu(x, approximate=True)

def _silu(x):
    return jax.nn.silu(x)

def _sigmoid(x):
    return jax.nn.sigmoid(x)

def _layernorm(x, axis=-1, eps=1e-05):
    m = jnp.mean(x, axis=axis, keepdims=True)
    v = jnp.var(x, axis=axis, keepdims=True)
    return (x - m) / jnp.sqrt(v + eps)

def _scatter_add(tgt, idx, src, axis=0):
    return tgt.at[idx].add(src)

def _segment_sum(src, seg, n):
    return jax.ops.segment_sum(src, seg, n)
kernel_name = 'mk_decoder_preln_d1_seqx_r2_0d7545'

def setup_inputs(seed: int=0):
    np.random.seed(seed)
    _w = jnp.asarray

    def _rec_inputs():
        import jax
        import jax.numpy as jnp
        _rk = jax.random.key(seed)
        x = -0.0003929 + 0.9999 * jax.random.normal(jax.random.fold_in(_rk, 1), (16, 256, 512), jnp.float32)
        _lenS = 256 - jax.random.randint(jax.random.fold_in(_rk, 7), (16,), 0, max(1, 256 // 4) + 1, jnp.int32)
        _lenS2 = 256 - jax.random.randint(jax.random.fold_in(_rk, 8), (16,), 0, max(1, 256 // 4) + 1, jnp.int32)
        _ctx_1024P = jax.random.normal(jax.random.fold_in(_rk, 11), (16, 16, 512), jnp.float32)
        _ctx_1024c = jax.random.dirichlet(jax.random.fold_in(_rk, 511), 0.3 * jnp.ones((16,), jnp.float32), (16, 256))
        _ctx_1024t = jnp.einsum('bsk,bkd->bsd', _ctx_1024c, _ctx_1024P)
        _ctx_1024t = _ctx_1024t * jax.lax.rsqrt(jnp.mean(jnp.square(_ctx_1024t)) + 1e-12) * 0.953939
        ctx_1024 = 2.81802e-05 + 1.00001 * (_ctx_1024t + 0.3 * jax.random.normal(jax.random.fold_in(_rk, 611), (16, 256, 512), jnp.float32))
        fside_BxSxS2_0 = 0.000173663 + 1.0001 * jax.random.normal(jax.random.fold_in(_rk, 12), (16, 256, 256), jnp.float32)
        return (x, ctx_1024, fside_BxSxS2_0)
    x, ctx_1024, fside_BxSxS2_0 = _rec_inputs()

    def _L0_attn_setup():
        import math
        import jax, jax.numpy as jnp
        import numpy as np
        N, T, C = (4, 1024, 512)
        H, HS = (16, 64)
        LAYER_ID, N_LAYERS = (1, 12)
        _EPS = math.exp(-LAYER_ID / N_LAYERS)
        EPS_R = _EPS / 2.0
        EPS_K = _EPS + 0.3 * LAYER_ID / (N_LAYERS - 1)
        EPS_V = _EPS

        def _time_interp(x, eps):
            Tn = x.shape[1]
            curr = jnp.pad(x, ((0, 0), (1, 0), (0, 0)))[:, :Tn]
            prev = jnp.pad(x, ((0, 0), (0, 1), (0, 0)))[:, 1:]
            return eps * curr + (1.0 - eps) * prev
        key = jax.random.key(seed)
        ks = jax.random.split(key, 9)
        s = 1.0 / math.sqrt(C)
        return {'x': jax.random.normal(ks[0], (N, T, C), dtype=jnp.float32), 'Wr': jax.random.normal(ks[1], (H * HS, C), dtype=jnp.float32) * s, 'br': jax.random.normal(ks[2], (H * HS,), dtype=jnp.float32) * 0.01, 'Wk': jax.random.normal(ks[3], (H * HS, C), dtype=jnp.float32) * s, 'bk': jax.random.normal(ks[4], (H * HS,), dtype=jnp.float32) * 0.01, 'Wv': jax.random.normal(ks[5], (H * HS, C), dtype=jnp.float32) * s, 'bv': jax.random.normal(ks[6], (H * HS,), dtype=jnp.float32) * 0.01, 'Wo': jax.random.normal(ks[7], (C, H * HS), dtype=jnp.float32) * s, 'bo': jax.random.normal(ks[8], (C,), dtype=jnp.float32) * 0.01, 'time_decay': jnp.full((H * HS,), 0.1, dtype=jnp.float32), 'U': jnp.full((H * HS,), 0.1, dtype=jnp.float32)}
    _L0_attn_all = _L0_attn_setup()
    _L0_attn_in = {k: v for k, v in _L0_attn_all.items() if k in ('Wr', 'br', 'Wk', 'bk', 'Wv', 'bv', 'Wo', 'bo', 'time_decay', 'U')}
    del _L0_attn_all

    def _L0_xattn_setup():
        import jax, jax.numpy as jnp
        import numpy as np
        B, N, D = (8, 1024, 512)
        NUM_HEADS = 16
        D_HEAD = D // NUM_HEADS
        key = jax.random.key(seed)
        ks = jax.random.split(key, 12)
        s = 1.0 / np.sqrt(D)
        return {'query': jax.random.normal(ks[0], (B, N, D), jnp.float32), 'key': jax.random.normal(ks[1], (B, N, D), jnp.float32), 'value': jax.random.normal(ks[2], (B, N, D), jnp.float32), 'score_matrix': jax.random.normal(ks[3], (B, N, N), jnp.float32), 'Wq': jax.random.normal(ks[4], (D, D), jnp.float32) * s, 'bq': jnp.zeros((D,), jnp.float32), 'Wk': jax.random.normal(ks[5], (D, D), jnp.float32) * s, 'bk': jnp.zeros((D,), jnp.float32), 'Wv': jax.random.normal(ks[6], (D, D), jnp.float32) * s, 'bv': jnp.zeros((D,), jnp.float32), 'Wo': jax.random.normal(ks[7], (D, D), jnp.float32) * s, 'bo': jnp.zeros((D,), jnp.float32)}
    _L0_xattn_all = _L0_xattn_setup()
    _L0_xattn_in = {k: v for k, v in _L0_xattn_all.items() if k in ('Wq', 'bq', 'Wk', 'bk', 'Wv', 'bv', 'Wo', 'bo')}
    del _L0_xattn_all

    def _L0_ffn_setup():
        import jax, jax.numpy as jnp
        import numpy as np
        DIM = 512

        def _reference_tuple_inner(x, W_r, W_k, W_v, mu_r, mu_k):
            B, T, C = x.shape
            x_prev = jnp.concatenate([jnp.zeros((B, 1, C), x.dtype), x[:, :-1, :]], axis=1)
            xr = mu_r * x + (1.0 - mu_r) * x_prev
            xk = mu_k * x + (1.0 - mu_k) * x_prev
            r = jax.nn.sigmoid(jnp.einsum('btc,dc->btd', xr, W_r))
            k = jnp.einsum('btc,dc->btd', xk, W_k)
            k_act = jnp.square(jax.nn.relu(k))
            out = r * jnp.einsum('btc,dc->btd', k_act, W_v)
            new_state = x[:, -1, :]
            return (out, new_state)
        key = jax.random.key(seed)
        ks = jax.random.split(key, 6)
        B, T, C = (8, 1024, DIM)
        x = jax.random.normal(ks[0], (B, T, C), dtype=jnp.float32)
        s = 1.0 / np.sqrt(C)
        W_r = jax.random.uniform(ks[1], (C, C), jnp.float32, -s, s)
        W_k = jax.random.uniform(ks[2], (C, C), jnp.float32, -s, s)
        W_v = jax.random.uniform(ks[3], (C, C), jnp.float32, -s, s)
        mu_r = jax.random.uniform(ks[4], (C,), jnp.float32)
        mu_k = jax.random.uniform(ks[5], (C,), jnp.float32)
        return {'x': x, 'W_r': W_r, 'W_k': W_k, 'W_v': W_v, 'mu_r': mu_r, 'mu_k': mu_k}
    _L0_ffn_all = _L0_ffn_setup()
    _L0_ffn_in = {k: v for k, v in _L0_ffn_all.items() if k in ('W_r', 'W_k', 'W_v', 'mu_r', 'mu_k')}
    del _L0_ffn_all
    return {'x': x, 'ctx_1024': ctx_1024, 'fside_BxSxS2_0': fside_BxSxS2_0, 'L0_attn_Wr': _L0_attn_in['Wr'], 'L0_attn_br': _L0_attn_in['br'], 'L0_attn_Wk': _L0_attn_in['Wk'], 'L0_attn_bk': _L0_attn_in['bk'], 'L0_attn_Wv': _L0_attn_in['Wv'], 'L0_attn_bv': _L0_attn_in['bv'], 'L0_attn_Wo': _L0_attn_in['Wo'], 'L0_attn_bo': _L0_attn_in['bo'], 'L0_attn_time_decay': _L0_attn_in['time_decay'], 'L0_attn_U': _L0_attn_in['U'], 'L0_xattn_Wq': _L0_xattn_in['Wq'], 'L0_xattn_bq': _L0_xattn_in['bq'], 'L0_xattn_Wk': _L0_xattn_in['Wk'], 'L0_xattn_bk': _L0_xattn_in['bk'], 'L0_xattn_Wv': _L0_xattn_in['Wv'], 'L0_xattn_bv': _L0_xattn_in['bv'], 'L0_xattn_Wo': _L0_xattn_in['Wo'], 'L0_xattn_bo': _L0_xattn_in['bo'], 'L0_ffn_W_r': _L0_ffn_in['W_r'], 'L0_ffn_W_k': _L0_ffn_in['W_k'], 'L0_ffn_W_v': _L0_ffn_in['W_v'], 'L0_ffn_mu_r': _L0_ffn_in['mu_r'], 'L0_ffn_mu_k': _L0_ffn_in['mu_k']}

def reference(x, ctx_1024, fside_BxSxS2_0, L0_attn_Wr, L0_attn_br, L0_attn_Wk, L0_attn_bk, L0_attn_Wv, L0_attn_bv, L0_attn_Wo, L0_attn_bo, L0_attn_time_decay, L0_attn_U, L0_xattn_Wq, L0_xattn_bq, L0_xattn_Wk, L0_xattn_bk, L0_xattn_Wv, L0_xattn_bv, L0_xattn_Wo, L0_xattn_bo, L0_ffn_W_r, L0_ffn_W_k, L0_ffn_W_v, L0_ffn_mu_r, L0_ffn_mu_k):
    import jax
    import jax.numpy as jnp

    def _L0_attn_ref(x, Wr, br, Wk, bk, Wv, bv, Wo, bo, time_decay, U):
        import math
        import jax, jax.numpy as jnp
        import numpy as np
        N, T, C = (4, 1024, 512)
        H, HS = (16, 64)
        LAYER_ID, N_LAYERS = (1, 12)
        _EPS = math.exp(-LAYER_ID / N_LAYERS)
        EPS_R = _EPS / 2.0
        EPS_K = _EPS + 0.3 * LAYER_ID / (N_LAYERS - 1)
        EPS_V = _EPS

        def _time_interp(x, eps):
            Tn = x.shape[1]
            curr = jnp.pad(x, ((0, 0), (1, 0), (0, 0)))[:, :Tn]
            prev = jnp.pad(x, ((0, 0), (0, 1), (0, 0)))[:, 1:]
            return eps * curr + (1.0 - eps) * prev
        n, t, c = x.shape
        R = (_time_interp(x, EPS_R) @ Wr.T + br).reshape(n, t, H, HS)
        K = (_time_interp(x, EPS_K) @ Wk.T + bk).reshape(n, t, H, HS)
        V = (_time_interp(x, EPS_V) @ Wv.T + bv).reshape(n, t, H, HS)
        w = jax.nn.relu(time_decay).reshape(1, 1, H, HS)
        t_rem = (t - jnp.arange(1, t + 1, dtype=x.dtype)).reshape(1, t, 1, 1)
        W = -w * t_rem
        e = jnp.exp(jnp.clip(W + K, -20.0, 10.0))
        past_attention = jnp.cumsum(e * V, axis=1)
        past_energy = jnp.cumsum(e, axis=1)
        shift = lambda a: jnp.pad(a, ((0, 0), (1, 0), (0, 0), (0, 0)))[:, :t]
        eu = jnp.exp(jnp.clip(U.reshape(1, 1, H, HS) + K, -20.0, 10.0))
        A = shift(past_attention) + eu * V
        B = shift(past_energy) + eu
        WKV = A / B
        out = (jax.nn.sigmoid(R) * WKV).reshape(n, t, -1) @ Wo.T + bo
        return out

    def _L0_xattn_ref(query, key, value, score_matrix, Wq, bq, Wk, bk, Wv, bv, Wo, bo):
        import jax, jax.numpy as jnp
        import numpy as np
        B, N, D = (8, 1024, 512)
        NUM_HEADS = 16
        D_HEAD = D // NUM_HEADS
        Q = jnp.einsum('bnd,ed->bne', query, Wq) + bq
        K = jnp.einsum('bnd,ed->bne', key, Wk) + bk
        V = jnp.einsum('bnd,ed->bne', value, Wv) + bv
        scores = (jnp.einsum('bqd,bkd->bqk', Q, K) + score_matrix) / jnp.sqrt(jnp.asarray(D_HEAD, jnp.float32))
        weights = jax.nn.softmax(scores, axis=-1)
        out = jnp.einsum('bqk,bkd->bqd', weights, V)
        return jnp.einsum('bnd,ed->bne', out, Wo) + bo

    def _L0_ffn_ref(x, W_r, W_k, W_v, mu_r, mu_k):
        import jax, jax.numpy as jnp
        import numpy as np
        DIM = 512

        def _reference_tuple_inner(x, W_r, W_k, W_v, mu_r, mu_k):
            B, T, C = x.shape
            x_prev = jnp.concatenate([jnp.zeros((B, 1, C), x.dtype), x[:, :-1, :]], axis=1)
            xr = mu_r * x + (1.0 - mu_r) * x_prev
            xk = mu_k * x + (1.0 - mu_k) * x_prev
            r = jax.nn.sigmoid(jnp.einsum('btc,dc->btd', xr, W_r))
            k = jnp.einsum('btc,dc->btd', xk, W_k)
            k_act = jnp.square(jax.nn.relu(k))
            out = r * jnp.einsum('btc,dc->btd', k_act, W_v)
            new_state = x[:, -1, :]
            return (out, new_state)
        return _reference_tuple_inner(x, W_r, W_k, W_v, mu_r, mu_k)[0]
    x = x + _L0_attn_ref(_layernorm(x, axis=-1), L0_attn_Wr, L0_attn_br, L0_attn_Wk, L0_attn_bk, L0_attn_Wv, L0_attn_bv, L0_attn_Wo, L0_attn_bo, L0_attn_time_decay, L0_attn_U)
    x = x + _L0_xattn_ref(_layernorm(x, axis=-1), ctx_1024, ctx_1024, fside_BxSxS2_0, L0_xattn_Wq, L0_xattn_bq, L0_xattn_Wk, L0_xattn_bk, L0_xattn_Wv, L0_xattn_bv, L0_xattn_Wo, L0_xattn_bo)
    x = x + _L0_ffn_ref(_layernorm(x, axis=-1), L0_ffn_W_r, L0_ffn_W_k, L0_ffn_W_v, L0_ffn_mu_r, L0_ffn_mu_k)
    return x

_drawn_inputs = setup_inputs


def setup_inputs(seed=0):
    import zlib

    import numpy as np

    out = dict(_drawn_inputs(seed))
    spreads = {'L0_attn_time_decay': (0.10000000149011612, 0.2),
     'L0_attn_U': (0.10000000149011612, 0.6),
     'L0_xattn_bq': (0.0, 0.1),
     'L0_xattn_bk': (0.0, 0.8),
     'L0_xattn_bv': (0.0, 0.1),
     'L0_xattn_bo': (0.0, 0.1)}
    factors = {'L0_attn_br': 8.0,
     'L0_attn_bk': 8.0,
     'L0_attn_bv': 8.0,
     'L0_attn_bo': 6.124,
     'L0_ffn_W_r': 4.365,
     'L0_ffn_mu_r': 8.0}
    for name, (base, spread) in spreads.items():
        noise = np.random.default_rng([zlib.crc32(name.encode()), seed]).standard_normal(out[name].shape)
        drawn = base * np.exp(spread * noise) if base else spread * noise
        out[name] = jnp.asarray(drawn.astype(out[name].dtype))
    for name, factor in factors.items():
        out[name] = (out[name] * factor).astype(out[name].dtype)
    return out
```

```python
import math
from contextlib import ExitStack

import concourse.bass as bass
from concourse import mybir

F32 = mybir.dt.float32
F32R = mybir.dt.float32r
ALU = mybir.AluOpType
ACT = mybir.ActivationFunctionType
AX = mybir.AxisListType

P = 128
B, T, C = 16, 256, 512
BT = 2
NT = B // BT
N = BT * T
SUB = N // P
KC = C // P
H = 1024
HC = H // P
LN_EPS = 1e-5
EPS = math.exp(-1.0 / 12.0)
MIX = {"k": EPS + 0.3 / 11.0, "v": EPS, "r": EPS / 2.0}
CLIP_LO, CLIP_HI = math.exp(-20.0), math.exp(10.0)
SIG_CAP = 2.0 ** 60
LN_SHIFT = 21
TABLES = "natural_log_exp_and_others"
LAG = 2


def wait(eng, sem, value):
    if not isinstance(value, int) or value > 0:
        eng.wait_ge(sem, value)


def over_tiles(eng, body, tail=1):
    body(0)
    with eng.Fori(1, NT - tail) as i:
        body(i)
    for j in range(NT - tail, NT):
        body(j)


def is_first(i):
    return isinstance(i, int) and i == 0


def is_last(i):
    return isinstance(i, int) and i == NT - 1


def tile_of(dram, i):
    if isinstance(i, int):
        return dram[i * BT:(i + 1) * BT].rearrange("b (h p) c -> p (b h) c", p=P)
    return dram[bass.ds(i * BT, BT)].rearrange("b (h p) c -> p (b h) c", p=P)


def three(pe, out, pairs):
    n = len(pairs)
    for j, ((ah, al), (bh, bl)) in enumerate(pairs):
        pe.matmul(out, ah, bh, start=(j == 0), stop=False)
        pe.matmul(out, ah, bl, start=False, stop=False)
        last = pe.matmul(out, al, bh, start=False, stop=(j == n - 1))
    return last


def attention_pass(nc, x, w_kvr, wo_t, cols, bo_b, trem, scanmask, ident, x1):
    with ExitStack() as ctx:
        def sb(name, shape, dt=F32):
            return ctx.enter_context(nc.sbuf_tensor("a_" + name, shape, dt))

        def sem(name):
            return ctx.enter_context(nc.semaphore("a_" + name))

        WM = "kvr"
        w_hi = {m: sb(f"w{m}_hi", [P, HC, KC * P], F32R) for m in WM}
        w_lo = {m: sb(f"w{m}_lo", [P, HC, KC * P], F32R) for m in WM}
        wo_hi, wo_lo = sb("wo_hi", [P, HC, C], F32R), sb("wo_lo", [P, HC, C], F32R)
        xin = sb("xin", [P, SUB, C])
        xres = sb("xres", [P, SUB, C])
        xt_hi, xt_lo = sb("xt_hi", [P, KC, N], F32R), sb("xt_lo", [P, KC, N], F32R)
        bo_sb, trem_sb, mask_sb = sb("bo", [P, C]), sb("trem", [P, T]), sb("mask", [P, BT * (T + 1)])
        id_sb = sb("ident", [P, P])
        col = sb("col", [P, 5, HC])
        nbr, buk, ebv, negw = (sb(n, [P, HC]) for n in ("nbr", "buk", "ebv", "negw"))
        zero = sb("zero", [P, BT, 2])
        shift = sb("shift", [P, 1])
        stats, mv = sb("stats", [P, SUB, 6]), sb("mv", [P, SUB, 2])
        rstd, half, eps = sb("rstd", [P, SUB]), sb("half", [P, SUB]), sb("eps", [P, SUB])
        u = {m: sb("u" + m, [P, BT, T + 2]) for m in WM}
        kt, vv, eu, euv, rt = (sb(n, [P, BT, T]) for n in ("kt", "vv", "eu", "euv", "rt"))
        ee, ev, ss, sv = (sb(n, [P, BT * (T + 1)]) for n in ("ee", "ev", "ss", "sv"))
        dd, rc, yy = (sb(n, [P, BT, T]) for n in ("dd", "rc", "yy"))
        y_hi, y_lo = sb("y_hi", [P, 2, N], F32R), sb("y_lo", [P, 2, N], F32R)
        two = lambda a: a[:, :].rearrange("p (b t) -> p b t", b=BT)
        ee3, ev3, ss3, sv3 = two(ee), two(ev), two(ss), two(sv)
        flat = lambda a: a[:, :, :].rearrange("p b t -> p (b t)")

        ps = {m: ctx.enter_context(nc.psum_tensor("a_ps" + m, [P, BT, T], F32)) for m in WM}
        acc = [ctx.enter_context(nc.psum_tensor(f"a_acc{s}", [P, C], F32)) for s in range(SUB)]
        tps = ctx.enter_context(nc.psum_tensor("a_tps", [P, N], F32))

        def turn_bank(i, k):
            return acc[k] if is_first(i) else tps

        consts_in, x_in, res_in, stored = sem("consts_in"), sem("x_in"), sem("res_in"), sem("stored")
        stage_in = [sem(f"stage_in{j}") for j in range(4)]
        proj = {m: sem("proj_" + m) for m in WM}
        wo_done, turned, slot_free = sem("wo_done"), sem("turned"), sem("slot_free")
        u_done = {m: sem("u_done_" + m) for m in WM}
        eu_exp, e_exp, r_exp, ln_done, rc_done, yhi_done, xhi_done, whi_done = (
            sem(n) for n in ("eu_exp", "e_exp", "r_exp", "ln_done", "rc_done", "yhi_done", "xhi_done", "whi_done"))
        k_mix, arg_done, v_mix, r_mix, eu_clip, e_clip, ev_done, s_scan, sv_scan = (
            sem(n) for n in ("k_mix", "arg_done", "v_mix", "r_mix", "eu_clip", "e_clip", "ev_done", "s_scan",
                             "sv_scan"))
        t_done, d_done, newton, y_done, ylo_done, xlo_done, st_done, mv_done, normed, res_done, setup = (
            sem(n) for n in ("t_done", "d_done", "newton", "y_done", "ylo_done", "xlo_done", "st_done", "mv_done",
                             "normed", "res_done", "setup"))
        euv_done, b_done, a_done, rd_done, veps_done, rstd_done, bo_added, wlo_done, consts_set = (
            sem(n) for n in ("euv_done", "b_done", "a_done", "rd_done", "veps_done", "rstd_done", "bo_added",
                             "wlo_done", "consts_set"))

        NCONST = 5
        STAGED = 4 * HC

        def piece(n):
            c, m = divmod(n, 4)
            if m == 3:
                return wo_t[c], wo_hi[:, c, :], wo_lo[:, c, :]
            return w_kvr[WM[m]][c], w_hi[WM[m]][:, c, :], w_lo[WM[m]][:, c, :]

        block = ctx.enter_context(nc.Block())

        @block.sync
        def _(sp):
            sp.dma_start(xin[:, :, :], tile_of(x, 0)).then_inc(x_in, 16)
            for dst, src in ((col[:, :, :], cols), (trem_sb[:, :], trem), (mask_sb[:, :], scanmask),
                             (id_sb[:, :], ident), (bo_sb[:, :], bo_b)):
                sp.dma_start(dst, src).then_inc(consts_in, 16)
            for n in range(STAGED):
                if n >= 4:
                    sp.wait_ge(wlo_done, n - 3)
                sp.dma_start(xres[:, n % 4, :], piece(n)[0]).then_inc(stage_in[n % 4], 16)
                if n == 7:
                    sp.wait_ge(turned, KC)
                    sp.dma_start(xin[:, :, :], tile_of(x, 1)).then_inc(x_in, 16)
            sp.wait_ge(wlo_done, STAGED)
            sp.dma_start(xres[:, :, :], tile_of(x, 0)).then_inc(res_in, 16)

            with sp.Fori(1, NT - 1) as i:
                sp.wait_ge(turned, i * KC + KC)
                sp.dma_start(xin[:, :, :], tile_of(x, i + 1)).then_inc(x_in, 16)
                sp.wait_ge(res_done, i * SUB)
                sp.dma_start(tile_of(x1, i - 1), xres[:, :, :]).then_inc(stored, 16)
                sp.wait_ge(stored, i * 16)
                sp.dma_start(xres[:, :, :], tile_of(x, i)).then_inc(res_in, 16)
            for i in (NT - 1, NT):
                sp.wait_ge(res_done, i * SUB)
                sp.dma_start(tile_of(x1, i - 1), xres[:, :, :]).then_inc(stored, 16)
                sp.wait_ge(stored, i * 16)
                if i < NT:
                    sp.dma_start(xres[:, :, :], tile_of(x, i)).then_inc(res_in, 16)

        @block.tensor
        def _(pe):
            te = nc.tensor

            def turn(i, k):
                wait(pe, normed, i * SUB + SUB)
                if not is_first(i):
                    wait(pe, xlo_done, i * KC + k)
                for s in range(SUB):
                    last = te.transpose(turn_bank(i, k)[:, s * P:(s + 1) * P], xin[:, s, k * P:(k + 1) * P], id_sb[:, :])
                last.then_inc(turned, 1)

            def operands(m, c, k):
                w = slice(k * P, (k + 1) * P)
                return ((w_hi[m][:, c, w], w_lo[m][:, c, w]), (xt_hi[:, k, :], xt_lo[:, k, :]))

            def project(i, c):
                g = i * HC + c
                if c < HC - 1:
                    for j, m in enumerate(WM):
                        if is_first(i):
                            pe.wait_ge(wlo_done, 4 * c + j + 1)
                        wait(pe, u_done[m], g)
                        if c == 0 and j == 0:
                            wait(pe, xlo_done, i * KC + KC)
                        three(te, flat(ps[m]), [operands(m, c, k) for k in range(KC)]).then_inc(proj[m], 1)
                    return
                if is_first(i):
                    pe.wait_ge(wlo_done, 4 * c + 3)
                for m in WM:
                    wait(pe, u_done[m], g)
                for k in range(KC):
                    for m in WM:
                        (ah, al), (bh, bl) = operands(m, c, k)
                        te.matmul(flat(ps[m]), ah, bh, start=(k == 0), stop=False)
                        te.matmul(flat(ps[m]), ah, bl, start=False, stop=False)
                        last = te.matmul(flat(ps[m]), al, bh, start=False, stop=(k == KC - 1))
                        if k == KC - 1:
                            last.then_inc(proj[m], 1)
                    if not is_last(i):
                        if k < KC - 1:
                            last.then_inc(slot_free, 1)
                        turn(i + 1, k)

            def output(i, c):
                g = i * HC + c
                if is_first(i):
                    pe.wait_ge(wlo_done, 4 * c + 4)
                wait(pe, ylo_done, g + 1)
                if c == 0:
                    wait(pe, res_done, i * SUB)
                    if is_first(i):
                        pe.wait_ge(xlo_done, KC)
                for s in range(SUB):
                    t = slice(s * P, (s + 1) * P)
                    for a, b in ((y_hi, wo_hi), (y_hi, wo_lo), (y_lo, wo_hi)):
                        last = te.matmul(acc[s][:, :], a[:, c % 2, t], b[:, c, :],
                                         start=(c == 0 and a is y_hi and b is wo_hi),
                                         stop=(c == HC - 1 and a is y_lo))
                last.then_inc(wo_done, 1)

            pe.wait_ge(consts_in, 16 * NCONST)
            for k in range(KC):
                turn(0, k)

            def body(i):
                for c in range(HC):
                    project(i, c)
                    if c >= LAG:
                        output(i, c - LAG)
                    elif not is_first(i):
                        output(i - 1, HC + c - LAG)

            over_tiles(pe, body)
            for c in range(HC - LAG, HC):
                output(NT - 1, c)

        @block.scalar
        def _(act):
            sc = nc.scalar
            sc.preload_act_table_set(TABLES)

            def split_high(n):
                act.wait_ge(stage_in[n % 4], 16 * (n // 4 + 1))
                sc.activation(piece(n)[1], xres[:, n % 4, :], ACT.Copy).then_inc(whi_done, 1)

            def xt_high(i, k):
                wait(act, turned, i * KC + k + 1)
                if not is_first(i):
                    if k < KC - 1:
                        act.wait_ge(slot_free, (i - 1) * (KC - 1) + k + 1)
                    else:
                        act.wait_ge(proj["r"], i * HC)
                sc.activation(xt_hi[:, k, :], turn_bank(i, k)[:, :], ACT.Copy).then_inc(xhi_done, 1)

            def leave(m, i, c):
                g = i * HC + c
                wait(act, {"k": k_mix, "v": v_mix, "r": r_mix}[m], g)
                if m == "v":
                    sc.activation(u["v"][:, :, 0:T + 2:T + 1], zero[:, :, :], ACT.Identity, bias=ebv[:, c:c + 1])
                act.wait_ge(proj[m], g + 1)
                if m == "v":
                    sc.activation(u[m][:, :, 1:T + 1], ps[m][:, :, :], ACT.Identity, bias=ebv[:, c:c + 1],
                                  scale=MIX[m]).then_inc(u_done[m], 1)
                else:
                    sc.activation(u[m][:, :, 1:T + 1], ps[m][:, :, :], ACT.Copy,
                                  scale=MIX[m]).then_inc(u_done[m], 1)

            def exp_k(i, c):
                g = i * HC + c
                act.wait_ge(k_mix, g + 1)
                wait(act, b_done, g)
                sc.activation(eu[:, :, :], kt[:, :, :], ACT.Exp, bias=buk[:, c:c + 1]).then_inc(eu_exp, 1)
                act.wait_ge(arg_done, g + 1)
                sc.activation(ee3[:, :, 1:], ee3[:, :, 1:], ACT.Exp, bias=col[:, 1, c:c + 1]).then_inc(e_exp, 1)

            def exp_r(i, c):
                g = i * HC + c
                act.wait_ge(r_mix, g + 1)
                sc.activation(rt[:, :, :], rt[:, :, :], ACT.Exp, bias=nbr[:, c:c + 1],
                              scale=-1.0).then_inc(r_exp, 1)

            def first_reciprocal(g):
                act.wait_ge(d_done, g + 1)
                wait(act, newton, g)
                sc.activation(rc[:, :, :], dd[:, :, :], ACT.Ln, scale=2.0 ** -LN_SHIFT).then_inc(ln_done, 1)
                act.wait_ge(ln_done, g + 1)
                sc.activation(rc[:, :, :], rc[:, :, :], ACT.Exp, scale=-1.0, bias=shift[:, 0:1]).then_inc(rc_done, 1)

            def y_high(g, c):
                act.wait_ge(y_done, g + 1)
                wait(act, wo_done, g - 1)
                sc.activation(y_hi[:, c % 2, :], flat(yy), ACT.Copy).then_inc(yhi_done, 1)

            for n in range(4):
                split_high(n)
            for k in range(KC):
                xt_high(0, k)
            act.wait_ge(setup, 5)
            act.wait_ge(consts_set, 3)

            def body(i):
                for c in range(HC):
                    g = i * HC + c
                    back = c > 0 or not is_first(i)
                    if is_first(i) and c < HC - 1:
                        for m in range(4):
                            split_high(4 * (c + 1) + m)
                    if c == HC - 1 and not is_last(i):
                        xt_high(i + 1, 0)
                        xt_high(i + 1, 1)
                        first_reciprocal(g - 1)
                        xt_high(i + 1, 2)
                        xt_high(i + 1, 3)
                        y_high(g - 1, c - 1)
                        for m in WM:
                            leave(m, i, c)
                        exp_k(i, c)
                        exp_r(i, c)
                        continue
                    leave("k", i, c)
                    if back:
                        first_reciprocal(g - 1)
                    leave("v", i, c)
                    exp_k(i, c)
                    leave("r", i, c)
                    if back:
                        y_high(g - 1, (c - 1) % HC)
                    exp_r(i, c)

            over_tiles(act, body)
            first_reciprocal(NT * HC - 1)
            y_high(NT * HC - 1, HC - 1)

        @block.vector
        def _(dve):
            ve = nc.vector

            def xt_rest(i, k):
                wait(dve, xhi_done, i * KC + k + 1)
                ve.tensor_tensor(xt_lo[:, k, :], turn_bank(i, k)[:, :], xt_hi[:, k, :].bitcast(F32),
                                 ALU.subtract).then_inc(xlo_done, 1)

            def mix(m, i, c, out, done):
                g = i * HC + c
                dve.wait_ge(u_done[m], g + 1)
                if m == "k":
                    wait(dve, eu_exp, g)
                    wait(dve, arg_done, g)
                if m == "v":
                    wait(dve, euv_done, g)
                    wait(dve, ev_done, g)
                if m == "r":
                    wait(dve, d_done, g)
                ve.scalar_tensor_tensor(out=out[:, :, :], in0=u[m][:, :, 2:], scalar=(1.0 - MIX[m]) / MIX[m],
                                        in1=u[m][:, :, 0:T], op0=ALU.mult, op1=ALU.add).then_inc(done, 1)

            def decayed(i, c):
                g = i * HC + c
                dve.wait_ge(k_mix, g + 1)
                wait(dve, s_scan, g)
                ve.scalar_tensor_tensor(out=ee3[:, :, 1:],
                                        in0=trem_sb[:, :].unsqueeze(1).to_broadcast([P, BT, T]),
                                        scalar=negw[:, c:c + 1], in1=kt[:, :, :],
                                        op0=ALU.mult, op1=ALU.add).then_inc(arg_done, 1)

            def clip_and_scan(g, before_product=None, before_scans=None):
                dve.wait_ge(eu_exp, g + 1)
                ve.tensor_scalar(eu[:, :, :], eu[:, :, :], CLIP_LO, CLIP_HI, ALU.max, ALU.min).then_inc(eu_clip, 1)
                dve.wait_ge(e_exp, g + 1)
                ve.tensor_scalar(ee3[:, :, 1:], ee3[:, :, 1:], CLIP_LO, CLIP_HI, ALU.max, ALU.min).then_inc(e_clip, 1)
                if before_product:
                    before_product()
                dve.wait_ge(e_clip, g + 1)
                wait(dve, sv_scan, g)
                ve.tensor_tensor(ev3[:, :, 1:], ee3[:, :, 1:], vv[:, :, :], ALU.mult).then_inc(ev_done, 1)
                if before_scans:
                    before_scans()
                wait(dve, d_done, g)
                ve.tensor_tensor_scan(ss[:, :], mask_sb[:, :], ee[:, :], 0.0, ALU.mult, ALU.add).then_inc(s_scan, 1)
                dve.wait_ge(ev_done, g + 1)
                wait(dve, y_done, g)
                ve.tensor_tensor_scan(sv[:, :], mask_sb[:, :], ev[:, :], 0.0, ALU.mult, ALU.add).then_inc(sv_scan, 1)

            def one_plus(g):
                dve.wait_ge(r_exp, g + 1)
                ve.tensor_scalar(rt[:, :, :], rt[:, :, :], SIG_CAP, 1.0, ALU.min, ALU.add).then_inc(t_done, 1)

            def denominator(g):
                dve.wait_ge(t_done, g + 1)
                dve.wait_ge(b_done, g + 1)
                wait(dve, rd_done, g)
                ve.tensor_tensor(dd[:, :, :], rt[:, :, :], ss3[:, :, 0:T], ALU.mult).then_inc(d_done, 1)

            def divide(g):
                dve.wait_ge(rd_done, g + 1)
                ve.scalar_tensor_tensor(out=rc[:, :, :], in0=dd[:, :, :], scalar=-2.0, in1=rc[:, :, :],
                                        op0=ALU.add, op1=ALU.mult).then_inc(newton, 1)
                dve.wait_ge(newton, g + 1)
                dve.wait_ge(a_done, g + 1)
                wait(dve, ylo_done, g)
                ve.scalar_tensor_tensor(out=yy[:, :, :], in0=rc[:, :, :], scalar=-1.0, in1=sv3[:, :, 0:T],
                                        op0=ALU.mult, op1=ALU.mult).then_inc(y_done, 1)

            def y_rest(g, c):
                dve.wait_ge(yhi_done, g + 1)
                ve.tensor_tensor(y_lo[:, c % 2, :], flat(yy), y_hi[:, c % 2, :].bitcast(F32),
                                 ALU.subtract).then_inc(ylo_done, 1)

            def statistics(i, s):
                if s == 0:
                    wait(dve, x_in, i * 16 + 16)
                    wait(dve, normed, i * SUB)
                ve.bn_stats(stats[:, s, :], xin[:, s, :]).then_inc(st_done, 1)

            def aggregate(s):
                ve.bn_aggr(mv[:, s, :], stats[:, s, :]).then_inc(mv_done, 1)

            def normalise(i, s):
                if s == 0:
                    dve.wait_ge(rstd_done, i + 1)
                ve.tensor_scalar(xin[:, s, :], xin[:, s, :], mv[:, s, 0:1], rstd[:, s:s + 1],
                                 ALU.subtract, ALU.mult).then_inc(normed, 1)

            def residual(i):
                wait(dve, wo_done, i * HC + HC)
                wait(dve, bo_added, i + 1)
                for s in range(SUB):
                    ve.tensor_tensor(xres[:, s, :], xres[:, s, :], acc[s][:, :], ALU.add).then_inc(res_done, 1)

            for a in (u["k"], u["r"]):
                ve.memset(a[:, :, 0:T + 2:T + 1], 0.0)
            for a in (ee3, ev3):
                ve.memset(a[:, :, 0:1], 0.0)
            for s in range(SUB):
                statistics(0, s)
            dve.wait_ge(st_done, SUB)
            for s in range(SUB):
                aggregate(s)
            for s in range(SUB):
                normalise(0, s)
            dve.wait_ge(consts_in, 16 * NCONST)
            ve.tensor_scalar(nbr[:, :], col[:, 0, :], -1.0, None, ALU.mult).then_inc(setup, 1)
            ve.tensor_tensor(buk[:, :], col[:, 1, :], col[:, 4, :], ALU.add).then_inc(setup, 1)
            ve.tensor_scalar(ebv[:, :], col[:, 2, :], MIX["v"], None, ALU.mult).then_inc(setup, 1)
            ve.tensor_scalar(negw[:, :], col[:, 3, :], 0.0, -1.0, ALU.max, ALU.mult).then_inc(setup, 1)
            ve.memset(zero[:, :, :], 0.0).then_inc(setup, 1)
            for k in range(KC):
                xt_rest(0, k)
            dve.wait_ge(setup, 5)

            def body(i):
                for c in range(HC):
                    g = i * HC + c
                    back = c > 0 or not is_first(i)
                    ahead = not is_last(i)
                    if back:
                        one_plus(g - 1)
                    if c == HC - 1 and ahead:
                        xt_rest(i + 1, 1)
                        denominator(g - 1)
                        xt_rest(i + 1, 2)
                        divide(g - 1)
                        xt_rest(i + 1, 3)
                        y_rest(g - 1, c - 1)
                        mix("k", i, c, kt, k_mix)
                        decayed(i, c)
                        mix("v", i, c, vv, v_mix)
                        mix("r", i, c, rt, r_mix)
                        clip_and_scan(g)
                        continue
                    if back:
                        denominator(g - 1)
                    mix("k", i, c, kt, k_mix)
                    decayed(i, c)
                    if ahead and c in (2, 3):
                        statistics(i + 1, 2 * c - 4)
                        statistics(i + 1, 2 * c - 3)
                        dve.wait_ge(st_done, (i + 1) * SUB + 2 * c - 2)
                    mix("v", i, c, vv, v_mix)
                    if ahead and c in (2, 3):
                        aggregate(2 * c - 4)
                        aggregate(2 * c - 3)
                    if back:
                        divide(g - 1)
                    if ahead and c in (5, 6):
                        normalise(i + 1, 2 * c - 10)
                        normalise(i + 1, 2 * c - 9)
                    mix("r", i, c, rt, r_mix)
                    clip_and_scan(g, (lambda: y_rest(g - 1, (c - 1) % HC)) if back else None,
                                  (lambda: xt_rest(i + 1, 0)) if ahead and c == HC - 2 else None)
                    if c == LAG - 1 and not is_first(i):
                        residual(i - 1)

            over_tiles(dve, body)
            g = NT * HC - 1
            one_plus(g)
            denominator(g)
            divide(g)
            y_rest(g, HC - 1)
            residual(NT - 1)

        @block.gpsimd
        def _(pool):
            gp = nc.gpsimd

            def rstd_of(i):
                wait(pool, mv_done, i * SUB + SUB)
                wait(pool, normed, i * SUB)
                gp.tensor_tensor(rstd[:, :], mv[:, :, 1], eps[:, :], ALU.add).then_inc(veps_done, 1)
                pool.wait_ge(veps_done, i + 1)
                gp.tensor_tensor(rstd[:, :], rstd[:, :], half[:, :], ALU.pow).then_inc(rstd_done, 1)

            def split_rest(n):
                pool.wait_ge(whi_done, n + 1)
                gp.tensor_tensor(piece(n)[2], xres[:, n % 4, :], piece(n)[1].bitcast(F32),
                                 ALU.subtract).then_inc(wlo_done, 1)

            def front(g):
                pool.wait_ge(v_mix, g + 1)
                pool.wait_ge(eu_clip, g + 1)
                wait(pool, a_done, g)
                gp.tensor_tensor(euv[:, :, :], eu[:, :, :], vv[:, :, :], ALU.mult).then_inc(euv_done, 1)
                pool.wait_ge(s_scan, g + 1)
                gp.tensor_tensor(ss3[:, :, 0:T], ss3[:, :, 0:T], eu[:, :, :], ALU.add).then_inc(b_done, 1)
                pool.wait_ge(sv_scan, g + 1)
                pool.wait_ge(euv_done, g + 1)
                gp.tensor_tensor(sv3[:, :, 0:T], sv3[:, :, 0:T], euv[:, :, :], ALU.add).then_inc(a_done, 1)

            def back_of(g):
                pool.wait_ge(rc_done, g + 1)
                gp.tensor_tensor(dd[:, :, :], dd[:, :, :], rc[:, :, :], ALU.mult).then_inc(rd_done, 1)

            gp.memset(half[:, :], -0.5).then_inc(consts_set, 1)
            gp.memset(shift[:, :], -LN_SHIFT * math.log(2.0)).then_inc(consts_set, 1)
            gp.memset(eps[:, :], LN_EPS).then_inc(consts_set, 1)
            pool.wait_ge(consts_set, 3)
            rstd_of(0)
            for n in range(4):
                split_rest(n)
            pool.wait_ge(consts_in, 16 * NCONST)

            def body(i):
                for c in range(HC):
                    g = i * HC + c
                    for m in range(4):
                        if m == 2 and (c > 0 or not is_first(i)):
                            back_of(g - 1)
                        if is_first(i) and c < HC - 1:
                            split_rest(4 * (c + 1) + m)
                    if c == 0 and not is_first(i):
                        pool.wait_ge(res_in, i * 16)
                        for s in range(SUB):
                            last = gp.tensor_tensor(xres[:, s, :], xres[:, s, :], bo_sb[:, :], ALU.add)
                        last.then_inc(bo_added, 1)
                    front(g)
                    if c == 3 and not is_last(i):
                        rstd_of(i + 1)

            over_tiles(pool, body)
            back_of(NT * HC - 1)
            pool.wait_ge(res_in, NT * 16)
            for s in range(SUB):
                last = gp.tensor_tensor(xres[:, s, :], xres[:, s, :], bo_sb[:, :], ALU.add)
            last.then_inc(bo_added, 1)


def cross_pass(nc, x1, ctx_in, ctx_t, fside, weights, biases, bo_b, ident, x2):
    with ExitStack() as ctx:
        def sb(name, shape, dt=F32):
            return ctx.enter_context(nc.sbuf_tensor("b_" + name, shape, dt))

        def sem(name):
            return ctx.enter_context(nc.semaphore("b_" + name))

        SCALE = 1.0 / math.sqrt(32.0)
        raw = {n: sb("raw_" + n, [P, KC, C]) for n in ("wq", "wk", "wv", "wo")}
        m_hi, m_lo = sb("m_hi", [P, KC, C], F32R), sb("m_lo", [P, KC, C], F32R)
        l_hi, l_lo = sb("l_hi", [P, KC, C], F32R), sb("l_lo", [P, KC, C], F32R)
        bcol = sb("bcol", [P, 3, KC])
        bwide = sb("bwide", [P, 2, KC, P])
        qb = sb("qb", [P, KC])
        rk_row = sb("rk_row", [P, C])
        bqk = sb("bqk", [P, 1])
        out_row = sb("out_row", [P, C])
        id_sb = sb("ident", [P, P])
        xin, xres = sb("xin", [P, SUB, C]), sb("xres", [P, SUB, C])
        junk = sb("junk", [P, C])
        xt_hi, xt_lo = sb("xt_hi", [P, KC, N], F32R), sb("xt_lo", [P, KC, N], F32R)
        q_hi, q_lo = sb("q_hi", [P, KC, N], F32R), sb("q_lo", [P, KC, N], F32R)
        cx, cx_hi, cx_lo = sb("cx", [P, SUB, C]), sb("cx_hi", [P, SUB, C], F32R), sb("cx_lo", [P, SUB, C], F32R)
        ct, ct_hi, ct_lo = sb("ct", [P, KC, N]), sb("ct_hi", [P, KC, N], F32R), sb("ct_lo", [P, KC, N], F32R)
        fs, pr = sb("fs", [P, SUB, T]), sb("pr", [P, SUB, T])
        pt_hi, pt_lo = sb("pt_hi", [P, BT, 2 * T], F32R), sb("pt_lo", [P, BT, 2 * T], F32R)
        pc_hi, pc_lo = sb("pc_hi", [P, KC, N], F32R), sb("pc_lo", [P, KC, N], F32R)
        stats, mv = sb("stats", [P, SUB, 6]), sb("mv", [P, SUB, 2])
        rstd, half, eps = sb("rstd", [P, SUB]), sb("half", [P, SUB]), sb("eps", [P, SUB])
        rq_next, rq, mx, nb, rowsum, rinv = (sb(n, [P, SUB]) for n in ("rq_next", "rq", "mx", "nb", "rowsum",
                                                                      "rinv"))
        flat = lambda a: a[:, :, :].rearrange("p a b -> p (a b)")

        bank = [ctx.enter_context(nc.psum_tensor(f"b_bank{j}", [P, N], F32)) for j in range(4)]
        acc = [ctx.enter_context(nc.psum_tensor(f"b_acc{s}", [P, C], F32)) for s in range(SUB)]

        w_in, x_in, res_in, cx_in, ct_in, fs_in, stored = (
            sem(n) for n in ("w_in", "x_in", "res_in", "cx_in", "ct_in", "fs_in", "stored"))
        fold_done, fold_left, bwide_done = sem("fold_done"), sem("fold_left"), sem("bwide_done")
        turned, q_proj, sc_done, pt_done, pc_done, out_done = (
            sem(n) for n in ("turned", "q_proj", "sc_done", "pt_done", "pc_done", "out_done"))
        xhi_done, qhi_done, exp_done, pthi_done, pchi_done, cxhi_done, cthi_done, mlhi_done = (
            sem(n) for n in ("xhi_done", "qhi_done", "exp_done", "pthi_done", "pchi_done", "cxhi_done", "cthi_done",
                             "mlhi_done"))
        xlo_done, qlo_done, sc_left, mx_done, nb_done, rinv_done, ptlo_done, pclo_done, res_done = (
            sem(n) for n in ("xlo_done", "qlo_done", "sc_left", "mx_done", "nb_done", "rinv_done", "ptlo_done",
                             "pclo_done", "res_done"))
        st_done, mv_done, normed, rq_made, rq_moved = (
            sem(n) for n in ("st_done", "mv_done", "normed", "rq_made", "rq_moved"))
        veps_done, rstd_done, bo_added, cxlo_done, ctlo_done, half_set = (
            sem(n) for n in ("veps_done", "rstd_done", "bo_added", "cxlo_done", "ctlo_done", "half_set"))

        def ct_view(i):
            sel = ctx_t[i:i + 1] if isinstance(i, int) else ctx_t[bass.ds(i, 1)]
            return sel.rearrange("o p k n -> p (o k) n")

        def fs_view(i):
            return tile_of(fside, i)

        NFOLD = 2 * KC + 4
        TAIL = 2
        block = ctx.enter_context(nc.Block())

        @block.sync
        def _(sp):
            sp.dma_start(xin[:, :, :], tile_of(x1, 0)).then_inc(x_in, 16)
            for dst, src in ((bcol[:, :, :], biases), (out_row[:, :], bo_b), (id_sb[:, :], ident),
                             (raw["wq"][:, :, :], weights["wq"]), (raw["wk"][:, :, :], weights["wk"]),
                             (raw["wv"][:, :, :], weights["wv"]), (raw["wo"][:, :, :], weights["wo"])):
                sp.dma_start(dst, src).then_inc(w_in, 16)
            sp.dma_start(ct[:, :, :], ct_view(0)).then_inc(ct_in, 16)
            sp.dma_start(fs[:, :, :], fs_view(0)).then_inc(fs_in, 16)
            sp.dma_start(cx[:, :, :], tile_of(ctx_in, 0)).then_inc(cx_in, 16)
            sp.dma_start(xres[:, :, :], tile_of(x1, 0)).then_inc(res_in, 16)
            sp.wait_ge(turned, KC)
            sp.dma_start(xin[:, :, :], tile_of(x1, 1)).then_inc(x_in, 16)

            def body(i):
                more = not is_last(i)
                if more:
                    sp.wait_ge(ctlo_done, i + 1)
                    sp.dma_start(ct[:, :, :], ct_view(i + 1)).then_inc(ct_in, 16)
                    sp.wait_ge(cxlo_done, i + 1)
                    sp.dma_start(cx[:, :, :], tile_of(ctx_in, i + 1)).then_inc(cx_in, 16)
                    sp.wait_ge(sc_left, i * SUB + SUB)
                    sp.dma_start(fs[:, :, :], fs_view(i + 1)).then_inc(fs_in, 16)
                    if not isinstance(i, int) or i < NT - TAIL:
                        sp.wait_ge(turned, i * KC + 2 * KC)
                        sp.dma_start(xin[:, :, :], tile_of(x1, i + 2)).then_inc(x_in, 16)
                sp.wait_ge(res_done, i * SUB + SUB)
                sp.dma_start(tile_of(x2, i), xres[:, :, :]).then_inc(stored, 16)
                sp.wait_ge(stored, i * 16 + 16)
                if more:
                    sp.dma_start(xres[:, :, :], tile_of(x1, i + 1)).then_inc(res_in, 16)

            over_tiles(sp, body, TAIL)

        @block.tensor
        def _(pe):
            te = nc.tensor

            def cut(a, k, j):
                return a[:, k, j * P:(j + 1) * P]

            def fold():
                pe.wait_ge(w_in, 16 * 7)
                n = 0
                for a, b in (("wq", "wk"), ("wv", "wo")):
                    for j in range(KC):
                        wait(pe, fold_left, n - 1)
                        for e in range(KC):
                            last = te.matmul(bank[n % 2][:, :], cut(raw[a], e, j), raw[b][:, e, :],
                                             start=(e == 0), stop=(e == KC - 1))
                        last.then_inc(fold_done, 1)
                        n += 1
                pe.wait_ge(bwide_done, 2)
                for j in range(KC):
                    for e in range(KC):
                        last = te.matmul(bank[2][:, j:j + 1], cut(raw["wk"], e, j), bcol[:, 0, e:e + 1],
                                         start=(e == 0), stop=(e == KC - 1))
                last.then_inc(fold_done, 1)
                for e in range(KC):
                    last = te.matmul(bank[3][:, :], bwide[:, 0, e, :], raw["wq"][:, e, :],
                                     start=(e == 0), stop=(e == KC - 1))
                last.then_inc(fold_done, 1)
                for e in range(KC):
                    last = te.matmul(acc[0][:, 0:1], bwide[:, 0, e, :], bcol[:, 0, e:e + 1],
                                     start=(e == 0), stop=(e == KC - 1))
                last.then_inc(fold_done, 1)
                for e in range(KC):
                    last = te.matmul(acc[1][:, :], bwide[:, 1, e, :], raw["wo"][:, e, :],
                                     start=(e == 0), stop=(e == KC - 1))
                last.then_inc(fold_done, 1)

            def turn(i, k):
                wait(pe, rq_made, i * SUB + SUB)
                if k >= 2:
                    wait(pe, xlo_done, i * KC + k - 1)
                else:
                    wait(pe, ptlo_done, (i - 2) * BT + k + 1)
                for s in range(SUB):
                    last = te.transpose(bank[2 + k % 2][:, s * P:(s + 1) * P], xin[:, s, k * P:(k + 1) * P],
                                        id_sb[:, :])
                last.then_inc(turned, 1)

            def query(i, c):
                if c == 0:
                    wait(pe, xlo_done, i * KC + KC)
                if c >= 2:
                    wait(pe, qlo_done, i * KC + c - 1)
                else:
                    wait(pe, sc_left, (i - 1) * SUB + 3 + c)
                three(te, bank[c % 2][:, :],
                      [((cut(m_hi, k, c), cut(m_lo, k, c)), (xt_hi[:, k, :], xt_lo[:, k, :]))
                       for k in range(KC)]).then_inc(q_proj, 1)

            def scores(i, s):
                b = s // 2
                if s == 0:
                    wait(pe, qlo_done, i * KC + KC)
                    wait(pe, ctlo_done, i + 1)
                if s >= 2:
                    wait(pe, sc_left, i * SUB + s - 1)
                else:
                    wait(pe, pclo_done, (i - 1) * KC + 3 + s)
                keys = slice(b * T, (b + 1) * T)
                three(te, bank[s % 2][:, 0:T],
                      [((cut(q_hi, k, s), cut(q_lo, k, s)), (ct_hi[:, k, keys], ct_lo[:, k, keys]))
                       for k in range(KC)]).then_inc(sc_done, 1)

            def turn_probs(i, b):
                wait(pe, exp_done, i * SUB + 2 * b + 2)
                if not is_last(i):
                    wait(pe, xlo_done, (i + 1) * KC + 3 + b)
                for kk in range(2):
                    for h in range(2):
                        last = te.transpose(bank[2 + b][:, kk * T + h * P:kk * T + (h + 1) * P],
                                            pr[:, 2 * b + h, kk * P:(kk + 1) * P], id_sb[:, :])
                last.then_inc(pt_done, 1)

            def context(i, c):
                if c == 0:
                    wait(pe, ptlo_done, i * BT + BT)
                    wait(pe, cxlo_done, i + 1)
                if c >= 2:
                    wait(pe, pclo_done, i * KC + c - 1)
                elif is_last(i):
                    wait(pe, sc_left, i * SUB + 3 + c)
                else:
                    wait(pe, qlo_done, (i + 1) * KC + 3 + c)
                for b in range(BT):
                    last = three(te, bank[c % 2][:, b * T:(b + 1) * T],
                                 [((cut(cx_hi, 2 * b + kk, c), cut(cx_lo, 2 * b + kk, c)),
                                   (pt_hi[:, b, kk * T:(kk + 1) * T], pt_lo[:, b, kk * T:(kk + 1) * T]))
                                  for kk in range(2)])
                last.then_inc(pc_done, 1)

            def output(i, c):
                wait(pe, pclo_done, i * KC + c + 1)
                if c == 0:
                    wait(pe, res_done, i * SUB)
                for s in range(SUB):
                    for a, b in ((pc_hi, l_hi), (pc_hi, l_lo), (pc_lo, l_hi)):
                        last = te.matmul(acc[s][:, :], cut(a, c, s), b[:, c, :],
                                         start=(c == 0 and a is pc_hi and b is l_hi),
                                         stop=(c == KC - 1 and a is pc_lo))
                if c == KC - 1:
                    last.then_inc(out_done, 1)

            fold()
            pe.wait_ge(fold_left, NFOLD)
            for k in range(KC):
                turn(0, k)
            for c in range(KC):
                query(0, c)

            def body(i):
                for s in range(SUB):
                    scores(i, s)
                    if not is_last(i):
                        turn(i + 1, s)
                if not is_last(i):
                    for c in range(KC - 1):
                        query(i + 1, c)
                turn_probs(i, 0)
                turn_probs(i, 1)
                if not is_last(i):
                    query(i + 1, KC - 1)
                context(i, 0)
                context(i, 1)
                output(i, 0)
                context(i, 2)
                output(i, 1)
                context(i, 3)
                output(i, 2)
                output(i, 3)

            over_tiles(pe, body, TAIL)

        @block.scalar
        def _(act):
            sc = nc.scalar
            sc.preload_act_table_set(TABLES)

            def x_high(i, k):
                wait(act, turned, i * KC + k + 1)
                sc.activation(xt_hi[:, k, :], bank[2 + k % 2][:, :], ACT.Copy).then_inc(xhi_done, 1)

            def q_high(i, c):
                wait(act, q_proj, i * KC + c + 1)
                sc.activation(q_hi[:, c, :], bank[c % 2][:, :], ACT.Identity, bias=qb[:, c:c + 1]).then_inc(qhi_done, 1)

            def context_high(i):
                wait(act, ct_in, i * 16 + 16)
                wait(act, sc_done, i * SUB)
                sc.activation(flat(ct_hi), flat(ct), ACT.Copy).then_inc(cthi_done, 1)

            def context_high2(i):
                wait(act, cx_in, i * 16 + 16)
                wait(act, pc_done, i * KC)
                sc.activation(flat(cx_hi), flat(cx), ACT.Copy).then_inc(cxhi_done, 1)

            def exponent(i, s):
                wait(act, nb_done, i * SUB + s + 1)
                if s == 0:
                    wait(act, rinv_done, i)
                sc.activation(pr[:, s, :], pr[:, s, :], ACT.Exp, scale=SCALE, bias=nb[:, s:s + 1],
                              accum_out=rowsum[:, s:s + 1]).then_inc(exp_done, 1)

            def probs_high(i, b):
                wait(act, pt_done, i * BT + b + 1)
                sc.activation(pt_hi[:, b, :], bank[2 + b][:, :], ACT.Copy).then_inc(pthi_done, 1)

            def pc_high(i, c):
                wait(act, pc_done, i * KC + c + 1)
                sc.activation(pc_hi[:, c, :], bank[c % 2][:, :], ACT.Copy).then_inc(pchi_done, 1)

            for n in range(2 * KC):
                act.wait_ge(fold_done, n + 1)
                dst = (m_hi, l_hi)[n // KC][:, n % KC, :]
                sc.activation(dst, bank[n % 2][:, :], ACT.Copy).then_inc(mlhi_done, 1)
            context_high(0)
            context_high2(0)
            for k in range(KC):
                x_high(0, k)
            act.wait_ge(fold_left, NFOLD)
            for c in range(KC):
                q_high(0, c)

            def body(i):
                ahead = not is_last(i)
                for s in range(SUB):
                    if ahead:
                        x_high(i + 1, s)
                    exponent(i, s)
                if ahead:
                    context_high(i + 1)
                    for c in range(KC - 1):
                        q_high(i + 1, c)
                probs_high(i, 0)
                probs_high(i, 1)
                if ahead:
                    q_high(i + 1, KC - 1)
                for c in range(KC):
                    pc_high(i, c)
                if ahead:
                    context_high2(i + 1)

            over_tiles(act, body, TAIL)

        @block.vector
        def _(dve):
            ve = nc.vector

            def rest(out, src, high, done):
                ve.tensor_tensor(out, src, high.bitcast(F32), ALU.subtract).then_inc(done, 1)

            def x_rest(i, k):
                wait(dve, xhi_done, i * KC + k + 1)
                rest(xt_lo[:, k, :], bank[2 + k % 2][:, :], xt_hi[:, k, :], xlo_done)

            def q_rest(i, c):
                wait(dve, qhi_done, i * KC + c + 1)
                ve.scalar_tensor_tensor(out=q_lo[:, c, :], in0=bank[c % 2][:, :], scalar=qb[:, c:c + 1],
                                        in1=q_hi[:, c, :].bitcast(F32), op0=ALU.add,
                                        op1=ALU.subtract).then_inc(qlo_done, 1)

            def score(i, s):
                g = i * SUB + s
                wait(dve, sc_done, g + 1)
                if s == 0:
                    wait(dve, fs_in, i * 16 + 16)
                    wait(dve, rq_moved, i + 1)
                    wait(dve, pt_done, i * BT)
                ve.scalar_tensor_tensor(out=pr[:, s, :], in0=bank[s % 2][:, 0:T], scalar=rq[:, s:s + 1],
                                        in1=fs[:, s, :], op0=ALU.add, op1=ALU.add).then_inc(sc_left, 1)
                wait(dve, sc_left, g + 1)
                wait(dve, nb_done, g)
                ve.reduce_max(mx[:, s:s + 1], pr[:, s, :], AX.X).then_inc(mx_done, 1)
                wait(dve, mx_done, g + 1)
                ve.tensor_scalar(nb[:, s:s + 1], mx[:, s:s + 1], -SCALE, None, ALU.mult).then_inc(nb_done, 1)

            def probs_rest(i, b):
                wait(dve, pthi_done, i * BT + b + 1)
                rest(pt_lo[:, b, :], bank[2 + b][:, :], pt_hi[:, b, :], ptlo_done)

            def pc_rest(i, c):
                wait(dve, pchi_done, i * KC + c + 1)
                rest(pc_lo[:, c, :], bank[c % 2][:, :], pc_hi[:, c, :], pclo_done)

            def inverse(i):
                wait(dve, exp_done, i * SUB + SUB)
                wait(dve, res_done, i * SUB)
                ve.reciprocal(rinv[:, :], rowsum[:, :]).then_inc(rinv_done, 1)

            def residual(i):
                wait(dve, out_done, i + 1)
                wait(dve, bo_added, i + 1)
                wait(dve, rinv_done, i + 1)
                for s in range(SUB):
                    ve.scalar_tensor_tensor(out=xres[:, s, :], in0=acc[s][:, :], scalar=rinv[:, s:s + 1],
                                            in1=xres[:, s, :], op0=ALU.mult, op1=ALU.add).then_inc(res_done, 1)

            def statistics(i):
                wait(dve, x_in, i * 16 + 16)
                for s in range(SUB):
                    ve.bn_stats(stats[:, s, :], xin[:, s, :]).then_inc(st_done, 1)

            def aggregate():
                for s in range(SUB):
                    ve.bn_aggr(mv[:, s, :], stats[:, s, :]).then_inc(mv_done, 1)

            def normalise(i):
                wait(dve, rstd_done, i + 1)
                for s in range(SUB):
                    ve.tensor_scalar(xin[:, s, :], xin[:, s, :], mv[:, s, 0:1], rstd[:, s:s + 1],
                                     ALU.subtract, ALU.mult).then_inc(normed, 1)
                for s in range(SUB):
                    wait(dve, normed, i * SUB + s + 1)
                    wait(dve, rq_made, i * SUB + s)
                    ve.tensor_tensor_reduce(out=junk[:, :], in0=xin[:, s, :], in1=rk_row[:, :], scale=1.0,
                                            scalar=bqk[:, 0:1], op0=ALU.mult, op1=ALU.add,
                                            accum_out=rq_next[:, s:s + 1]).then_inc(rq_made, 1)

            def move_rq(i):
                wait(dve, rq_made, i * SUB + SUB)
                ve.tensor_copy(rq[:, :], rq_next[:, :]).then_inc(rq_moved, 1)

            statistics(0)
            dve.wait_ge(st_done, SUB)
            aggregate()
            dve.wait_ge(w_in, 16 * 7)
            for j in range(2):
                ve.tensor_copy(bwide[:, j, :, :],
                               bcol[:, 1 + j, :].unsqueeze(2).to_broadcast([P, KC, P])).then_inc(bwide_done, 1)
            for n in range(2 * KC):
                dve.wait_ge(mlhi_done, n + 1)
                hi, lo = ((m_hi, m_lo), (l_hi, l_lo))[n // KC]
                rest(lo[:, n % KC, :], bank[n % 2][:, :], hi[:, n % KC, :], fold_left)
            for n, (dst, src) in enumerate(((qb[:, :], bank[2][:, 0:KC]), (rk_row[:, :], bank[3][:, :]),
                                            (bqk[:, :], acc[0][:, 0:1]))):
                dve.wait_ge(fold_done, 2 * KC + n + 1)
                ve.tensor_copy(dst, src).then_inc(fold_left, 1)
            dve.wait_ge(fold_done, NFOLD)
            ve.tensor_tensor(out_row[:, :], out_row[:, :], acc[1][:, :], ALU.add).then_inc(fold_left, 1)
            dve.wait_ge(fold_left, NFOLD)
            normalise(0)
            move_rq(0)
            for k in range(KC):
                x_rest(0, k)
            statistics(1)
            dve.wait_ge(st_done, 2 * SUB)
            aggregate()
            for c in range(KC):
                q_rest(0, c)
            normalise(1)

            def body(i):
                ahead = not is_last(i)
                for s in range(SUB):
                    score(i, s)
                    if ahead:
                        x_rest(i + 1, s)
                inverse(i)
                if ahead:
                    move_rq(i + 1)
                    for c in range(KC - 1):
                        q_rest(i + 1, c)
                probs_rest(i, 0)
                probs_rest(i, 1)
                two_ahead = not isinstance(i, int) or i < NT - TAIL
                if ahead:
                    if two_ahead:
                        statistics(i + 2)
                        dve.wait_ge(st_done, i * SUB + 3 * SUB)
                    q_rest(i + 1, KC - 1)
                    if two_ahead:
                        aggregate()
                for c in range(KC):
                    pc_rest(i, c)
                if two_ahead:
                    normalise(i + 2)
                residual(i)

            over_tiles(dve, body, TAIL)

        @block.gpsimd
        def _(pool):
            gp = nc.gpsimd

            def rstd_of(i):
                wait(pool, mv_done, i * SUB + SUB)
                wait(pool, normed, i * SUB)
                gp.tensor_tensor(rstd[:, :], mv[:, :, 1], eps[:, :], ALU.add).then_inc(veps_done, 1)
                wait(pool, veps_done, i + 1)
                gp.tensor_tensor(rstd[:, :], rstd[:, :], half[:, :], ALU.pow).then_inc(rstd_done, 1)

            def context_rest(i):
                wait(pool, cthi_done, i + 1)
                gp.tensor_tensor(flat(ct_lo), flat(ct), flat(ct_hi).bitcast(F32), ALU.subtract).then_inc(ctlo_done, 1)

            def context_rest2(i):
                wait(pool, cxhi_done, i + 1)
                gp.tensor_tensor(flat(cx_lo), flat(cx), flat(cx_hi).bitcast(F32), ALU.subtract).then_inc(cxlo_done, 1)

            def add_bias(i):
                wait(pool, res_in, i * 16 + 16)
                for s in range(SUB):
                    last = gp.tensor_tensor(xres[:, s, :], xres[:, s, :], out_row[:, :], ALU.add)
                last.then_inc(bo_added, 1)

            gp.memset(half[:, :], -0.5).then_inc(half_set, 1)
            gp.memset(eps[:, :], LN_EPS).then_inc(half_set, 1)
            pool.wait_ge(half_set, 2)
            rstd_of(0)
            context_rest(0)
            context_rest2(0)
            pool.wait_ge(fold_left, NFOLD)
            rstd_of(1)

            def body(i):
                add_bias(i)
                if not is_last(i):
                    context_rest(i + 1)
                    if not isinstance(i, int) or i < NT - TAIL:
                        rstd_of(i + 2)
                    context_rest2(i + 1)

            over_tiles(pool, body, TAIL)


def ffn_pass(nc, x2, weights, mu, ident, x3):
    with ExitStack() as ctx:
        def sb(name, shape, dt=F32):
            return ctx.enter_context(nc.sbuf_tensor("c_" + name, shape, dt))

        def sem(name):
            return ctx.enter_context(nc.semaphore("c_" + name))

        WM = "rkv"
        raw = {m: sb("raw_" + m, [P, KC, C]) for m in WM}
        w_hi = {m: sb(f"w{m}_hi", [P, KC, C], F32R) for m in WM}
        w_lo = {m: sb(f"w{m}_lo", [P, KC, C], F32R) for m in WM}
        mu_sb = sb("mu", [P, 2, KC])
        id_sb = sb("ident", [P, P])
        xin, xres = sb("xin", [P, SUB, C]), sb("xres", [P, SUB, C])
        xt = sb("xt", [P, KC, BT, T + 1])
        diff = sb("diff", [P, KC, N])
        mixed = {m: sb("mixed_" + m, [P, KC, N]) for m in "rk"}
        m_hi = {m: sb(f"mixed_{m}_hi", [P, KC, N], F32R) for m in "rk"}
        m_lo = {m: sb(f"mixed_{m}_lo", [P, KC, N], F32R) for m in "rk"}
        gate, grec = sb("gate", [P, SUB, C]), sb("grec", [P, SUB, C])
        ka = sb("ka", [P, 2, N])
        k_hi, k_lo = sb("k_hi", [P, KC, N], F32R), sb("k_lo", [P, KC, N], F32R)
        stats, mv = sb("stats", [P, SUB, 6]), sb("mv", [P, SUB, 2])
        rstd, half, eps = sb("rstd", [P, SUB]), sb("half", [P, SUB]), sb("eps", [P, SUB])
        flat = lambda a: a[:, :, :].rearrange("p a b -> p (a b)")
        seqs = lambda a: a.rearrange("p (b t) -> p b t", b=BT)

        bank = [ctx.enter_context(nc.psum_tensor(f"c_bank{j}", [P, N], F32)) for j in range(4)]
        acc = [ctx.enter_context(nc.psum_tensor(f"c_acc{s}", [P, C], F32)) for s in range(SUB)]

        consts_in, x_in, res_in, stored = sem("consts_in"), sem("x_in"), sem("res_in"), sem("stored")
        w_in = {m: sem("w_in_" + m) for m in WM}
        turned, r_proj, k_proj, v_done = sem("turned"), sem("r_proj"), sem("k_proj"), sem("v_done")
        whi_done, wlo_done, xt_left = sem("whi_done"), sem("wlo_done"), sem("xt_left")
        e_exp, ln_done, rc_done, relu_done, square_done, khi_done, klo_done = (
            sem(n) for n in ("e_exp", "ln_done", "rc_done", "relu_done", "square_done", "khi_done", "klo_done"))
        diffed = sem("diffed")
        mix_done = {m: sem("mix_done_" + m) for m in "rk"}
        mhi_done = {m: sem("mhi_done_" + m) for m in "rk"}
        mlo_done = {m: sem("mlo_done_" + m) for m in "rk"}
        capped, rd_done, newton, gated, res_done = (
            sem(n) for n in ("capped", "rd_done", "newton", "gated", "res_done"))
        st_done, mv_done, normed, veps_done, rstd_done, half_set, margin = (
            sem(n) for n in ("st_done", "mv_done", "normed", "veps_done", "rstd_done", "half_set", "margin"))

        TAIL = 2
        block = ctx.enter_context(nc.Block())

        @block.sync
        def _(sp):
            sp.dma_start(xin[:, :, :], tile_of(x2, 0)).then_inc(x_in, 16)
            sp.dma_start(mu_sb[:, :, :], mu).then_inc(consts_in, 16)
            sp.dma_start(id_sb[:, :], ident).then_inc(consts_in, 16)
            for m in WM:
                sp.dma_start(raw[m][:, :, :], weights[m]).then_inc(w_in[m], 16)
            sp.dma_start(xres[:, :, :], tile_of(x2, 0)).then_inc(res_in, 16)
            sp.wait_ge(turned, KC)
            sp.dma_start(xin[:, :, :], tile_of(x2, 1)).then_inc(x_in, 16)

            def body(i):
                if not isinstance(i, int) or i < NT - TAIL:
                    sp.wait_ge(turned, i * KC + 2 * KC)
                    sp.dma_start(xin[:, :, :], tile_of(x2, i + 2)).then_inc(x_in, 16)
                sp.wait_ge(res_done, i * SUB + SUB)
                sp.dma_start(tile_of(x3, i), xres[:, :, :]).then_inc(stored, 16)
                sp.wait_ge(stored, i * 16 + 16)
                if not is_last(i):
                    sp.dma_start(xres[:, :, :], tile_of(x2, i + 1)).then_inc(res_in, 16)

            over_tiles(sp, body, TAIL)

        @block.tensor
        def _(pe):
            te = nc.tensor

            def cut(a, k, j):
                return a[:, k, j * P:(j + 1) * P]

            def turn(i, k):
                wait(pe, normed, i * SUB + SUB)
                wait(pe, xt_left, i * KC + k - 1)
                for s in range(SUB):
                    last = te.transpose(bank[2 + k % 2][:, s * P:(s + 1) * P], xin[:, s, k * P:(k + 1) * P],
                                        id_sb[:, :])
                last.then_inc(turned, 1)

            def receptance(i, s):
                if s == 0:
                    wait(pe, mlo_done["r"], i * KC + KC)
                if s >= 2:
                    wait(pe, capped, i * SUB + s - 1)
                else:
                    wait(pe, relu_done, (i - 1) * KC + 3 + s)
                three(te, bank[s % 2][:, :],
                      [((cut(m_hi["r"], k, s), cut(m_lo["r"], k, s)), (w_hi["r"][:, k, :], w_lo["r"][:, k, :]))
                       for k in range(KC)]).then_inc(r_proj, 1)

            def key(i, c):
                if c == 0:
                    wait(pe, mlo_done["k"], i * KC + KC)
                if c >= 2:
                    wait(pe, relu_done, i * KC + c - 1)
                else:
                    wait(pe, capped, i * SUB + 3 + c)
                three(te, bank[c % 2][:, :],
                      [((cut(w_hi["k"], k, c), cut(w_lo["k"], k, c)), (m_hi["k"][:, k, :], m_lo["k"][:, k, :]))
                       for k in range(KC)]).then_inc(k_proj, 1)

            def value(i, c):
                wait(pe, klo_done, i * KC + c + 1)
                if c == 0:
                    wait(pe, gated, i * SUB)
                for s in range(SUB):
                    for a, b in ((k_hi, w_hi["v"]), (k_hi, w_lo["v"]), (k_lo, w_hi["v"])):
                        last = te.matmul(acc[s][:, :], cut(a, c, s), b[:, c, :],
                                         start=(c == 0 and a is k_hi and b is w_hi["v"]),
                                         stop=(c == KC - 1 and a is k_lo))
                if c == KC - 1:
                    last.then_inc(v_done, 1)

            pe.wait_ge(consts_in, 32)
            for k in range(KC):
                turn(0, k)
            pe.wait_ge(wlo_done, 3)

            def body(i):
                for s in range(SUB):
                    receptance(i, s)
                for c in range(KC):
                    key(i, c)
                    if not is_last(i):
                        turn(i + 1, c)
                for c in range(KC):
                    value(i, c)

            over_tiles(pe, body, TAIL)

        @block.scalar
        def _(act):
            sc = nc.scalar
            sc.preload_act_table_set(TABLES)

            def leave(i, k):
                wait(act, turned, i * KC + k + 1)
                for m in "rk":
                    wait(act, mix_done[m], (i - 1) * KC + k + 1)
                sc.activation(xt[:, k, :, 1:], seqs(bank[2 + k % 2][:, :]), ACT.Copy).then_inc(xt_left, 1)

            def mixed_high(m, i, k):
                wait(act, mix_done[m], i * KC + k + 1)
                if k == 0:
                    wait(act, {"r": r_proj, "k": k_proj}[m], i * KC)
                sc.activation(m_hi[m][:, k, :], mixed[m][:, k, :], ACT.Copy).then_inc(mhi_done[m], 1)

            def exp_r(i, s):
                wait(act, capped, i * SUB + s + 1)
                sc.activation(gate[:, s, :], gate[:, s, :], ACT.Exp, scale=-1.0).then_inc(e_exp, 1)

            def first_reciprocal(i, s):
                wait(act, e_exp, i * SUB + s + 1)
                wait(act, res_done, (i - 1) * SUB + s + 1)
                sc.activation(grec[:, s, :], gate[:, s, :], ACT.Ln, bias=1.0).then_inc(ln_done, 1)
                wait(act, ln_done, i * SUB + s + 1)
                sc.activation(grec[:, s, :], grec[:, s, :], ACT.Exp, scale=-1.0).then_inc(rc_done, 1)

            def relu_square(i, c):
                g = i * KC + c
                wait(act, k_proj, g + 1)
                wait(act, klo_done, g - 1)
                sc.activation(ka[:, c % 2, :], bank[c % 2][:, :], ACT.Relu).then_inc(relu_done, 1)
                wait(act, relu_done, g + 1)
                sc.activation(ka[:, c % 2, :], ka[:, c % 2, :], ACT.Square).then_inc(square_done, 1)
                wait(act, square_done, g + 1)
                if c == 0:
                    wait(act, v_done, i)
                sc.activation(k_hi[:, c, :], ka[:, c % 2, :], ACT.Copy).then_inc(khi_done, 1)

            for k in range(KC):
                leave(0, k)
            for n, m in enumerate(WM):
                act.wait_ge(w_in[m], 16)
                sc.activation(flat(w_hi[m]), flat(raw[m]), ACT.Copy).then_inc(whi_done, 1)
            for m in "rk":
                for k in range(KC):
                    mixed_high(m, 0, k)

            def body(i):
                for s in range(SUB):
                    exp_r(i, s)
                for c in range(KC):
                    relu_square(i, c)
                    if not is_last(i):
                        leave(i + 1, c)
                    first_reciprocal(i, c)
                if not is_last(i):
                    for m in "rk":
                        for k in range(KC):
                            mixed_high(m, i + 1, k)

            over_tiles(act, body, TAIL)

        @block.vector
        def _(dve):
            ve = nc.vector

            def statistics(i):
                wait(dve, x_in, i * 16 + 16)
                for s in range(SUB):
                    ve.bn_stats(stats[:, s, :], xin[:, s, :]).then_inc(st_done, 1)

            def aggregate():
                for s in range(SUB):
                    ve.bn_aggr(mv[:, s, :], stats[:, s, :]).then_inc(mv_done, 1)

            def normalise(i):
                wait(dve, rstd_done, i + 1)
                for s in range(SUB):
                    ve.tensor_scalar(xin[:, s, :], xin[:, s, :], mv[:, s, 0:1], rstd[:, s:s + 1],
                                     ALU.subtract, ALU.mult).then_inc(normed, 1)

            def mix(m, i, k):
                wait(dve, diffed, i * KC + k + 1)
                wait(dve, mhi_done[m], (i - 1) * KC + k + 1)
                wait(dve, mlo_done[m], (i - 1) * KC + k + 1)
                ve.scalar_tensor_tensor(out=seqs(mixed[m][:, k, :]), in0=seqs(diff[:, k, :]),
                                        scalar=mu_sb[:, "rk".index(m), k:k + 1], in1=xt[:, k, :, 0:T],
                                        op0=ALU.mult, op1=ALU.add).then_inc(mix_done[m], 1)

            def mixed_rest(m, i, k):
                wait(dve, mhi_done[m], i * KC + k + 1)
                ve.tensor_tensor(m_lo[m][:, k, :], mixed[m][:, k, :], m_hi[m][:, k, :].bitcast(F32),
                                 ALU.subtract).then_inc(mlo_done[m], 1)

            def cap(i, s):
                wait(dve, r_proj, i * SUB + s + 1)
                ve.tensor_scalar(gate[:, s, :], bank[s % 2][:, :], -math.log(SIG_CAP), None,
                                 ALU.max).then_inc(capped, 1)

            def k_rest(i, c):
                wait(dve, khi_done, i * KC + c + 1)
                ve.tensor_tensor(k_lo[:, c, :], ka[:, c % 2, :], k_hi[:, c, :].bitcast(F32),
                                 ALU.subtract).then_inc(klo_done, 1)

            def refine(i, s):
                wait(dve, rc_done, i * SUB + s + 1)
                ve.scalar_tensor_tensor(out=gate[:, s, :], in0=gate[:, s, :], scalar=1.0, in1=grec[:, s, :],
                                        op0=ALU.add, op1=ALU.mult).then_inc(rd_done, 1)
                wait(dve, rd_done, i * SUB + s + 1)
                ve.scalar_tensor_tensor(out=grec[:, s, :], in0=gate[:, s, :], scalar=-2.0, in1=grec[:, s, :],
                                        op0=ALU.add, op1=ALU.mult).then_inc(newton, 1)

            def residual(i):
                wait(dve, v_done, i + 1)
                wait(dve, newton, i * SUB + SUB)
                for s in range(SUB):
                    ve.scalar_tensor_tensor(out=grec[:, s, :], in0=acc[s][:, :], scalar=-1.0, in1=grec[:, s, :],
                                            op0=ALU.mult, op1=ALU.mult).then_inc(gated, 1)

            ve.memset(xt[:, :, :, 0:1], 0.0).then_inc(margin, 1)
            statistics(0)
            dve.wait_ge(st_done, SUB)
            aggregate()
            normalise(0)
            dve.wait_ge(consts_in, 32)
            dve.wait_ge(margin, 1)
            for m in "rk":
                for k in range(KC):
                    mix(m, 0, k)
            for n, m in enumerate(WM):
                dve.wait_ge(whi_done, n + 1)
                ve.tensor_tensor(flat(w_lo[m]), flat(raw[m]), flat(w_hi[m]).bitcast(F32),
                                 ALU.subtract).then_inc(wlo_done, 1)
            for m in "rk":
                for k in range(KC):
                    mixed_rest(m, 0, k)
            statistics(1)
            dve.wait_ge(st_done, 2 * SUB)
            aggregate()
            normalise(1)

            def body(i):
                ahead = not is_last(i)
                for s in range(SUB):
                    cap(i, s)
                for c in range(KC):
                    k_rest(i, c)
                    if ahead:
                        mix("r", i + 1, c)
                        mix("k", i + 1, c)
                    refine(i, c)
                two_ahead = not isinstance(i, int) or i < NT - TAIL
                if two_ahead:
                    statistics(i + 2)
                    dve.wait_ge(st_done, i * SUB + 3 * SUB)
                if ahead:
                    mixed_rest("r", i + 1, 0)
                if two_ahead:
                    aggregate()
                if ahead:
                    for k in range(1, KC):
                        mixed_rest("r", i + 1, k)
                if two_ahead:
                    normalise(i + 2)
                if ahead:
                    for k in range(KC):
                        mixed_rest("k", i + 1, k)
                residual(i)

            over_tiles(dve, body, TAIL)

        @block.gpsimd
        def _(pool):
            gp = nc.gpsimd

            def rstd_of(i):
                wait(pool, mv_done, i * SUB + SUB)
                wait(pool, normed, i * SUB)
                gp.tensor_tensor(rstd[:, :], mv[:, :, 1], eps[:, :], ALU.add).then_inc(veps_done, 1)
                wait(pool, veps_done, i + 1)
                gp.tensor_tensor(rstd[:, :], rstd[:, :], half[:, :], ALU.pow).then_inc(rstd_done, 1)

            def difference(i, k):
                wait(pool, xt_left, i * KC + k + 1)
                wait(pool, mix_done["k"], (i - 1) * KC + k + 1)
                gp.tensor_tensor(seqs(diff[:, k, :]), xt[:, k, :, 1:], xt[:, k, :, 0:T],
                                 ALU.subtract).then_inc(diffed, 1)

            def add(i):
                wait(pool, res_in, i * 16 + 16)
                for s in range(SUB):
                    wait(pool, gated, i * SUB + s + 1)
                    gp.tensor_tensor(xres[:, s, :], xres[:, s, :], grec[:, s, :], ALU.add).then_inc(res_done, 1)

            gp.memset(half[:, :], -0.5).then_inc(half_set, 1)
            gp.memset(eps[:, :], LN_EPS).then_inc(half_set, 1)
            pool.wait_ge(half_set, 2)
            pool.wait_ge(margin, 1)
            rstd_of(0)
            for k in range(KC):
                difference(0, k)
            rstd_of(1)

            def body(i):
                for c in range(KC):
                    if not is_last(i):
                        difference(i + 1, c)
                if not isinstance(i, int) or i < NT - TAIL:
                    rstd_of(i + 2)
                add(i)

            over_tiles(pool, body, TAIL)


def decoder(nc, a, out):
    x1 = nc.dram_tensor("x_after_attention", (B, T, C), F32, kind="Internal").ap()
    x2 = nc.dram_tensor("x_after_cross", (B, T, C), F32, kind="Internal").ap()
    attention_pass(nc, a["x"], {m: a["w_" + m] for m in "kvr"}, a["wo_t"], a["cols"], a["bo_b"], a["trem"],
                   a["scanmask"], a["ident"], x1)
    cross_pass(nc, x1, a["ctx"], a["ctx_t"], a["fside"], {m: a["x" + m] for m in ("wq", "wk", "wv", "wo")},
               a["xbias"], a["xbo_b"], a["ident"], x2)
    ffn_pass(nc, x2, {m: a["f" + m] for m in "rkv"}, a["mu"], a["ident"], out)


def layouts(inp):
    import numpy as np

    def chunks_of(w, n):
        a = np.asarray(w).reshape(n, P, w.shape[1] // P, P)
        return np.ascontiguousarray(a.transpose(0, 3, 2, 1)).reshape(n, P, -1)

    def rows(w):
        return np.ascontiguousarray(np.asarray(w).reshape(KC, P, C).transpose(1, 0, 2))

    def columns(names, n):
        return np.ascontiguousarray(np.stack([np.asarray(inp[m]).reshape(n, P).T for m in names], 1))

    def on_all(v):
        return np.ascontiguousarray(np.broadcast_to(np.asarray(v), (P, len(v))))

    out = {"x": np.asarray(inp["x"]), "ctx": np.asarray(inp["ctx_1024"]), "fside": np.asarray(inp["fside_BxSxS2_0"])}
    out["ctx_t"] = np.ascontiguousarray(
        out["ctx"].reshape(NT, BT, T, KC, P).transpose(0, 4, 3, 1, 2)).reshape(NT, P, KC, N)
    for m in "kvr":
        out["w_" + m] = chunks_of(inp[f"L0_attn_W{m}"], HC)
    out["wo_t"] = np.ascontiguousarray(np.asarray(inp["L0_attn_Wo"]).T).reshape(HC, P, C)
    out["cols"] = columns(["L0_attn_" + n for n in ("br", "bk", "bv", "time_decay", "U")], HC)
    out["bo_b"] = on_all(inp["L0_attn_bo"])
    for m in "qkv":
        out["xw" + m] = rows(inp[f"L0_xattn_W{m}"])
    out["xwo"] = rows(np.asarray(inp["L0_xattn_Wo"]).T)
    out["xbias"] = columns(["L0_xattn_bq", "L0_xattn_bk", "L0_xattn_bv"], KC)
    out["xbo_b"] = on_all(inp["L0_xattn_bo"])
    for m in "rkv":
        out["f" + m] = rows(np.asarray(inp[f"L0_ffn_W_{m}"]).T)
    out["mu"] = columns(["L0_ffn_mu_r", "L0_ffn_mu_k"], KC)
    out["trem"] = np.ascontiguousarray(np.broadcast_to(np.arange(T - 1, -1, -1, dtype=np.float32), (P, T)))
    mask = np.ones((P, BT, T + 1), np.float32)
    mask[:, :, 0] = 0
    out["scanmask"] = mask.reshape(P, -1)
    out["ident"] = np.eye(P, dtype=np.float32)
    return out


def kernel(**inputs):
    import concourse.bacc as bacc
    from concourse.bass_utils import run_bass_kernel_spmd

    nc = bacc.Bacc("TRN2", target_bir_lowering=False, num_devices=1)
    arrays, args = {}, {}
    for name, a in layouts(inputs).items():
        arrays[f"in_{name}"] = a
        args[name] = nc.dram_tensor(f"in_{name}", a.shape, mybir.dt.from_np(a.dtype), kind="ExternalInput").ap()
    out = nc.dram_tensor("out_x", (B, T, C), F32, kind="ExternalOutput").ap()
    decoder(nc, args, out)
    r = run_bass_kernel_spmd(nc, [arrays], core_ids=[0])
    return r.results[0]["out_x"]
```

```python
import math
from contextlib import ExitStack

import concourse.bass as bass
from concourse import mybir

F32 = mybir.dt.float32
F32R = mybir.dt.float32r
ALU = mybir.AluOpType
ACT = mybir.ActivationFunctionType
AX = mybir.AxisListType

P = 128
B, T, C = 16, 256, 512
BT = 2
NT = B // BT
N = BT * T
SUB = N // P
KC = C // P
H = 1024
HC = H // P
LN_EPS = 1e-5
EPS = math.exp(-1.0 / 12.0)
MIX = {"k": EPS + 0.3 / 11.0, "v": EPS, "r": EPS / 2.0}
CLIP_LO, CLIP_HI = math.exp(-20.0), math.exp(10.0)
SIG_CAP = 2.0 ** 60
LN_SHIFT = 21
TABLES = "natural_log_exp_and_others"
LAG = 2


def wait(eng, sem, value):
    if not isinstance(value, int) or value > 0:
        eng.wait_ge(sem, value)


def over_tiles(eng, body, tail=1):
    body(0)
    with eng.Fori(1, NT - tail) as i:
        body(i)
    for j in range(NT - tail, NT):
        body(j)


def is_first(i):
    return isinstance(i, int) and i == 0


def is_last(i):
    return isinstance(i, int) and i == NT - 1


def tile_of(dram, i):
    if isinstance(i, int):
        return dram[i * BT:(i + 1) * BT].rearrange("b (h p) c -> p (b h) c", p=P)
    return dram[bass.ds(i * BT, BT)].rearrange("b (h p) c -> p (b h) c", p=P)


def three(pe, out, pairs):
    n = len(pairs)
    for j, ((ah, al), (bh, bl)) in enumerate(pairs):
        pe.matmul(out, ah, bh, start=(j == 0), stop=False)
        pe.matmul(out, ah, bl, start=False, stop=False)
        last = pe.matmul(out, al, bh, start=False, stop=(j == n - 1))
    return last


class Shared:

    def __init__(self, nc, ctx):
        def sb(name, shape):
            return ctx.enter_context(nc.sbuf_tensor(name, shape, F32))

        self.nc, self.slot_base = nc, -(-nc.sbuf_base // 32) * 32
        sb("slots", [P, 12, KC, C])
        self.fold_raw = {m: self.slot("b_raw_" + m, F32, 2 * j) for j, m in enumerate(("wq", "wk", "wv", "wo"))}
        self.ffn_raw = {m: self.slot("c_raw_" + m, F32, 2 * j) for j, m in enumerate("rkv")}
        self.ffn_lo = {m: self.slot(f"c_w{m}_lo", F32R, 2 * j) for j, m in enumerate("rkv")}
        self.ffn_hi = {m: self.slot(f"c_w{m}_hi", F32R, j) for m, j in (("r", 6), ("k", 10), ("v", 11))}
        self.id_sb = sb("ident_sb", [P, P])
        self.xin, self.xres = sb("xin", [P, SUB, C]), sb("xres", [P, SUB, C])
        self.bcol = sb("bcol", [P, 3, KC])
        self.out_row = sb("out_row", [P, C])
        self.mu_sb = sb("mu_sb", [P, 2, KC])
        self.stats, self.mv = sb("stats", [P, SUB, 6]), sb("mv", [P, SUB, 2])
        self.rstd, self.half, self.eps = sb("rstd", [P, SUB]), sb("half", [P, SUB]), sb("eps", [P, SUB])
        self.x1_stored, self.x2_stored = (ctx.enter_context(nc.semaphore(n)) for n in ("x1_stored", "x2_stored"))
        self.bias_in = ctx.enter_context(nc.semaphore("bias_in"))
        self.fold_in = ctx.enter_context(nc.semaphore("fold_in"))
        self.x1_in = ctx.enter_context(nc.semaphore("x1_in"))
        self.ffn_in = ctx.enter_context(nc.semaphore("ffn_in"))
        self.x2_in = ctx.enter_context(nc.semaphore("x2_in"))

    def slot(self, name, dt, j, n=1):
        return self.nc.alloc_sbuf_tensor_at(name, [P, n * KC, C], dt,
                                             offset=self.slot_base + j * KC * C * 4)


def attention_pass(nc, sh, x, w_kvr, wo_t, cols, bo_b, trem, scanmask, ident, x1, cross):
    with ExitStack() as ctx:
        def sb(name, shape, dt=F32):
            return ctx.enter_context(nc.sbuf_tensor("a_" + name, shape, dt))

        def sem(name):
            return ctx.enter_context(nc.semaphore("a_" + name))

        WM = "kvr"
        w_hi = {m: sh.slot(f"a_w{m}_hi", F32R, 2 * j, 2) for j, m in enumerate(WM)}
        w_lo = {m: sh.slot(f"a_w{m}_lo", F32R, 6 + 2 * j, 2) for j, m in enumerate(WM)}
        wo_hi, wo_lo = sb("wo_hi", [P, HC, C], F32R), sb("wo_lo", [P, HC, C], F32R)
        xin, xres, id_sb, stats, mv, rstd, half, eps = (
            sh.xin, sh.xres, sh.id_sb, sh.stats, sh.mv, sh.rstd, sh.half, sh.eps)
        xt_hi, xt_lo = sb("xt_hi", [P, KC, N], F32R), sb("xt_lo", [P, KC, N], F32R)
        bo_sb, trem_sb, mask_sb = sb("bo", [P, C]), sb("trem", [P, T]), sb("mask", [P, BT * (T + 1)])
        col = sb("col", [P, 5, HC])
        nbr, buk, ebv, negw = (sb(n, [P, HC]) for n in ("nbr", "buk", "ebv", "negw"))
        zero = sb("zero", [P, BT, 2])
        shift = sb("shift", [P, 1])
        u = {m: sb("u" + m, [P, BT, T + 2]) for m in WM}
        kt, vv, eu, euv, rt = (sb(n, [P, BT, T]) for n in ("kt", "vv", "eu", "euv", "rt"))
        ee, ev, ss, sv = (sb(n, [P, BT * (T + 1)]) for n in ("ee", "ev", "ss", "sv"))
        dd, rc, yy = (sb(n, [P, BT, T]) for n in ("dd", "rc", "yy"))
        y_hi, y_lo = sb("y_hi", [P, 2, N], F32R), sb("y_lo", [P, 2, N], F32R)
        two = lambda a: a[:, :].rearrange("p (b t) -> p b t", b=BT)
        ee3, ev3, ss3, sv3 = two(ee), two(ev), two(ss), two(sv)
        flat = lambda a: a[:, :, :].rearrange("p b t -> p (b t)")

        ps = {m: ctx.enter_context(nc.psum_tensor("a_ps" + m, [P, BT, T], F32)) for m in WM}
        acc = [ctx.enter_context(nc.psum_tensor(f"a_acc{s}", [P, C], F32)) for s in range(SUB)]
        tps = ctx.enter_context(nc.psum_tensor("a_tps", [P, N], F32))

        def turn_bank(i, k):
            return acc[k] if is_first(i) else tps

        consts_in, x_in, res_in, stored = sem("consts_in"), sem("x_in"), sem("res_in"), sh.x1_stored
        stage_in = [sem(f"stage_in{j}") for j in range(4)]
        proj = {m: sem("proj_" + m) for m in WM}
        wo_done, turned, slot_free = sem("wo_done"), sem("turned"), sem("slot_free")
        u_done = {m: sem("u_done_" + m) for m in WM}
        eu_exp, e_exp, r_exp, ln_done, rc_done, yhi_done, xhi_done, whi_done = (
            sem(n) for n in ("eu_exp", "e_exp", "r_exp", "ln_done", "rc_done", "yhi_done", "xhi_done", "whi_done"))
        k_mix, arg_done, v_mix, r_mix, eu_clip, e_clip, ev_done, s_scan, sv_scan = (
            sem(n) for n in ("k_mix", "arg_done", "v_mix", "r_mix", "eu_clip", "e_clip", "ev_done", "s_scan",
                             "sv_scan"))
        t_done, d_done, newton, y_done, ylo_done, xlo_done, st_done, mv_done, normed, res_done, setup = (
            sem(n) for n in ("t_done", "d_done", "newton", "y_done", "ylo_done", "xlo_done", "st_done", "mv_done",
                             "normed", "res_done", "setup"))
        euv_done, b_done, a_done, rd_done, veps_done, rstd_done, bo_added, wlo_done, consts_set = (
            sem(n) for n in ("euv_done", "b_done", "a_done", "rd_done", "veps_done", "rstd_done", "bo_added",
                             "wlo_done", "consts_set"))

        NCONST = 5
        STAGED = 4 * HC

        def piece(n):
            c, m = divmod(n, 4)
            if m == 3:
                return wo_t[c], wo_hi[:, c, :], wo_lo[:, c, :]
            return w_kvr[WM[m]][c], w_hi[WM[m]][:, c, :], w_lo[WM[m]][:, c, :]

        block = ctx.enter_context(nc.Block())

        @block.sync
        def _(sp):
            sp.dma_start(xin[:, :, :], tile_of(x, 0)).then_inc(x_in, 16)
            for dst, src in ((col[:, :, :], cols), (trem_sb[:, :], trem), (mask_sb[:, :], scanmask),
                             (id_sb[:, :], ident), (bo_sb[:, :], bo_b)):
                sp.dma_start(dst, src).then_inc(consts_in, 16)
            for n in range(STAGED):
                if n >= 4:
                    sp.wait_ge(wlo_done, n - 3)
                sp.dma_start(xres[:, n % 4, :], piece(n)[0]).then_inc(stage_in[n % 4], 16)
                if n == 7:
                    sp.wait_ge(turned, KC)
                    sp.dma_start(xin[:, :, :], tile_of(x, 1)).then_inc(x_in, 16)
            sp.wait_ge(wlo_done, STAGED)
            sp.dma_start(xres[:, :, :], tile_of(x, 0)).then_inc(res_in, 16)

            with sp.Fori(1, NT - 1) as i:
                sp.wait_ge(turned, i * KC + KC)
                sp.dma_start(xin[:, :, :], tile_of(x, i + 1)).then_inc(x_in, 16)
                sp.wait_ge(res_done, i * SUB)
                sp.dma_start(tile_of(x1, i - 1), xres[:, :, :]).then_inc(stored, 16)
                sp.wait_ge(stored, i * 16)
                sp.dma_start(xres[:, :, :], tile_of(x, i)).then_inc(res_in, 16)
            for i in (NT - 1, NT):
                sp.wait_ge(res_done, i * SUB)
                sp.dma_start(tile_of(x1, i - 1), xres[:, :, :]).then_inc(stored, 16)
                if i < NT:
                    sp.wait_ge(stored, i * 16)
                    sp.dma_start(xres[:, :, :], tile_of(x, i)).then_inc(res_in, 16)
                    for m in WM:
                        sp.wait_ge(proj[m], i * HC + KC)
                    for m in ("wq", "wk", "wv", "wo"):
                        sp.dma_start(sh.fold_raw[m][:, :, :], cross[m]).then_inc(sh.fold_in, 16)
                    sp.wait_ge(turned, NT * KC)
                    sp.dma_start(xin[:, :, :], tile_of(x1, 0)).then_inc(sh.x1_in, 16)
                    sp.dma_start(sh.bcol[:, :, :], cross["biases"]).then_inc(sh.bias_in, 16)
                    sp.dma_start(sh.out_row[:, :], cross["bo"]).then_inc(sh.bias_in, 16)

        @block.tensor
        def _(pe):
            te = nc.tensor

            def turn(i, k):
                wait(pe, normed, i * SUB + SUB)
                if not is_first(i):
                    wait(pe, xlo_done, i * KC + k)
                for s in range(SUB):
                    last = te.transpose(turn_bank(i, k)[:, s * P:(s + 1) * P], xin[:, s, k * P:(k + 1) * P], id_sb[:, :])
                last.then_inc(turned, 1)

            def operands(m, c, k):
                w = slice(k * P, (k + 1) * P)
                return ((w_hi[m][:, c, w], w_lo[m][:, c, w]), (xt_hi[:, k, :], xt_lo[:, k, :]))

            def project(i, c):
                g = i * HC + c
                if c < HC - 1:
                    for j, m in enumerate(WM):
                        if is_first(i):
                            pe.wait_ge(wlo_done, 4 * c + j + 1)
                        wait(pe, u_done[m], g)
                        if c == 0 and j == 0:
                            wait(pe, xlo_done, i * KC + KC)
                        three(te, flat(ps[m]), [operands(m, c, k) for k in range(KC)]).then_inc(proj[m], 1)
                    return
                if is_first(i):
                    pe.wait_ge(wlo_done, 4 * c + 3)
                for m in WM:
                    wait(pe, u_done[m], g)
                for k in range(KC):
                    for m in WM:
                        (ah, al), (bh, bl) = operands(m, c, k)
                        te.matmul(flat(ps[m]), ah, bh, start=(k == 0), stop=False)
                        te.matmul(flat(ps[m]), ah, bl, start=False, stop=False)
                        last = te.matmul(flat(ps[m]), al, bh, start=False, stop=(k == KC - 1))
                        if k == KC - 1:
                            last.then_inc(proj[m], 1)
                    if not is_last(i):
                        if k < KC - 1:
                            last.then_inc(slot_free, 1)
                        turn(i + 1, k)

            def output(i, c):
                g = i * HC + c
                if is_first(i):
                    pe.wait_ge(wlo_done, 4 * c + 4)
                wait(pe, ylo_done, g + 1)
                if c == 0:
                    wait(pe, res_done, i * SUB)
                    if is_first(i):
                        pe.wait_ge(xlo_done, KC)
                for s in range(SUB):
                    t = slice(s * P, (s + 1) * P)
                    for a, b in ((y_hi, wo_hi), (y_hi, wo_lo), (y_lo, wo_hi)):
                        last = te.matmul(acc[s][:, :], a[:, c % 2, t], b[:, c, :],
                                         start=(c == 0 and a is y_hi and b is wo_hi),
                                         stop=(c == HC - 1 and a is y_lo))
                last.then_inc(wo_done, 1)

            pe.wait_ge(consts_in, 16 * NCONST)
            for k in range(KC):
                turn(0, k)

            def body(i):
                for c in range(HC):
                    project(i, c)
                    if c >= LAG:
                        output(i, c - LAG)
                    elif not is_first(i):
                        output(i - 1, HC + c - LAG)

            over_tiles(pe, body)
            for c in range(HC - LAG, HC):
                output(NT - 1, c)

        @block.scalar
        def _(act):
            sc = nc.scalar
            sc.preload_act_table_set(TABLES)

            def split_high(n):
                act.wait_ge(stage_in[n % 4], 16 * (n // 4 + 1))
                sc.activation(piece(n)[1], xres[:, n % 4, :], ACT.Copy).then_inc(whi_done, 1)

            def xt_high(i, k):
                wait(act, turned, i * KC + k + 1)
                if not is_first(i):
                    if k < KC - 1:
                        act.wait_ge(slot_free, (i - 1) * (KC - 1) + k + 1)
                    else:
                        act.wait_ge(proj["r"], i * HC)
                sc.activation(xt_hi[:, k, :], turn_bank(i, k)[:, :], ACT.Copy).then_inc(xhi_done, 1)

            def leave(m, i, c):
                g = i * HC + c
                wait(act, {"k": k_mix, "v": v_mix, "r": r_mix}[m], g)
                if m == "v":
                    sc.activation(u["v"][:, :, 0:T + 2:T + 1], zero[:, :, :], ACT.Identity, bias=ebv[:, c:c + 1])
                act.wait_ge(proj[m], g + 1)
                if m == "v":
                    sc.activation(u[m][:, :, 1:T + 1], ps[m][:, :, :], ACT.Identity, bias=ebv[:, c:c + 1],
                                  scale=MIX[m]).then_inc(u_done[m], 1)
                else:
                    sc.activation(u[m][:, :, 1:T + 1], ps[m][:, :, :], ACT.Copy,
                                  scale=MIX[m]).then_inc(u_done[m], 1)

            def exp_k(i, c):
                g = i * HC + c
                act.wait_ge(k_mix, g + 1)
                wait(act, b_done, g)
                sc.activation(eu[:, :, :], kt[:, :, :], ACT.Exp, bias=buk[:, c:c + 1]).then_inc(eu_exp, 1)
                act.wait_ge(arg_done, g + 1)
                sc.activation(ee3[:, :, 1:], ee3[:, :, 1:], ACT.Exp, bias=col[:, 1, c:c + 1]).then_inc(e_exp, 1)

            def exp_r(i, c):
                g = i * HC + c
                act.wait_ge(r_mix, g + 1)
                sc.activation(rt[:, :, :], rt[:, :, :], ACT.Exp, bias=nbr[:, c:c + 1],
                              scale=-1.0).then_inc(r_exp, 1)

            def first_reciprocal(g):
                act.wait_ge(d_done, g + 1)
                wait(act, newton, g)
                sc.activation(rc[:, :, :], dd[:, :, :], ACT.Ln, scale=2.0 ** -LN_SHIFT).then_inc(ln_done, 1)
                act.wait_ge(ln_done, g + 1)
                sc.activation(rc[:, :, :], rc[:, :, :], ACT.Exp, scale=-1.0, bias=shift[:, 0:1]).then_inc(rc_done, 1)

            def y_high(g, c):
                act.wait_ge(y_done, g + 1)
                wait(act, wo_done, g - 1)
                sc.activation(y_hi[:, c % 2, :], flat(yy), ACT.Copy).then_inc(yhi_done, 1)

            for n in range(4):
                split_high(n)
            for k in range(KC):
                xt_high(0, k)
            act.wait_ge(setup, 5)
            act.wait_ge(consts_set, 3)

            def body(i):
                for c in range(HC):
                    g = i * HC + c
                    back = c > 0 or not is_first(i)
                    if is_first(i) and c < HC - 1:
                        for m in range(4):
                            split_high(4 * (c + 1) + m)
                    if c == HC - 1 and not is_last(i):
                        xt_high(i + 1, 0)
                        xt_high(i + 1, 1)
                        first_reciprocal(g - 1)
                        xt_high(i + 1, 2)
                        xt_high(i + 1, 3)
                        y_high(g - 1, c - 1)
                        for m in WM:
                            leave(m, i, c)
                        exp_k(i, c)
                        exp_r(i, c)
                        continue
                    leave("k", i, c)
                    if back:
                        first_reciprocal(g - 1)
                    leave("v", i, c)
                    exp_k(i, c)
                    leave("r", i, c)
                    if back:
                        y_high(g - 1, (c - 1) % HC)
                    exp_r(i, c)

            over_tiles(act, body)
            first_reciprocal(NT * HC - 1)
            y_high(NT * HC - 1, HC - 1)

        @block.vector
        def _(dve):
            ve = nc.vector

            def xt_rest(i, k):
                wait(dve, xhi_done, i * KC + k + 1)
                ve.tensor_tensor(xt_lo[:, k, :], turn_bank(i, k)[:, :], xt_hi[:, k, :].bitcast(F32),
                                 ALU.subtract).then_inc(xlo_done, 1)

            def mix(m, i, c, out, done):
                g = i * HC + c
                dve.wait_ge(u_done[m], g + 1)
                if m == "k":
                    wait(dve, eu_exp, g)
                    wait(dve, arg_done, g)
                if m == "v":
                    wait(dve, euv_done, g)
                    wait(dve, ev_done, g)
                if m == "r":
                    wait(dve, d_done, g)
                ve.scalar_tensor_tensor(out=out[:, :, :], in0=u[m][:, :, 2:], scalar=(1.0 - MIX[m]) / MIX[m],
                                        in1=u[m][:, :, 0:T], op0=ALU.mult, op1=ALU.add).then_inc(done, 1)

            def decayed(i, c):
                g = i * HC + c
                dve.wait_ge(k_mix, g + 1)
                wait(dve, s_scan, g)
                ve.scalar_tensor_tensor(out=ee3[:, :, 1:],
                                        in0=trem_sb[:, :].unsqueeze(1).to_broadcast([P, BT, T]),
                                        scalar=negw[:, c:c + 1], in1=kt[:, :, :],
                                        op0=ALU.mult, op1=ALU.add).then_inc(arg_done, 1)

            def clip_and_scan(g, before_product=None, before_scans=None):
                dve.wait_ge(eu_exp, g + 1)
                ve.tensor_scalar(eu[:, :, :], eu[:, :, :], CLIP_LO, CLIP_HI, ALU.max, ALU.min).then_inc(eu_clip, 1)
                dve.wait_ge(e_exp, g + 1)
                ve.tensor_scalar(ee3[:, :, 1:], ee3[:, :, 1:], CLIP_LO, CLIP_HI, ALU.max, ALU.min).then_inc(e_clip, 1)
                if before_product:
                    before_product()
                dve.wait_ge(e_clip, g + 1)
                wait(dve, sv_scan, g)
                ve.tensor_tensor(ev3[:, :, 1:], ee3[:, :, 1:], vv[:, :, :], ALU.mult).then_inc(ev_done, 1)
                if before_scans:
                    before_scans()
                wait(dve, d_done, g)
                ve.tensor_tensor_scan(ss[:, :], mask_sb[:, :], ee[:, :], 0.0, ALU.mult, ALU.add).then_inc(s_scan, 1)
                dve.wait_ge(ev_done, g + 1)
                wait(dve, y_done, g)
                ve.tensor_tensor_scan(sv[:, :], mask_sb[:, :], ev[:, :], 0.0, ALU.mult, ALU.add).then_inc(sv_scan, 1)

            def one_plus(g):
                dve.wait_ge(r_exp, g + 1)
                ve.tensor_scalar(rt[:, :, :], rt[:, :, :], SIG_CAP, 1.0, ALU.min, ALU.add).then_inc(t_done, 1)

            def denominator(g):
                dve.wait_ge(t_done, g + 1)
                dve.wait_ge(b_done, g + 1)
                wait(dve, rd_done, g)
                ve.tensor_tensor(dd[:, :, :], rt[:, :, :], ss3[:, :, 0:T], ALU.mult).then_inc(d_done, 1)

            def divide(g):
                dve.wait_ge(rd_done, g + 1)
                ve.scalar_tensor_tensor(out=rc[:, :, :], in0=dd[:, :, :], scalar=-2.0, in1=rc[:, :, :],
                                        op0=ALU.add, op1=ALU.mult).then_inc(newton, 1)
                dve.wait_ge(newton, g + 1)
                dve.wait_ge(a_done, g + 1)
                wait(dve, ylo_done, g)
                ve.scalar_tensor_tensor(out=yy[:, :, :], in0=rc[:, :, :], scalar=-1.0, in1=sv3[:, :, 0:T],
                                        op0=ALU.mult, op1=ALU.mult).then_inc(y_done, 1)

            def y_rest(g, c):
                dve.wait_ge(yhi_done, g + 1)
                ve.tensor_tensor(y_lo[:, c % 2, :], flat(yy), y_hi[:, c % 2, :].bitcast(F32),
                                 ALU.subtract).then_inc(ylo_done, 1)

            def statistics(i, s):
                if s == 0:
                    wait(dve, x_in, i * 16 + 16)
                    wait(dve, normed, i * SUB)
                ve.bn_stats(stats[:, s, :], xin[:, s, :]).then_inc(st_done, 1)

            def aggregate(s):
                ve.bn_aggr(mv[:, s, :], stats[:, s, :]).then_inc(mv_done, 1)

            def normalise(i, s):
                if s == 0:
                    dve.wait_ge(rstd_done, i + 1)
                ve.tensor_scalar(xin[:, s, :], xin[:, s, :], mv[:, s, 0:1], rstd[:, s:s + 1],
                                 ALU.subtract, ALU.mult).then_inc(normed, 1)

            def residual(i):
                wait(dve, wo_done, i * HC + HC)
                wait(dve, bo_added, i + 1)
                for s in range(SUB):
                    ve.tensor_tensor(xres[:, s, :], xres[:, s, :], acc[s][:, :], ALU.add).then_inc(res_done, 1)

            for a in (u["k"], u["r"]):
                ve.memset(a[:, :, 0:T + 2:T + 1], 0.0)
            for a in (ee3, ev3):
                ve.memset(a[:, :, 0:1], 0.0)
            for s in range(SUB):
                statistics(0, s)
            dve.wait_ge(st_done, SUB)
            for s in range(SUB):
                aggregate(s)
            for s in range(SUB):
                normalise(0, s)
            dve.wait_ge(consts_in, 16 * NCONST)
            ve.tensor_scalar(nbr[:, :], col[:, 0, :], -1.0, None, ALU.mult).then_inc(setup, 1)
            ve.tensor_tensor(buk[:, :], col[:, 1, :], col[:, 4, :], ALU.add).then_inc(setup, 1)
            ve.tensor_scalar(ebv[:, :], col[:, 2, :], MIX["v"], None, ALU.mult).then_inc(setup, 1)
            ve.tensor_scalar(negw[:, :], col[:, 3, :], 0.0, -1.0, ALU.max, ALU.mult).then_inc(setup, 1)
            ve.memset(zero[:, :, :], 0.0).then_inc(setup, 1)
            for k in range(KC):
                xt_rest(0, k)
            dve.wait_ge(setup, 5)

            def body(i):
                for c in range(HC):
                    g = i * HC + c
                    back = c > 0 or not is_first(i)
                    ahead = not is_last(i)
                    if back:
                        one_plus(g - 1)
                    if c == HC - 1 and ahead:
                        xt_rest(i + 1, 1)
                        denominator(g - 1)
                        xt_rest(i + 1, 2)
                        divide(g - 1)
                        xt_rest(i + 1, 3)
                        y_rest(g - 1, c - 1)
                        mix("k", i, c, kt, k_mix)
                        decayed(i, c)
                        mix("v", i, c, vv, v_mix)
                        mix("r", i, c, rt, r_mix)
                        clip_and_scan(g)
                        continue
                    if back:
                        denominator(g - 1)
                    mix("k", i, c, kt, k_mix)
                    decayed(i, c)
                    if ahead and c in (2, 3):
                        statistics(i + 1, 2 * c - 4)
                        statistics(i + 1, 2 * c - 3)
                        dve.wait_ge(st_done, (i + 1) * SUB + 2 * c - 2)
                    mix("v", i, c, vv, v_mix)
                    if ahead and c in (2, 3):
                        aggregate(2 * c - 4)
                        aggregate(2 * c - 3)
                    if back:
                        divide(g - 1)
                    if ahead and c in (5, 6):
                        normalise(i + 1, 2 * c - 10)
                        normalise(i + 1, 2 * c - 9)
                    mix("r", i, c, rt, r_mix)
                    clip_and_scan(g, (lambda: y_rest(g - 1, (c - 1) % HC)) if back else None,
                                  (lambda: xt_rest(i + 1, 0)) if ahead and c == HC - 2 else None)
                    if c == LAG - 1 and not is_first(i):
                        residual(i - 1)

            over_tiles(dve, body)
            g = NT * HC - 1
            one_plus(g)
            denominator(g)
            divide(g)
            y_rest(g, HC - 1)
            residual(NT - 1)

        @block.gpsimd
        def _(pool):
            gp = nc.gpsimd

            def rstd_of(i):
                wait(pool, mv_done, i * SUB + SUB)
                wait(pool, normed, i * SUB)
                gp.tensor_tensor(rstd[:, :], mv[:, :, 1], eps[:, :], ALU.add).then_inc(veps_done, 1)
                pool.wait_ge(veps_done, i + 1)
                gp.tensor_tensor(rstd[:, :], rstd[:, :], half[:, :], ALU.pow).then_inc(rstd_done, 1)

            def split_rest(n):
                pool.wait_ge(whi_done, n + 1)
                gp.tensor_tensor(piece(n)[2], xres[:, n % 4, :], piece(n)[1].bitcast(F32),
                                 ALU.subtract).then_inc(wlo_done, 1)

            def front(g):
                pool.wait_ge(v_mix, g + 1)
                pool.wait_ge(eu_clip, g + 1)
                wait(pool, a_done, g)
                gp.tensor_tensor(euv[:, :, :], eu[:, :, :], vv[:, :, :], ALU.mult).then_inc(euv_done, 1)
                pool.wait_ge(s_scan, g + 1)
                gp.tensor_tensor(ss3[:, :, 0:T], ss3[:, :, 0:T], eu[:, :, :], ALU.add).then_inc(b_done, 1)
                pool.wait_ge(sv_scan, g + 1)
                pool.wait_ge(euv_done, g + 1)
                gp.tensor_tensor(sv3[:, :, 0:T], sv3[:, :, 0:T], euv[:, :, :], ALU.add).then_inc(a_done, 1)

            def back_of(g):
                pool.wait_ge(rc_done, g + 1)
                gp.tensor_tensor(dd[:, :, :], dd[:, :, :], rc[:, :, :], ALU.mult).then_inc(rd_done, 1)

            gp.memset(half[:, :], -0.5).then_inc(consts_set, 1)
            gp.memset(shift[:, :], -LN_SHIFT * math.log(2.0)).then_inc(consts_set, 1)
            gp.memset(eps[:, :], LN_EPS).then_inc(consts_set, 1)
            pool.wait_ge(consts_set, 3)
            rstd_of(0)
            for n in range(4):
                split_rest(n)
            pool.wait_ge(consts_in, 16 * NCONST)

            def body(i):
                for c in range(HC):
                    g = i * HC + c
                    for m in range(4):
                        if m == 2 and (c > 0 or not is_first(i)):
                            back_of(g - 1)
                        if is_first(i) and c < HC - 1:
                            split_rest(4 * (c + 1) + m)
                    if c == 0 and not is_first(i):
                        pool.wait_ge(res_in, i * 16)
                        for s in range(SUB):
                            last = gp.tensor_tensor(xres[:, s, :], xres[:, s, :], bo_sb[:, :], ALU.add)
                        last.then_inc(bo_added, 1)
                    front(g)
                    if c == 3 and not is_last(i):
                        rstd_of(i + 1)

            over_tiles(pool, body)
            back_of(NT * HC - 1)
            pool.wait_ge(res_in, NT * 16)
            for s in range(SUB):
                last = gp.tensor_tensor(xres[:, s, :], xres[:, s, :], bo_sb[:, :], ALU.add)
            last.then_inc(bo_added, 1)


def cross_pass(nc, sh, x1, ctx_in, ctx_t, fside, x2, ffn):
    with ExitStack() as ctx:
        def sb(name, shape, dt=F32):
            return ctx.enter_context(nc.sbuf_tensor("b_" + name, shape, dt))

        def sem(name):
            return ctx.enter_context(nc.semaphore("b_" + name))

        SCALE = 1.0 / math.sqrt(32.0)
        raw = sh.fold_raw
        m_hi, m_lo, l_hi, l_lo, xt_hi, xt_lo = (
            sh.slot("b_" + n, F32R, j) for n, j in (("m_hi", 1), ("m_lo", 3), ("l_hi", 5), ("l_lo", 7),
                                                    ("xt_hi", 10), ("xt_lo", 11)))
        ct, cx = sh.slot("b_ct", F32, 8), sh.slot("b_cx", F32, 9)
        bcol, out_row, id_sb, xin, xres, stats, mv, rstd, half, eps = (
            sh.bcol, sh.out_row, sh.id_sb, sh.xin, sh.xres, sh.stats, sh.mv, sh.rstd, sh.half, sh.eps)
        bwide = sb("bwide", [P, 2, KC, P])
        qb = sb("qb", [P, KC])
        rk_row = sb("rk_row", [P, C])
        bqk = sb("bqk", [P, 1])
        junk = sb("junk", [P, C])
        q_hi, q_lo = sb("q_hi", [P, KC, N], F32R), sb("q_lo", [P, KC, N], F32R)
        ct_hi, ct_lo = sb("ct_hi", [P, KC, N], F32R), sb("ct_lo", [P, KC, N], F32R)
        cx_hi, cx_lo = sb("cx_hi", [P, SUB, C], F32R), sb("cx_lo", [P, SUB, C], F32R)
        fs, pr = sb("fs", [P, SUB, T]), sb("pr", [P, SUB, T])
        pt_hi, pt_lo = sb("pt_hi", [P, BT, 2 * T], F32R), sb("pt_lo", [P, BT, 2 * T], F32R)
        pc_hi, pc_lo = sb("pc_hi", [P, KC, N], F32R), sb("pc_lo", [P, KC, N], F32R)
        rq_next, rq, mx, nb, rowsum, rinv = (sb(n, [P, SUB]) for n in ("rq_next", "rq", "mx", "nb", "rowsum",
                                                                      "rinv"))
        flat = lambda a: a[:, :, :].rearrange("p a b -> p (a b)")

        bank = [ctx.enter_context(nc.psum_tensor(f"b_bank{j}", [P, N], F32)) for j in range(4)]
        acc = [ctx.enter_context(nc.psum_tensor(f"b_acc{s}", [P, C], F32)) for s in range(SUB)]

        x_in, res_in, cx_in, ct_in, fs_in = (sem(n) for n in ("x_in", "res_in", "cx_in", "ct_in", "fs_in"))
        stored = sh.x2_stored
        fold_done, fold_left, bwide_done = sem("fold_done"), sem("fold_left"), sem("bwide_done")
        turned, q_proj, sc_done, pt_done, pc_done, out_done = (
            sem(n) for n in ("turned", "q_proj", "sc_done", "pt_done", "pc_done", "out_done"))
        xhi_done, qhi_done, exp_done, pthi_done, pchi_done, cxhi_done, cthi_done, mlhi_done = (
            sem(n) for n in ("xhi_done", "qhi_done", "exp_done", "pthi_done", "pchi_done", "cxhi_done", "cthi_done",
                             "mlhi_done"))
        xlo_done, qlo_done, sc_left, mx_done, nb_done, rinv_done, ptlo_done, pclo_done, res_done = (
            sem(n) for n in ("xlo_done", "qlo_done", "sc_left", "mx_done", "nb_done", "rinv_done", "ptlo_done",
                             "pclo_done", "res_done"))
        st_done, mv_done, normed, rq_made, rq_moved = (
            sem(n) for n in ("st_done", "mv_done", "normed", "rq_made", "rq_moved"))
        veps_done, rstd_done, bo_added, cxlo_done, ctlo_done = (
            sem(n) for n in ("veps_done", "rstd_done", "bo_added", "cxlo_done", "ctlo_done"))
        fwhi_done = sem("fwhi_done")

        def ct_view(i):
            sel = ctx_t[i:i + 1] if isinstance(i, int) else ctx_t[bass.ds(i, 1)]
            return sel.rearrange("o p k n -> p (o k) n")

        def fs_view(i):
            return tile_of(fside, i)

        def ffn_slots(m):
            return sh.ffn_hi[m], sh.ffn_raw[m], sh.ffn_lo[m]

        NFOLD = 2 * KC + 4
        TAIL = 2
        block = ctx.enter_context(nc.Block())

        @block.sync
        def _(sp):
            sp.dma_start(ct[:, :, :], ct_view(0)).then_inc(ct_in, 16)
            sp.dma_start(fs[:, :, :], fs_view(0)).then_inc(fs_in, 16)
            sp.dma_start(cx[:, :, :], tile_of(ctx_in, 0)).then_inc(cx_in, 16)
            sp.wait_ge(sh.x1_stored, 16 * NT)
            sp.dma_start(xres[:, :, :], tile_of(x1, 0)).then_inc(res_in, 16)
            sp.wait_ge(turned, KC)
            sp.wait_ge(rq_made, SUB)
            sp.dma_start(xin[:, :, :], tile_of(x1, 1)).then_inc(x_in, 16)
            sp.wait_ge(turned, 2 * KC)
            sp.wait_ge(rq_made, 2 * SUB)
            sp.dma_start(xin[:, :, :], tile_of(x1, 2)).then_inc(x_in, 16)
            sp.wait_ge(fold_left, NFOLD)
            for m in "rkv":
                sp.dma_start(sh.ffn_raw[m][:, :, :], ffn[m]).then_inc(sh.ffn_in, 16)
            sp.dma_start(sh.mu_sb[:, :, :], ffn["mu"]).then_inc(sh.ffn_in, 16)

            def body(i):
                more = not is_last(i)
                if more:
                    sp.wait_ge(ctlo_done, (i + 1) * KC)
                    sp.dma_start(ct[:, :, :], ct_view(i + 1)).then_inc(ct_in, 16)
                    sp.wait_ge(cxlo_done, (i + 1) * SUB)
                    sp.dma_start(cx[:, :, :], tile_of(ctx_in, i + 1)).then_inc(cx_in, 16)
                    sp.wait_ge(sc_left, i * SUB + SUB)
                    sp.dma_start(fs[:, :, :], fs_view(i + 1)).then_inc(fs_in, 16)
                if not isinstance(i, int) or i <= NT - 3:
                    sp.wait_ge(rq_made, i * SUB + 3 * SUB)
                    sp.wait_ge(turned, i * KC + 3 * KC)
                    if isinstance(i, int) and i == NT - 3:
                        sp.dma_start(xin[:, :, :], tile_of(x2, 0)).then_inc(sh.x2_in, 16)
                    else:
                        sp.dma_start(xin[:, :, :], tile_of(x1, i + 3)).then_inc(x_in, 16)
                sp.wait_ge(res_done, i * SUB + SUB)
                sp.dma_start(tile_of(x2, i), xres[:, :, :]).then_inc(stored, 16)
                if more:
                    sp.wait_ge(stored, i * 16 + 16)
                    sp.dma_start(xres[:, :, :], tile_of(x1, i + 1)).then_inc(res_in, 16)

            over_tiles(sp, body, 3)

        @block.tensor
        def _(pe):
            te = nc.tensor

            def cut(a, k, j):
                return a[:, k, j * P:(j + 1) * P]

            def fold(out, lhs, rhs):
                for e in range(KC):
                    last = te.matmul(out, lhs(e), rhs(e), start=(e == 0), stop=(e == KC - 1))
                return last

            def fold_queries():
                pe.wait_ge(sh.fold_in, 16 * 4)
                pe.wait_ge(bwide_done, 2)
                fold(bank[3][:, :], lambda e: bwide[:, 0, e, :], lambda e: raw["wq"][:, e, :]).then_inc(fold_done, 1)
                for j in range(KC):
                    last = fold(bank[2][:, j:j + 1], lambda e: cut(raw["wk"], e, j), lambda e: bcol[:, 0, e:e + 1])
                last.then_inc(fold_done, 1)
                fold(bank[1][:, 0:1], lambda e: bwide[:, 0, e, :], lambda e: bcol[:, 0, e:e + 1]).then_inc(fold_done, 1)
                for j in range(KC):
                    fold(acc[j][:, :], lambda e: cut(raw["wq"], e, j),
                         lambda e: raw["wk"][:, e, :]).then_inc(fold_done, 1)

            def fold_outputs():
                fold(bank[0][:, :], lambda e: bwide[:, 1, e, :], lambda e: raw["wo"][:, e, :]).then_inc(fold_done, 1)
                for j in range(KC):
                    pe.wait_ge(fold_left, 3 + j + 1)
                    fold(acc[j][:, :], lambda e: cut(raw["wv"], e, j),
                         lambda e: raw["wo"][:, e, :]).then_inc(fold_done, 1)

            def turn(i, k):
                wait(pe, normed, i * SUB + SUB)
                if k < 2 and not is_first(i):
                    wait(pe, ptlo_done, (i - 2) * BT + k + 1)
                    wait(pe, xlo_done, (i - 1) * KC + k + 3)
                elif k >= 2:
                    wait(pe, xlo_done, i * KC + k - 1)
                for s in range(SUB):
                    last = te.transpose(bank[2 + k % 2][:, s * P:(s + 1) * P], xin[:, s, k * P:(k + 1) * P],
                                        id_sb[:, :])
                last.then_inc(turned, 1)

            def query(i, c):
                if c == 0:
                    wait(pe, xlo_done, i * KC + KC)
                if c >= 2:
                    wait(pe, qlo_done, i * KC + c - 1)
                elif not is_first(i):
                    wait(pe, sc_left, (i - 1) * SUB + c + 1)
                else:
                    wait(pe, fold_left, 3 + KC + 1)
                three(te, bank[c % 2][:, :],
                      [((cut(m_hi, k, c), cut(m_lo, k, c)), (xt_hi[:, k, :], xt_lo[:, k, :]))
                       for k in range(KC)]).then_inc(q_proj, 1)

            def scores(i, s):
                b = s // 2
                if s == 0:
                    wait(pe, qlo_done, i * KC + KC)
                    wait(pe, ctlo_done, i * KC + KC)
                if s < 2:
                    wait(pe, pclo_done, (i - 1) * KC + 3 + s)
                elif not is_last(i):
                    wait(pe, xlo_done, (i + 1) * KC + s + 1)
                keys = slice(b * T, (b + 1) * T)
                three(te, bank[s][:, 0:T],
                      [((cut(q_hi, k, s), cut(q_lo, k, s)), (ct_hi[:, k, keys], ct_lo[:, k, keys]))
                       for k in range(KC)]).then_inc(sc_done, 1)

            def turn_probs(i, b):
                wait(pe, exp_done, i * SUB + 2 * b + 2)
                wait(pe, sc_left, i * SUB + 3 + b)
                if not is_last(i):
                    wait(pe, xlo_done, (i + 1) * KC + 3 + b)
                for kk in range(2):
                    for h in range(2):
                        last = te.transpose(bank[2 + b][:, kk * T + h * P:kk * T + (h + 1) * P],
                                            pr[:, 2 * b + h, kk * P:(kk + 1) * P], id_sb[:, :])
                last.then_inc(pt_done, 1)

            def context(i, c):
                if c == 0:
                    wait(pe, ptlo_done, i * BT + BT)
                    wait(pe, cxlo_done, i * SUB + SUB)
                if c >= 2:
                    wait(pe, pclo_done, i * KC + c - 1)
                elif is_last(i):
                    wait(pe, sc_left, i * SUB + c + 1)
                else:
                    wait(pe, qlo_done, (i + 1) * KC + 3 + c)
                for b in range(BT):
                    last = three(te, bank[c % 2][:, b * T:(b + 1) * T],
                                 [((cut(cx_hi, 2 * b + kk, c), cut(cx_lo, 2 * b + kk, c)),
                                   (pt_hi[:, b, kk * T:(kk + 1) * T], pt_lo[:, b, kk * T:(kk + 1) * T]))
                                  for kk in range(2)])
                last.then_inc(pc_done, 1)

            def output(i, c):
                wait(pe, pclo_done, i * KC + c + 1)
                if c == 0:
                    wait(pe, res_done, i * SUB)
                    if is_first(i):
                        pe.wait_ge(fold_left, NFOLD)
                for s in range(SUB):
                    for a, b in ((pc_hi, l_hi), (pc_hi, l_lo), (pc_lo, l_hi)):
                        last = te.matmul(acc[s][:, :], cut(a, c, s), b[:, c, :],
                                         start=(c == 0 and a is pc_hi and b is l_hi),
                                         stop=(c == KC - 1 and a is pc_lo))
                if c == KC - 1:
                    last.then_inc(out_done, 1)

            fold_queries()
            pe.wait_ge(fold_left, 2)
            for k in range(KC):
                turn(0, k)
            fold_outputs()
            for c in range(KC):
                query(0, c)
            for k in range(KC):
                turn(1, k)

            def body(i):
                two_ahead = not isinstance(i, int) or i < NT - TAIL
                for s in range(SUB):
                    scores(i, s)
                if not is_last(i):
                    for c in range(KC - 1):
                        query(i + 1, c)
                turn_probs(i, 0)
                turn_probs(i, 1)
                if not is_last(i):
                    query(i + 1, KC - 1)
                context(i, 0)
                context(i, 1)
                for c in range(KC):
                    output(i, c)
                    if c < 2:
                        context(i, c + 2)
                    if two_ahead:
                        turn(i + 2, c)

            over_tiles(pe, body, TAIL)

        @block.scalar
        def _(act):
            sc = nc.scalar
            sc.preload_act_table_set(TABLES)

            def x_high(i, k):
                wait(act, turned, i * KC + k + 1)
                sc.activation(xt_hi[:, k, :], bank[2 + k % 2][:, :], ACT.Copy).then_inc(xhi_done, 1)

            def q_high(i, c):
                wait(act, q_proj, i * KC + c + 1)
                sc.activation(q_hi[:, c, :], bank[c % 2][:, :], ACT.Identity, bias=qb[:, c:c + 1]).then_inc(qhi_done, 1)

            def context_high(i, k):
                wait(act, ct_in, i * 16 + 16)
                wait(act, sc_done, i * SUB)
                sc.activation(ct_hi[:, k, :], ct[:, k, :], ACT.Copy).then_inc(cthi_done, 1)

            def context_high2(i, s):
                wait(act, cx_in, i * 16 + 16)
                wait(act, pc_done, i * KC)
                sc.activation(cx_hi[:, s, :], cx[:, s, :], ACT.Copy).then_inc(cxhi_done, 1)

            def ffn_high(m, k):
                act.wait_ge(sh.ffn_in, 16 * 4)
                if m != "r":
                    act.wait_ge(q_proj, NT * KC)
                sc.activation(ffn_slots(m)[0][:, k, :], ffn_slots(m)[1][:, k, :], ACT.Copy).then_inc(fwhi_done, 1)

            def exponent(i, s):
                wait(act, nb_done, i * SUB + s + 1)
                if s == 0:
                    wait(act, rinv_done, i)
                sc.activation(pr[:, s, :], pr[:, s, :], ACT.Exp, scale=SCALE, bias=nb[:, s:s + 1],
                              accum_out=rowsum[:, s:s + 1]).then_inc(exp_done, 1)

            def probs_high(i, b):
                wait(act, pt_done, i * BT + b + 1)
                sc.activation(pt_hi[:, b, :], bank[2 + b][:, :], ACT.Copy).then_inc(pthi_done, 1)

            def pc_high(i, c):
                wait(act, pc_done, i * KC + c + 1)
                sc.activation(pc_hi[:, c, :], bank[c % 2][:, :], ACT.Copy).then_inc(pchi_done, 1)

            def fold_high(n):
                act.wait_ge(fold_done, 3 + n + n // KC + 1)
                dst = (m_hi, l_hi)[n // KC][:, n % KC, :]
                sc.activation(dst, acc[n % KC][:, :], ACT.Copy).then_inc(mlhi_done, 1)

            for k in range(KC):
                context_high(0, k)
            for n in range(KC):
                fold_high(n)
            for k in range(KC):
                x_high(0, k)
            for s in range(SUB):
                context_high2(0, s)
            for n in range(KC):
                fold_high(KC + n)
            for c in range(KC):
                q_high(0, c)
            for k in range(KC):
                x_high(1, k)

            def body(i):
                ahead = not is_last(i)
                two_ahead = not isinstance(i, int) or i < NT - TAIL
                for s in range(SUB):
                    exponent(i, s)
                if ahead:
                    for c in range(KC - 1):
                        q_high(i + 1, c)
                probs_high(i, 0)
                probs_high(i, 1)
                if ahead:
                    context_high(i + 1, 0)
                    context_high(i + 1, 1)
                    q_high(i + 1, KC - 1)
                    context_high(i + 1, 2)
                    context_high(i + 1, 3)
                for c in range(KC):
                    pc_high(i, c)
                    if c >= 2 and two_ahead:
                        x_high(i + 2, c - 2)
                    if not ahead:
                        ffn_high("k", c)
                        ffn_high("v", c)
                if two_ahead:
                    x_high(i + 2, 2)
                    x_high(i + 2, 3)
                if ahead:
                    for s in range(SUB):
                        context_high2(i + 1, s)
                if ahead and not two_ahead:
                    for k in range(KC):
                        ffn_high("r", k)

            over_tiles(act, body, TAIL)

        @block.vector
        def _(dve):
            ve = nc.vector

            def rest(out, src, high, done):
                ve.tensor_tensor(out, src, high.bitcast(F32), ALU.subtract).then_inc(done, 1)

            def x_rest(i, k):
                wait(dve, xhi_done, i * KC + k + 1)
                rest(xt_lo[:, k, :], bank[2 + k % 2][:, :], xt_hi[:, k, :], xlo_done)

            def q_rest(i, c):
                wait(dve, qhi_done, i * KC + c + 1)
                ve.scalar_tensor_tensor(out=q_lo[:, c, :], in0=bank[c % 2][:, :], scalar=qb[:, c:c + 1],
                                        in1=q_hi[:, c, :].bitcast(F32), op0=ALU.add,
                                        op1=ALU.subtract).then_inc(qlo_done, 1)

            def score(i, s):
                g = i * SUB + s
                wait(dve, sc_done, g + 1)
                if s == 0:
                    wait(dve, fs_in, i * 16 + 16)
                    wait(dve, rq_moved, i + 1)
                    wait(dve, pt_done, i * BT)
                ve.scalar_tensor_tensor(out=pr[:, s, :], in0=bank[s][:, 0:T], scalar=rq[:, s:s + 1],
                                        in1=fs[:, s, :], op0=ALU.add, op1=ALU.add).then_inc(sc_left, 1)
                wait(dve, sc_left, g + 1)
                wait(dve, nb_done, g)
                ve.reduce_max(mx[:, s:s + 1], pr[:, s, :], AX.X).then_inc(mx_done, 1)
                wait(dve, mx_done, g + 1)
                ve.tensor_scalar(nb[:, s:s + 1], mx[:, s:s + 1], -SCALE, None, ALU.mult).then_inc(nb_done, 1)

            def probs_rest(i, b):
                wait(dve, pthi_done, i * BT + b + 1)
                rest(pt_lo[:, b, :], bank[2 + b][:, :], pt_hi[:, b, :], ptlo_done)

            def pc_rest(i, c):
                wait(dve, pchi_done, i * KC + c + 1)
                rest(pc_lo[:, c, :], bank[c % 2][:, :], pc_hi[:, c, :], pclo_done)

            def inverse(i):
                wait(dve, exp_done, i * SUB + SUB)
                wait(dve, res_done, i * SUB)
                ve.reciprocal(rinv[:, :], rowsum[:, :]).then_inc(rinv_done, 1)

            def residual(i):
                wait(dve, out_done, i + 1)
                wait(dve, bo_added, i + 1)
                wait(dve, rinv_done, i + 1)
                for s in range(SUB):
                    ve.scalar_tensor_tensor(out=xres[:, s, :], in0=acc[s][:, :], scalar=rinv[:, s:s + 1],
                                            in1=xres[:, s, :], op0=ALU.mult, op1=ALU.add).then_inc(res_done, 1)

            def statistics(i, subs=range(SUB)):
                if 0 not in subs:
                    pass
                elif is_first(i):
                    dve.wait_ge(sh.x1_in, 16)
                elif isinstance(i, int) and i == NT:
                    dve.wait_ge(sh.x2_in, 16)
                else:
                    wait(dve, x_in, i * 16)
                for s in subs:
                    ve.bn_stats(stats[:, s, :], xin[:, s, :]).then_inc(st_done, 1)

            def aggregate():
                for s in range(SUB):
                    ve.bn_aggr(mv[:, s, :], stats[:, s, :]).then_inc(mv_done, 1)

            def normalise(i):
                wait(dve, rstd_done, i + 1)
                for s in range(SUB):
                    ve.tensor_scalar(xin[:, s, :], xin[:, s, :], mv[:, s, 0:1], rstd[:, s:s + 1],
                                     ALU.subtract, ALU.mult).then_inc(normed, 1)

            def row_products(i, subs=range(SUB)):
                for s in subs:
                    wait(dve, normed, i * SUB + s + 1)
                    wait(dve, rq_made, i * SUB + s)
                    wait(dve, rq_moved, i)
                    ve.tensor_tensor_reduce(out=junk[:, :], in0=xin[:, s, :], in1=rk_row[:, :], scale=1.0,
                                            scalar=bqk[:, 0:1], op0=ALU.mult, op1=ALU.add,
                                            accum_out=rq_next[:, s:s + 1]).then_inc(rq_made, 1)

            def move_rq(i):
                wait(dve, rq_made, i * SUB + SUB)
                if not is_first(i):
                    wait(dve, sc_left, i * SUB)
                ve.tensor_copy(rq[:, :], rq_next[:, :]).then_inc(rq_moved, 1)

            def fold_rest(n):
                dve.wait_ge(mlhi_done, n + 1)
                hi, lo = ((m_hi, m_lo), (l_hi, l_lo))[n // KC]
                rest(lo[:, n % KC, :], acc[n % KC][:, :], hi[:, n % KC, :], fold_left)

            dve.wait_ge(sh.bias_in, 32)
            for j in range(2):
                ve.tensor_copy(bwide[:, j, :, :],
                               bcol[:, 1 + j, :].unsqueeze(2).to_broadcast([P, KC, P])).then_inc(bwide_done, 1)
            statistics(0)
            dve.wait_ge(st_done, SUB)
            aggregate()
            for n, (dst, src) in enumerate(((rk_row[:, :], bank[3][:, :]), (qb[:, :], bank[2][:, 0:KC]),
                                            (bqk[:, :], bank[1][:, 0:1]))):
                dve.wait_ge(fold_done, n + 1)
                ve.tensor_copy(dst, src).then_inc(fold_left, 1)
            normalise(0)
            dve.wait_ge(fold_left, 3)
            row_products(0)
            move_rq(0)
            for n in range(KC):
                fold_rest(n)
            for k in range(KC):
                x_rest(0, k)
            statistics(1)
            dve.wait_ge(st_done, 2 * SUB)
            aggregate()
            dve.wait_ge(fold_done, 3 + KC + 1)
            ve.tensor_tensor(out_row[:, :], out_row[:, :], bank[0][:, :], ALU.add).then_inc(fold_left, 1)
            for n in range(KC):
                fold_rest(KC + n)
            normalise(1)
            for c in range(KC):
                q_rest(0, c)
            row_products(1)
            for k in range(KC):
                x_rest(1, k)

            def body(i):
                ahead = not is_last(i)
                two_ahead = not isinstance(i, int) or i < NT - TAIL
                for s in range(SUB):
                    score(i, s)
                if ahead:
                    move_rq(i + 1)
                    statistics(i + 2, (0, 1))
                    q_rest(i + 1, 0)
                    statistics(i + 2, (2, 3))
                    dve.wait_ge(st_done, i * SUB + 3 * SUB)
                    q_rest(i + 1, 1)
                    aggregate()
                    inverse(i)
                    q_rest(i + 1, 2)
                else:
                    inverse(i)
                probs_rest(i, 0)
                probs_rest(i, 1)
                if ahead:
                    q_rest(i + 1, KC - 1)
                for c in range(KC):
                    pc_rest(i, c)
                    if c == 0 and ahead:
                        normalise(i + 2)
                    if c == 1 and two_ahead:
                        row_products(i + 2)
                    if c >= 2 and two_ahead:
                        x_rest(i + 2, c - 2)
                if two_ahead:
                    x_rest(i + 2, 2)
                    x_rest(i + 2, 3)
                residual(i)

            over_tiles(dve, body, TAIL)

        @block.gpsimd
        def _(pool):
            gp = nc.gpsimd

            def rstd_of(i):
                wait(pool, mv_done, i * SUB + SUB)
                wait(pool, normed, i * SUB)
                gp.tensor_tensor(rstd[:, :], mv[:, :, 1], eps[:, :], ALU.add).then_inc(veps_done, 1)
                wait(pool, veps_done, i + 1)
                gp.tensor_tensor(rstd[:, :], rstd[:, :], half[:, :], ALU.pow).then_inc(rstd_done, 1)

            def context_rest(i, k):
                wait(pool, cthi_done, i * KC + k + 1)
                gp.tensor_tensor(ct_lo[:, k, :], ct[:, k, :], ct_hi[:, k, :].bitcast(F32),
                                 ALU.subtract).then_inc(ctlo_done, 1)

            def context_rest2(i, s):
                wait(pool, cxhi_done, i * SUB + s + 1)
                gp.tensor_tensor(cx_lo[:, s, :], cx[:, s, :], cx_hi[:, s, :].bitcast(F32),
                                 ALU.subtract).then_inc(cxlo_done, 1)

            def ffn_rest(n, m, k):
                pool.wait_ge(fwhi_done, n + 1)
                hi, raw_m, lo = ffn_slots(m)
                gp.tensor_tensor(lo[:, k, :], raw_m[:, k, :], hi[:, k, :].bitcast(F32), ALU.subtract)

            def add_bias(i):
                wait(pool, res_in, i * 16 + 16)
                for s in range(SUB):
                    last = gp.tensor_tensor(xres[:, s, :], xres[:, s, :], out_row[:, :], ALU.add)
                last.then_inc(bo_added, 1)

            rstd_of(0)
            for k in range(KC):
                context_rest(0, k)
            for s in range(SUB):
                context_rest2(0, s)
            rstd_of(1)
            pool.wait_ge(fold_left, NFOLD)

            def body(i):
                if not is_last(i):
                    rstd_of(i + 2)
                    for k in range(KC):
                        context_rest(i + 1, k)
                add_bias(i)
                if not is_last(i):
                    for s in range(SUB):
                        context_rest2(i + 1, s)
                    if isinstance(i, int) and i == NT - TAIL:
                        for k in range(KC):
                            ffn_rest(k, "r", k)
                else:
                    for k in range(KC):
                        ffn_rest(KC + 2 * k, "k", k)
                        ffn_rest(KC + 2 * k + 1, "v", k)

            over_tiles(pool, body, TAIL)


def ffn_pass(nc, sh, x2, x3):
    with ExitStack() as ctx:
        def sb(name, shape, dt=F32):
            return ctx.enter_context(nc.sbuf_tensor("c_" + name, shape, dt))

        def sem(name):
            return ctx.enter_context(nc.semaphore("c_" + name))

        WM = "rkv"
        w_hi, w_lo = sh.ffn_hi, sh.ffn_lo
        mu_sb, id_sb, xin, xres, stats, mv, rstd, half, eps = (
            sh.mu_sb, sh.id_sb, sh.xin, sh.xres, sh.stats, sh.mv, sh.rstd, sh.half, sh.eps)
        xt = sb("xt", [P, KC, BT, T + 1])
        diff = sh.slot("c_diff", F32, 1)
        mixed = {m: sh.slot("c_mixed_" + m, F32, j) for m, j in (("r", 3), ("k", 5))}
        m_hi = {m: sb(f"mixed_{m}_hi", [P, KC, N], F32R) for m in "rk"}
        m_lo = {m: sb(f"mixed_{m}_lo", [P, KC, N], F32R) for m in "rk"}
        gate, grec = sb("gate", [P, SUB, C]), sb("grec", [P, SUB, C])
        ka = sb("ka", [P, 2, N])
        k_hi, k_lo = sb("k_hi", [P, KC, N], F32R), sb("k_lo", [P, KC, N], F32R)
        seqs = lambda a: a.rearrange("p (b t) -> p b t", b=BT)

        bank = [ctx.enter_context(nc.psum_tensor(f"c_bank{j}", [P, N], F32)) for j in range(4)]
        acc = [ctx.enter_context(nc.psum_tensor(f"c_acc{s}", [P, C], F32)) for s in range(SUB)]

        x_in, res_in, stored = sem("x_in"), sem("res_in"), sem("stored")
        turned, r_proj, k_proj, v_done = sem("turned"), sem("r_proj"), sem("k_proj"), sem("v_done")
        xt_left = sem("xt_left")
        e_exp, ln_done, rc_done, relu_done, square_done, khi_done, klo_done = (
            sem(n) for n in ("e_exp", "ln_done", "rc_done", "relu_done", "square_done", "khi_done", "klo_done"))
        diffed = sem("diffed")
        mix_done = {m: sem("mix_done_" + m) for m in "rk"}
        mhi_done = {m: sem("mhi_done_" + m) for m in "rk"}
        mlo_done = {m: sem("mlo_done_" + m) for m in "rk"}
        capped, rd_done, newton, gated, res_done = (
            sem(n) for n in ("capped", "rd_done", "newton", "gated", "res_done"))
        st_done, mv_done, normed, veps_done, rstd_done, margin = (
            sem(n) for n in ("st_done", "mv_done", "normed", "veps_done", "rstd_done", "margin"))

        TAIL = 2
        block = ctx.enter_context(nc.Block())

        @block.sync
        def _(sp):
            sp.wait_ge(sh.x2_stored, 16 * NT)
            sp.dma_start(xres[:, :, :], tile_of(x2, 0)).then_inc(res_in, 16)
            sp.wait_ge(turned, KC)
            sp.dma_start(xin[:, :, :], tile_of(x2, 1)).then_inc(x_in, 16)

            def body(i):
                if not isinstance(i, int) or i < NT - TAIL:
                    sp.wait_ge(turned, i * KC + 2 * KC)
                    sp.dma_start(xin[:, :, :], tile_of(x2, i + 2)).then_inc(x_in, 16)
                sp.wait_ge(res_done, i * SUB + SUB)
                sp.dma_start(tile_of(x3, i), xres[:, :, :]).then_inc(stored, 16)
                sp.wait_ge(stored, i * 16 + 16)
                if not is_last(i):
                    sp.dma_start(xres[:, :, :], tile_of(x2, i + 1)).then_inc(res_in, 16)

            over_tiles(sp, body, TAIL)

        @block.tensor
        def _(pe):
            te = nc.tensor

            def cut(a, k, j):
                return a[:, k, j * P:(j + 1) * P]

            def turn(i, k):
                wait(pe, normed, i * SUB)
                wait(pe, xt_left, i * KC + k - 1)
                for s in range(SUB):
                    last = te.transpose(bank[2 + k % 2][:, s * P:(s + 1) * P], xin[:, s, k * P:(k + 1) * P],
                                        id_sb[:, :])
                last.then_inc(turned, 1)

            def receptance(i, s):
                if s == 0:
                    wait(pe, mlo_done["r"], i * KC + KC)
                if s >= 2:
                    wait(pe, capped, i * SUB + s - 1)
                else:
                    wait(pe, relu_done, (i - 1) * KC + 3 + s)
                three(te, bank[s % 2][:, :],
                      [((cut(m_hi["r"], k, s), cut(m_lo["r"], k, s)), (w_hi["r"][:, k, :], w_lo["r"][:, k, :]))
                       for k in range(KC)]).then_inc(r_proj, 1)

            def key(i, c):
                if c == 0:
                    wait(pe, mlo_done["k"], i * KC + KC)
                if c >= 2:
                    wait(pe, relu_done, i * KC + c - 1)
                else:
                    wait(pe, capped, i * SUB + 3 + c)
                three(te, bank[c % 2][:, :],
                      [((cut(w_hi["k"], k, c), cut(w_lo["k"], k, c)), (m_hi["k"][:, k, :], m_lo["k"][:, k, :]))
                       for k in range(KC)]).then_inc(k_proj, 1)

            def value(i, c):
                wait(pe, klo_done, i * KC + c + 1)
                if c == 0:
                    wait(pe, gated, i * SUB)
                for s in range(SUB):
                    for a, b in ((k_hi, w_hi["v"]), (k_hi, w_lo["v"]), (k_lo, w_hi["v"])):
                        last = te.matmul(acc[s][:, :], cut(a, c, s), b[:, c, :],
                                         start=(c == 0 and a is k_hi and b is w_hi["v"]),
                                         stop=(c == KC - 1 and a is k_lo))
                if c == KC - 1:
                    last.then_inc(v_done, 1)

            for k in range(KC):
                turn(0, k)

            def body(i):
                for s in range(SUB):
                    receptance(i, s)
                for c in range(KC):
                    key(i, c)
                    if not is_last(i):
                        turn(i + 1, c)
                for c in range(KC):
                    value(i, c)

            over_tiles(pe, body, TAIL)

        @block.scalar
        def _(act):
            sc = nc.scalar
            sc.preload_act_table_set(TABLES)

            def leave(i, k):
                wait(act, turned, i * KC + k + 1)
                for m in "rk":
                    wait(act, mix_done[m], (i - 1) * KC + k + 1)
                sc.activation(xt[:, k, :, 1:], seqs(bank[2 + k % 2][:, :]), ACT.Copy).then_inc(xt_left, 1)

            def mixed_high(m, i, k):
                wait(act, mix_done[m], i * KC + k + 1)
                if k == 0:
                    wait(act, {"r": r_proj, "k": k_proj}[m], i * KC)
                sc.activation(m_hi[m][:, k, :], mixed[m][:, k, :], ACT.Copy).then_inc(mhi_done[m], 1)

            def exp_r(i, s):
                wait(act, capped, i * SUB + s + 1)
                sc.activation(gate[:, s, :], gate[:, s, :], ACT.Exp, scale=-1.0).then_inc(e_exp, 1)

            def first_reciprocal(i, s):
                wait(act, e_exp, i * SUB + s + 1)
                wait(act, res_done, (i - 1) * SUB + s + 1)
                sc.activation(grec[:, s, :], gate[:, s, :], ACT.Ln, bias=1.0).then_inc(ln_done, 1)
                wait(act, ln_done, i * SUB + s + 1)
                sc.activation(grec[:, s, :], grec[:, s, :], ACT.Exp, scale=-1.0).then_inc(rc_done, 1)

            def relu_square(i, c):
                g = i * KC + c
                wait(act, k_proj, g + 1)
                wait(act, klo_done, g - 1)
                sc.activation(ka[:, c % 2, :], bank[c % 2][:, :], ACT.Relu).then_inc(relu_done, 1)
                wait(act, relu_done, g + 1)
                sc.activation(ka[:, c % 2, :], ka[:, c % 2, :], ACT.Square).then_inc(square_done, 1)
                wait(act, square_done, g + 1)
                if c == 0:
                    wait(act, v_done, i)
                sc.activation(k_hi[:, c, :], ka[:, c % 2, :], ACT.Copy).then_inc(khi_done, 1)

            for k in range(KC):
                leave(0, k)
            for m in "rk":
                for k in range(KC):
                    mixed_high(m, 0, k)

            def body(i):
                for s in range(SUB):
                    exp_r(i, s)
                    if s:
                        first_reciprocal(i, s - 1)
                for c in range(KC):
                    relu_square(i, c)
                    if not is_last(i):
                        leave(i + 1, c)
                    if c == 0:
                        first_reciprocal(i, SUB - 1)
                if not is_last(i):
                    for m in "rk":
                        for k in range(KC):
                            mixed_high(m, i + 1, k)

            over_tiles(act, body, TAIL)

        @block.vector
        def _(dve):
            ve = nc.vector

            def statistics(i):
                wait(dve, x_in, i * 16)
                for s in range(SUB):
                    ve.bn_stats(stats[:, s, :], xin[:, s, :]).then_inc(st_done, 1)

            def aggregate():
                for s in range(SUB):
                    ve.bn_aggr(mv[:, s, :], stats[:, s, :]).then_inc(mv_done, 1)

            def normalise(i):
                wait(dve, rstd_done, i)
                for s in range(SUB):
                    ve.tensor_scalar(xin[:, s, :], xin[:, s, :], mv[:, s, 0:1], rstd[:, s:s + 1],
                                     ALU.subtract, ALU.mult).then_inc(normed, 1)

            def mix(m, i, k):
                wait(dve, diffed, i * KC + k + 1)
                wait(dve, mhi_done[m], (i - 1) * KC + k + 1)
                wait(dve, mlo_done[m], (i - 1) * KC + k + 1)
                ve.scalar_tensor_tensor(out=seqs(mixed[m][:, k, :]), in0=seqs(diff[:, k, :]),
                                        scalar=mu_sb[:, "rk".index(m), k:k + 1], in1=xt[:, k, :, 0:T],
                                        op0=ALU.mult, op1=ALU.add).then_inc(mix_done[m], 1)

            def mixed_rest(m, i, k):
                wait(dve, mhi_done[m], i * KC + k + 1)
                ve.tensor_tensor(m_lo[m][:, k, :], mixed[m][:, k, :], m_hi[m][:, k, :].bitcast(F32),
                                 ALU.subtract).then_inc(mlo_done[m], 1)

            def cap(i, s):
                wait(dve, r_proj, i * SUB + s + 1)
                ve.tensor_scalar(gate[:, s, :], bank[s % 2][:, :], -math.log(SIG_CAP), None,
                                 ALU.max).then_inc(capped, 1)

            def k_rest(i, c):
                wait(dve, khi_done, i * KC + c + 1)
                ve.tensor_tensor(k_lo[:, c, :], ka[:, c % 2, :], k_hi[:, c, :].bitcast(F32),
                                 ALU.subtract).then_inc(klo_done, 1)

            def refine(i, s):
                wait(dve, rc_done, i * SUB + s + 1)
                ve.scalar_tensor_tensor(out=gate[:, s, :], in0=gate[:, s, :], scalar=1.0, in1=grec[:, s, :],
                                        op0=ALU.add, op1=ALU.mult).then_inc(rd_done, 1)
                wait(dve, rd_done, i * SUB + s + 1)
                ve.scalar_tensor_tensor(out=grec[:, s, :], in0=gate[:, s, :], scalar=-2.0, in1=grec[:, s, :],
                                        op0=ALU.add, op1=ALU.mult).then_inc(newton, 1)

            def residual(i):
                wait(dve, v_done, i + 1)
                wait(dve, newton, i * SUB + SUB)
                for s in range(SUB):
                    ve.scalar_tensor_tensor(out=grec[:, s, :], in0=acc[s][:, :], scalar=-1.0, in1=grec[:, s, :],
                                            op0=ALU.mult, op1=ALU.mult).then_inc(gated, 1)

            ve.memset(xt[:, :, :, 0:1], 0.0).then_inc(margin, 1)
            dve.wait_ge(margin, 1)
            for k in range(KC):
                mix("r", 0, k)
                if k:
                    mixed_rest("r", 0, k - 1)
            mixed_rest("r", 0, KC - 1)
            for k in range(KC):
                mix("k", 0, k)
            statistics(1)
            dve.wait_ge(st_done, SUB)

            def body(i):
                ahead = not is_last(i)
                for s in range(SUB):
                    cap(i, s)
                    if s == 1 and ahead:
                        aggregate()
                    if s == 2 and ahead:
                        normalise(i + 1)
                    if s >= 2:
                        refine(i, s - 2)
                for c in range(KC):
                    k_rest(i, c)
                    if ahead:
                        mix("r", i + 1, c)
                        mix("k", i + 1, c)
                    if c < 2:
                        refine(i, c + 2)
                if ahead:
                    for k in range(KC):
                        mixed_rest("r", i + 1, k)
                if not isinstance(i, int) or i < NT - TAIL:
                    statistics(i + 2)
                    dve.wait_ge(st_done, i * SUB + 2 * SUB)
                residual(i)

            over_tiles(dve, body, TAIL)

        @block.gpsimd
        def _(pool):
            gp = nc.gpsimd

            def rstd_of(i):
                wait(pool, mv_done, i * SUB)
                wait(pool, normed, (i - 1) * SUB)
                gp.tensor_tensor(rstd[:, :], mv[:, :, 1], eps[:, :], ALU.add).then_inc(veps_done, 1)
                wait(pool, veps_done, i)
                gp.tensor_tensor(rstd[:, :], rstd[:, :], half[:, :], ALU.pow).then_inc(rstd_done, 1)

            def difference(i, k):
                wait(pool, xt_left, i * KC + k + 1)
                wait(pool, mix_done["k"], (i - 1) * KC + k + 1)
                gp.tensor_tensor(seqs(diff[:, k, :]), xt[:, k, :, 1:], xt[:, k, :, 0:T],
                                 ALU.subtract).then_inc(diffed, 1)

            def mixed_rest(m, i, k):
                wait(pool, mhi_done[m], i * KC + k + 1)
                gp.tensor_tensor(m_lo[m][:, k, :], mixed[m][:, k, :], m_hi[m][:, k, :].bitcast(F32),
                                 ALU.subtract).then_inc(mlo_done[m], 1)

            def add(i):
                wait(pool, res_in, i * 16 + 16)
                for s in range(SUB):
                    wait(pool, gated, i * SUB + s + 1)
                    gp.tensor_tensor(xres[:, s, :], xres[:, s, :], grec[:, s, :], ALU.add).then_inc(res_done, 1)

            pool.wait_ge(margin, 1)
            for k in range(KC):
                difference(0, k)
            for k in range(KC):
                mixed_rest("k", 0, k)

            def body(i):
                if not is_last(i):
                    rstd_of(i + 1)
                if not is_first(i):
                    add(i - 1)
                if not is_last(i):
                    for c in range(KC):
                        difference(i + 1, c)
                    for k in range(KC):
                        mixed_rest("k", i + 1, k)

            over_tiles(pool, body, TAIL)
            add(NT - 1)


def decoder(nc, a, out):
    x1 = nc.dram_tensor("x_after_attention", (B, T, C), F32, kind="Internal").ap()
    x2 = nc.dram_tensor("x_after_cross", (B, T, C), F32, kind="Internal").ap()
    with ExitStack() as ctx:
        sh = Shared(nc, ctx)
        attention_pass(nc, sh, a["x"], {m: a["w_" + m] for m in "kvr"}, a["wo_t"], a["cols"], a["bo_b"], a["trem"],
                       a["scanmask"], a["ident"], x1,
                       dict(wq=a["xwq"], wk=a["xwk"], wv=a["xwv"], wo=a["xwo"], biases=a["xbias"], bo=a["xbo_b"]))
        cross_pass(nc, sh, x1, a["ctx"], a["ctx_t"], a["fside"], x2,
                   dict(r=a["fr"], k=a["fk"], v=a["fv"], mu=a["mu"]))
        ffn_pass(nc, sh, x2, out)


def layouts(inp):
    import numpy as np

    def chunks_of(w, n):
        a = np.asarray(w).reshape(n, P, w.shape[1] // P, P)
        return np.ascontiguousarray(a.transpose(0, 3, 2, 1)).reshape(n, P, -1)

    def rows(w):
        return np.ascontiguousarray(np.asarray(w).reshape(KC, P, C).transpose(1, 0, 2))

    def columns(names, n):
        return np.ascontiguousarray(np.stack([np.asarray(inp[m]).reshape(n, P).T for m in names], 1))

    def on_all(v):
        return np.ascontiguousarray(np.broadcast_to(np.asarray(v), (P, len(v))))

    out = {"x": np.asarray(inp["x"]), "ctx": np.asarray(inp["ctx_1024"]), "fside": np.asarray(inp["fside_BxSxS2_0"])}
    out["ctx_t"] = np.ascontiguousarray(
        out["ctx"].reshape(NT, BT, T, KC, P).transpose(0, 4, 3, 1, 2)).reshape(NT, P, KC, N)
    for m in "kvr":
        out["w_" + m] = chunks_of(inp[f"L0_attn_W{m}"], HC)
    out["wo_t"] = np.ascontiguousarray(np.asarray(inp["L0_attn_Wo"]).T).reshape(HC, P, C)
    out["cols"] = columns(["L0_attn_" + n for n in ("br", "bk", "bv", "time_decay", "U")], HC)
    out["bo_b"] = on_all(inp["L0_attn_bo"])
    for m in "qkv":
        out["xw" + m] = rows(inp[f"L0_xattn_W{m}"])
    out["xwo"] = rows(np.asarray(inp["L0_xattn_Wo"]).T)
    out["xbias"] = columns(["L0_xattn_bq", "L0_xattn_bk", "L0_xattn_bv"], KC)
    out["xbo_b"] = on_all(inp["L0_xattn_bo"])
    for m in "rkv":
        out["f" + m] = rows(np.asarray(inp[f"L0_ffn_W_{m}"]).T)
    out["mu"] = columns(["L0_ffn_mu_r", "L0_ffn_mu_k"], KC)
    out["trem"] = np.ascontiguousarray(np.broadcast_to(np.arange(T - 1, -1, -1, dtype=np.float32), (P, T)))
    mask = np.ones((P, BT, T + 1), np.float32)
    mask[:, :, 0] = 0
    out["scanmask"] = mask.reshape(P, -1)
    out["ident"] = np.eye(P, dtype=np.float32)
    return out


def kernel(**inputs):
    import concourse.bacc as bacc
    from concourse.bass_utils import run_bass_kernel_spmd

    nc = bacc.Bacc("TRN2", target_bir_lowering=False, num_devices=1)
    arrays, args = {}, {}
    for name, a in layouts(inputs).items():
        arrays[f"in_{name}"] = a
        args[name] = nc.dram_tensor(f"in_{name}", a.shape, mybir.dt.from_np(a.dtype), kind="ExternalInput").ap()
    out = nc.dram_tensor("out_x", (B, T, C), F32, kind="ExternalOutput").ap()
    decoder(nc, args, out)
    r = run_bass_kernel_spmd(nc, [arrays], core_ids=[0])
    return r.results[0]["out_x"]
```

```python
import math
from contextlib import ExitStack

import concourse.bass as bass
from concourse import mybir

F32 = mybir.dt.float32
F32R = mybir.dt.float32r
ALU = mybir.AluOpType
ACT = mybir.ActivationFunctionType
AX = mybir.AxisListType

P = 128
B, T, C = 16, 256, 512
BT = 2
NT = B // BT
N = BT * T
SUB = N // P
KC = C // P
H = 1024
HC = H // P
LN_EPS = 1e-5
EPS = math.exp(-1.0 / 12.0)
MIX = {"k": EPS + 0.3 / 11.0, "v": EPS, "r": EPS / 2.0}
CLIP_LO, CLIP_HI = math.exp(-20.0), math.exp(10.0)
SIG_CAP = 2.0 ** 60
LN_SHIFT = 21
TABLES = "natural_log_exp_and_others"
LAG = 2


def wait(eng, sem, value):
    if not isinstance(value, int) or value > 0:
        eng.wait_ge(sem, value)


def over_tiles(eng, body, tail=1):
    body(0)
    with eng.Fori(1, NT - tail) as i:
        body(i)
    for j in range(NT - tail, NT):
        body(j)


def is_first(i):
    return isinstance(i, int) and i == 0


def is_last(i):
    return isinstance(i, int) and i == NT - 1


def tile_of(dram, i):
    if isinstance(i, int):
        return dram[i * BT:(i + 1) * BT].rearrange("b (h p) c -> p (b h) c", p=P)
    return dram[bass.ds(i * BT, BT)].rearrange("b (h p) c -> p (b h) c", p=P)


def three(pe, out, pairs, before=None):
    n = len(pairs)
    for j, ((ah, al), (bh, bl)) in enumerate(pairs):
        if before:
            before(j)
        pe.matmul(out, ah, bh, start=(j == 0), stop=False)
        pe.matmul(out, ah, bl, start=False, stop=False)
        last = pe.matmul(out, al, bh, start=False, stop=(j == n - 1))
    return last


def fold(pe, sh, a, b, banks, chunks, before=None):
    for e in chunks:
        done = e + 1 if a == "wq" else KC + e + 1
        pe.wait_ge(sh.wq_rest, done)
        pe.wait_ge(sh.wk_rest, done)
        for j in (1, 0, 3, 2):
            if e == 0 and before:
                before(j)
            cols = slice(j * P, (j + 1) * P)
            high, rest = sh.fold_hi[a][:, e, cols], sh.fold_lo[a][:, e, cols]
            pe.matmul(banks[j][:, :], high, sh.fold_hi[b][:, e, :], start=(e == 0), stop=False)
            pe.matmul(banks[j][:, :], high, sh.fold_lo[b][:, e, :], start=False, stop=False)
            last = pe.matmul(banks[j][:, :], rest, sh.fold_hi[b][:, e, :], start=False, stop=(e == KC - 1))
    return last


class Shared:

    def __init__(self, nc, ctx):
        def sb(name, shape):
            return ctx.enter_context(nc.sbuf_tensor(name, shape, F32))

        self.nc, self.slot_base = nc, -(-nc.sbuf_base // 32) * 32
        sb("slots", [P, 14, KC, C])
        self.fold_raw = {m: self.slot("b_raw_" + m, F32, 2 * j) for j, m in enumerate(("wq", "wk", "wv", "wo"))}
        self.ffn_raw = {m: self.slot("c_raw_" + m, F32, 2 * j) for j, m in enumerate("rkv")}
        self.ffn_lo = {m: self.slot(f"c_w{m}_lo", F32R, 2 * j) for j, m in enumerate("rkv")}
        self.ffn_hi = {m: self.slot(f"c_w{m}_hi", F32R, j) for m, j in (("r", 6), ("k", 10), ("v", 11))}
        self.xt = nc.alloc_sbuf_tensor_at("c_xt", [P, KC, BT, T + 1], F32, offset=self.slot_base + 8 * KC * C * 4)
        self.diff = self.slot("c_diff", F32, 1)
        self.mixed = {m: self.slot("c_mixed_" + m, F32, j) for m, j in (("r", 3), ("k", 5))}
        self.mr_hi, self.mr_lo = self.slot("c_mixed_r_hi", F32R, 12), self.slot("c_mixed_r_lo", F32R, 13)
        self.ffn_turned, self.xt_left, self.diffed, self.r_mixed, self.r_high, self.r_rest, self.margin = (
            ctx.enter_context(nc.semaphore(n)) for n in ("ffn_turned", "xt_left", "diffed", "r_mixed", "r_high",
                                                         "r_rest", "margin"))
        self.r_split, self.r_proj, self.ffn_stats = (
            ctx.enter_context(nc.semaphore(n)) for n in ("r_split", "r_proj", "ffn_stats"))
        self.id_sb = sb("ident_sb", [P, P])
        self.xin, self.xres = sb("xin", [P, SUB, C]), sb("xres", [P, SUB, C])
        self.bcol = sb("bcol", [P, 3, KC])
        self.out_row = sb("out_row", [P, C])
        self.mu_sb = sb("mu_sb", [P, 2, KC])
        self.stats, self.mv = sb("stats", [P, SUB, 6]), sb("mv", [P, SUB, 2])
        self.rstd, self.half, self.eps = sb("rstd", [P, SUB]), sb("half", [P, SUB]), sb("eps", [P, SUB])
        self.x1_stored, self.x2_stored = (ctx.enter_context(nc.semaphore(n)) for n in ("x1_stored", "x2_stored"))
        self.bank = [ctx.enter_context(nc.psum_tensor(f"bank{j}", [P, N], F32)) for j in range(8)]
        self.bias_folded = ctx.enter_context(nc.semaphore("bias_folded"))
        self.fold_hi = {m: self.slot(f"b_{m}_hi", F32R, j) for m, j in (("wq", 12), ("wk", 13), ("wv", 10), ("wo", 11))}
        self.fold_lo = {m: self.slot(f"b_{m}_lo", F32R, 2 * j) for j, m in enumerate(("wq", "wk", "wv", "wo"))}
        self.fold_high, self.wq_rest, self.wk_rest, self.fold_done, self.bias_left = (
            ctx.enter_context(nc.semaphore(n)) for n in ("fold_high", "wq_rest", "wk_rest", "fold_done", "bias_left"))
        self.qb = sb("qb", [P, KC])
        self.k_or_row = sb("k_or_row", [P, BT * (T + 2)])
        self.rk_row = self.k_or_row[:, 0:C]
        self.bqk = sb("bqk", [P, 1])
        self.bwide = self.slot("bwide", F32, 8)
        self.bias_in = ctx.enter_context(nc.semaphore("bias_in"))
        self.fold_in = ctx.enter_context(nc.semaphore("fold_in"))
        self.x1_in = ctx.enter_context(nc.semaphore("x1_in"))
        self.ffn_in = ctx.enter_context(nc.semaphore("ffn_in"))
        self.x2_in = ctx.enter_context(nc.semaphore("x2_in"))

    def slot(self, name, dt, j, n=1):
        return self.nc.alloc_sbuf_tensor_at(name, [P, n * KC, C], dt,
                                             offset=self.slot_base + j * KC * C * 4)


def attention_pass(nc, sh, x, w_kvr, wo_t, cols, bo_b, trem, scanmask, ident, x1, cross):
    with ExitStack() as ctx:
        def sb(name, shape, dt=F32):
            return ctx.enter_context(nc.sbuf_tensor("a_" + name, shape, dt))

        def sem(name):
            return ctx.enter_context(nc.semaphore("a_" + name))

        WM = "kvr"
        w_hi = {m: sh.slot(f"a_w{m}_hi", F32R, 2 * j, 2) for j, m in enumerate(WM)}
        w_lo = {m: sh.slot(f"a_w{m}_lo", F32R, 6 + 2 * j, 2) for j, m in enumerate(WM)}
        wo_hi, wo_lo = sb("wo_hi", [P, HC, C], F32R), sb("wo_lo", [P, HC, C], F32R)
        xin, xres, id_sb, stats, mv, rstd, half, eps = (
            sh.xin, sh.xres, sh.id_sb, sh.stats, sh.mv, sh.rstd, sh.half, sh.eps)
        xt_hi, xt_lo = sh.slot("a_xt_hi", F32R, 12), sh.slot("a_xt_lo", F32R, 13)
        bo_sb, trem_sb, mask_sb = sb("bo", [P, C]), sb("trem", [P, T]), sb("mask", [P, BT * (T + 1)])
        col = sb("col", [P, 5, HC])
        nbr, buk, ebv, negw = (sb(n, [P, HC]) for n in ("nbr", "buk", "ebv", "negw"))
        zero = sb("zero", [P, BT, 2])
        shift = sb("shift", [P, 1])
        u = {m: sb("u" + m, [P, BT, T + 2]) for m in "vr"}
        u["k"] = sh.k_or_row[:, :].rearrange("p (b t) -> p b t", b=BT)
        kt, vv, eu, euv, rt = (sb(n, [P, BT, T]) for n in ("kt", "vv", "eu", "euv", "rt"))
        ee, ev, ss, sv = (sb(n, [P, BT * (T + 1)]) for n in ("ee", "ev", "ss", "sv"))
        dd, rc, yy = (sb(n, [P, BT, T]) for n in ("dd", "rc", "yy"))
        y_hi, y_lo = sb("y_hi", [P, 2, N], F32R), sb("y_lo", [P, 2, N], F32R)
        two = lambda a: a[:, :].rearrange("p (b t) -> p b t", b=BT)
        ee3, ev3, ss3, sv3 = two(ee), two(ev), two(ss), two(sv)
        flat = lambda a: a[:, :, :].rearrange("p b t -> p (b t)")

        ps = {m: sh.bank[j][:, :].rearrange("p (b t) -> p b t", b=BT) for j, m in enumerate(WM)}
        tps, acc = sh.bank[3], sh.bank[4:]

        def turn_bank(i, k):
            return acc[k] if is_first(i) else tps

        consts_in, x_in, res_in, stored = sem("consts_in"), sem("x_in"), sem("res_in"), sh.x1_stored
        x0_in = [sem(f"x0_in{s}") for s in range(SUB)]
        stage_in = [sem(f"stage_in{j}") for j in range(4)]
        proj = {m: sem("proj_" + m) for m in WM}
        wo_done, turned, slot_free = sem("wo_done"), sem("turned"), sem("slot_free")
        u_done = {m: sem("u_done_" + m) for m in WM}
        eu_exp, e_exp, r_exp, ln_done, rc_done, yhi_done, xhi_done, whi_done = (
            sem(n) for n in ("eu_exp", "e_exp", "r_exp", "ln_done", "rc_done", "yhi_done", "xhi_done", "whi_done"))
        k_mix, arg_done, v_mix, r_mix, eu_clip, e_clip, ev_done, s_scan, sv_scan = (
            sem(n) for n in ("k_mix", "arg_done", "v_mix", "r_mix", "eu_clip", "e_clip", "ev_done", "s_scan",
                             "sv_scan"))
        t_done, d_done, newton, y_done, ylo_done, xlo_done, st_done, mv_done, normed, res_done, setup = (
            sem(n) for n in ("t_done", "d_done", "newton", "y_done", "ylo_done", "xlo_done", "st_done", "mv_done",
                             "normed", "res_done", "setup"))
        bwide_done, dots_done = sem("bwide_done"), sem("dots_done")
        euv_done, b_done, a_done, rd_done, veps_done, rstd_done, bo_added, consts_set = (
            sem(n) for n in ("euv_done", "b_done", "a_done", "rd_done", "veps_done", "rstd_done", "bo_added",
                             "consts_set"))
        wlo_done = {m: sem("wlo_done_" + m) for m in "kvro"}

        NCONST = 5
        STAGED = 4 * HC

        def piece(n):
            c, m = divmod(n, 4)
            if m == 3:
                return wo_t[c], wo_hi[:, c, :], wo_lo[:, c, :]
            return w_kvr[WM[m]][c], w_hi[WM[m]][:, c, :], w_lo[WM[m]][:, c, :]

        block = ctx.enter_context(nc.Block())

        @block.sync
        def _(sp):
            for s in range(SUB):
                sp.dma_start(xin[:, s:s + 1, :], tile_of(x, 0)[:, s:s + 1, :]).then_inc(x0_in[s], 16)
            for dst, src in ((col[:, :, :], cols), (trem_sb[:, :], trem), (mask_sb[:, :], scanmask),
                             (id_sb[:, :], ident), (bo_sb[:, :], bo_b)):
                sp.dma_start(dst, src).then_inc(consts_in, 16)
            for n in range(STAGED):
                if n >= 4:
                    sp.wait_ge(wlo_done["kvro"[n % 4]], n // 4)
                sp.dma_start(xres[:, n % 4, :], piece(n)[0]).then_inc(stage_in[n % 4], 16)
                if n == 7:
                    sp.wait_ge(turned, KC)
                    sp.dma_start(xin[:, :, :], tile_of(x, 1)).then_inc(x_in, 16)
            for m in "kvro":
                sp.wait_ge(wlo_done[m], HC)
            sp.dma_start(xres[:, :, :], tile_of(x, 0)).then_inc(res_in, 16)

            with sp.Fori(1, NT - 1) as i:
                sp.wait_ge(turned, i * KC + KC)
                sp.dma_start(xin[:, :, :], tile_of(x, i + 1)).then_inc(x_in, 16)
                sp.wait_ge(res_done, i * SUB)
                sp.dma_start(tile_of(x1, i - 1), xres[:, :, :]).then_inc(stored, 16)
                sp.wait_ge(stored, i * 16)
                sp.dma_start(xres[:, :, :], tile_of(x, i)).then_inc(res_in, 16)
            for i in (NT - 1, NT):
                sp.wait_ge(res_done, i * SUB)
                sp.dma_start(tile_of(x1, i - 1), xres[:, :, :]).then_inc(stored, 16)
                if i < NT:
                    sp.wait_ge(stored, i * 16)
                    sp.dma_start(xres[:, :, :], tile_of(x, i)).then_inc(res_in, 16)
                    for m in WM:
                        sp.wait_ge(proj[m], i * HC + KC)
                    for m in ("wq", "wk", "wv", "wo"):
                        sp.dma_start(sh.fold_raw[m][:, :, :], cross[m]).then_inc(sh.fold_in, 16)
                    sp.wait_ge(turned, NT * KC)
                    sp.dma_start(xin[:, :, :], tile_of(x1, 0)).then_inc(sh.x1_in, 16)
                    sp.dma_start(sh.bcol[:, :, :], cross["biases"]).then_inc(sh.bias_in, 16)
                    sp.dma_start(sh.out_row[:, :], cross["bo"]).then_inc(sh.bias_in, 16)

        @block.tensor
        def _(pe):
            te = nc.tensor

            def turn(i, k):
                wait(pe, normed, i * SUB + SUB)
                if not is_first(i):
                    wait(pe, xlo_done, i * KC + k)
                for s in range(SUB):
                    last = te.transpose(turn_bank(i, k)[:, s * P:(s + 1) * P], xin[:, s, k * P:(k + 1) * P],
                                        id_sb[:, :])
                last.then_inc(turned, 1)

            def operands(m, c, k):
                w = slice(k * P, (k + 1) * P)
                return ((w_hi[m][:, c, w], w_lo[m][:, c, w]), (xt_hi[:, k, :], xt_lo[:, k, :]))

            def project(i, c):
                g = i * HC + c

                def split(k):
                    if is_first(i) or k == 0:
                        wait(pe, xlo_done, i * KC + (k + 1 if is_first(i) else KC))

                if c < HC - 1:
                    for j, m in enumerate(WM):
                        if is_first(i):
                            pe.wait_ge(wlo_done[m], c + 1)
                        wait(pe, u_done[m], g)
                        three(te, flat(ps[m]), [operands(m, c, k) for k in range(KC)],
                              split if c == 0 and j == 0 else None).then_inc(proj[m], 1)
                    return
                for k in range(KC):
                    for m in WM:
                        if k == 0:
                            if is_first(i):
                                pe.wait_ge(wlo_done[m], c + 1)
                            wait(pe, u_done[m], g)
                        (ah, al), (bh, bl) = operands(m, c, k)
                        te.matmul(flat(ps[m]), ah, bh, start=(k == 0), stop=False)
                        te.matmul(flat(ps[m]), ah, bl, start=False, stop=False)
                        last = te.matmul(flat(ps[m]), al, bh, start=False, stop=(k == KC - 1))
                        if k == KC - 1:
                            last.then_inc(proj[m], 1)
                    if not is_last(i):
                        if k < KC - 1:
                            last.then_inc(slot_free, 1)
                        turn(i + 1, k)

            def output(i, c):
                g = i * HC + c
                if is_first(i):
                    pe.wait_ge(wlo_done["o"], c + 1)
                wait(pe, ylo_done, g + 1)
                if c == 0:
                    wait(pe, res_done, i * SUB)
                    if is_first(i):
                        pe.wait_ge(xlo_done, KC)
                for s in range(SUB):
                    t = slice(s * P, (s + 1) * P)
                    for a, b in ((y_hi, wo_hi), (y_hi, wo_lo), (y_lo, wo_hi)):
                        last = te.matmul(acc[s][:, :], a[:, c % 2, t], b[:, c, :],
                                         start=(c == 0 and a is y_hi and b is wo_hi),
                                         stop=(c == HC - 1 and a is y_lo))
                last.then_inc(wo_done, 1)

            def bias_product(bank, lhs, rhs):
                for e in range(KC):
                    last = te.matmul(bank, lhs(e), rhs(e), start=(e == 0), stop=(e == KC - 1))
                return last

            def wide(j, e):
                return sh.bwide[:, j, e * P:(e + 1) * P]

            pe.wait_ge(consts_in, 16 * NCONST)
            for k in range(KC):
                turn(0, k)

            def body(i):
                for c in range(HC):
                    if is_last(i) and c == HC - 1:
                        pe.wait_ge(sh.fold_in, 16 * 4)
                        pe.wait_ge(bwide_done, 4)
                        pe.wait_ge(xlo_done, NT * KC)
                        bias_product(tps[:, :], lambda e: wide(2, e),
                                     lambda e: sh.fold_raw["wk"][:, e, :]).then_inc(sh.bias_folded, 1)
                    project(i, c)
                    if c >= LAG:
                        output(i, c - LAG)
                    elif not is_first(i):
                        output(i - 1, HC + c - LAG)

            over_tiles(pe, body)
            raw = sh.fold_raw
            pe.wait_ge(u_done["k"], NT * HC)
            bias_product(sh.bank[0][:, :], lambda e: wide(0, e), lambda e: raw["wq"][:, e, :])
            pe.wait_ge(u_done["v"], NT * HC)
            one = mask_sb[:, 1:2]
            te.matmul(sh.bank[1][:, 0:1], wide(3, 0), one, start=True, stop=True).then_inc(sh.bias_folded, 1)
            output(NT - 1, HC - 2)
            pe.wait_ge(u_done["r"], NT * HC)
            bias_product(sh.bank[2][:, :], lambda e: wide(1, e),
                         lambda e: raw["wo"][:, e, :]).then_inc(sh.bias_folded, 1)

            def bank_left(j):
                pe.wait_ge(sh.bias_left, 3 if j == 2 else 2)

            fold(te, sh, "wq", "wk", sh.bank, (0,), bank_left)
            output(NT - 1, HC - 1)
            fold(te, sh, "wq", "wk", sh.bank, range(1, KC)).then_inc(sh.fold_done, 1)

        @block.scalar
        def _(act):
            sc = nc.scalar
            sc.preload_act_table_set(TABLES)

            def split_high(n):
                act.wait_ge(stage_in[n % 4], 16 * (n // 4 + 1))
                sc.activation(piece(n)[1], xres[:, n % 4, :], ACT.Copy).then_inc(whi_done, 1)

            def xt_high(i, k):
                wait(act, turned, i * KC + k + 1)
                if not is_first(i):
                    if k < KC - 1:
                        act.wait_ge(slot_free, (i - 1) * (KC - 1) + k + 1)
                    else:
                        act.wait_ge(proj["r"], i * HC)
                sc.activation(xt_hi[:, k, :], turn_bank(i, k)[:, :], ACT.Copy).then_inc(xhi_done, 1)

            def leave(m, i, c):
                g = i * HC + c
                wait(act, {"k": k_mix, "v": v_mix, "r": r_mix}[m], g)
                if m == "v":
                    sc.activation(u["v"][:, :, 0:T + 2:T + 1], zero[:, :, :], ACT.Identity, bias=ebv[:, c:c + 1])
                act.wait_ge(proj[m], g + 1)
                if m == "v":
                    sc.activation(u[m][:, :, 1:T + 1], ps[m][:, :, :], ACT.Identity, bias=ebv[:, c:c + 1],
                                  scale=MIX[m]).then_inc(u_done[m], 1)
                else:
                    sc.activation(u[m][:, :, 1:T + 1], ps[m][:, :, :], ACT.Copy,
                                  scale=MIX[m]).then_inc(u_done[m], 1)

            def exp_k(i, c):
                g = i * HC + c
                act.wait_ge(k_mix, g + 1)
                wait(act, b_done, g)
                sc.activation(eu[:, :, :], kt[:, :, :], ACT.Exp, bias=buk[:, c:c + 1]).then_inc(eu_exp, 1)
                act.wait_ge(arg_done, g + 1)
                sc.activation(ee3[:, :, 1:], ee3[:, :, 1:], ACT.Exp, bias=col[:, 1, c:c + 1]).then_inc(e_exp, 1)

            def exp_r(i, c):
                g = i * HC + c
                act.wait_ge(r_mix, g + 1)
                sc.activation(rt[:, :, :], rt[:, :, :], ACT.Exp, bias=nbr[:, c:c + 1],
                              scale=-1.0).then_inc(r_exp, 1)

            def first_reciprocal(g):
                act.wait_ge(d_done, g + 1)
                wait(act, newton, g)
                sc.activation(rc[:, :, :], dd[:, :, :], ACT.Ln, scale=2.0 ** -LN_SHIFT).then_inc(ln_done, 1)
                act.wait_ge(ln_done, g + 1)
                sc.activation(rc[:, :, :], rc[:, :, :], ACT.Exp, scale=-1.0, bias=shift[:, 0:1]).then_inc(rc_done, 1)

            def y_high(g, c):
                act.wait_ge(y_done, g + 1)
                wait(act, wo_done, g - 1)
                sc.activation(y_hi[:, c % 2, :], flat(yy), ACT.Copy).then_inc(yhi_done, 1)

            for n in range(4):
                split_high(n)
            for k in range(KC):
                xt_high(0, k)
            act.wait_ge(setup, 5)
            act.wait_ge(consts_set, 3)

            def body(i):
                for c in range(HC):
                    g = i * HC + c
                    back = c > 0 or not is_first(i)
                    if is_first(i) and c < HC - 1:
                        for m in range(4):
                            split_high(4 * (c + 1) + m)
                    if c == HC - 1 and not is_last(i):
                        xt_high(i + 1, 0)
                        xt_high(i + 1, 1)
                        first_reciprocal(g - 1)
                        xt_high(i + 1, 2)
                        xt_high(i + 1, 3)
                        y_high(g - 1, c - 1)
                        for m in WM:
                            leave(m, i, c)
                        exp_k(i, c)
                        exp_r(i, c)
                        continue
                    leave("k", i, c)
                    if back:
                        first_reciprocal(g - 1)
                    leave("v", i, c)
                    exp_k(i, c)
                    leave("r", i, c)
                    if back:
                        y_high(g - 1, (c - 1) % HC)
                    exp_r(i, c)

            def fold_split_high(e, a, b):
                for m in (a, b):
                    sc.activation(sh.fold_hi[m][:, e, :], sh.fold_raw[m][:, e, :], ACT.Copy).then_inc(sh.fold_high, 1)

            over_tiles(act, body)
            act.wait_ge(sh.fold_in, 16 * 4)
            for e in range(KC):
                fold_split_high(e, "wq", "wk")
            first_reciprocal(NT * HC - 1)
            y_high(NT * HC - 1, HC - 1)
            for e in range(KC):
                fold_split_high(e, "wv", "wo")

        @block.vector
        def _(dve):
            ve = nc.vector

            def split_rest(n):
                dve.wait_ge(whi_done, n + 1)
                ve.tensor_tensor(piece(n)[2], xres[:, n % 4, :], piece(n)[1].bitcast(F32),
                                 ALU.subtract).then_inc(wlo_done["kvro"[n % 4]], 1)

            def xt_rest(i, k):
                wait(dve, xhi_done, i * KC + k + 1)
                ve.tensor_tensor(xt_lo[:, k, :], turn_bank(i, k)[:, :], xt_hi[:, k, :].bitcast(F32),
                                 ALU.subtract).then_inc(xlo_done, 1)

            def mix(m, i, c, out, done):
                g = i * HC + c
                dve.wait_ge(u_done[m], g + 1)
                if m == "k":
                    wait(dve, eu_exp, g)
                    wait(dve, arg_done, g)
                if m == "v":
                    wait(dve, euv_done, g)
                    wait(dve, ev_done, g)
                if m == "r":
                    wait(dve, d_done, g)
                ve.scalar_tensor_tensor(out=out[:, :, :], in0=u[m][:, :, 2:], scalar=(1.0 - MIX[m]) / MIX[m],
                                        in1=u[m][:, :, 0:T], op0=ALU.mult, op1=ALU.add).then_inc(done, 1)

            def decayed(i, c):
                g = i * HC + c
                dve.wait_ge(k_mix, g + 1)
                wait(dve, s_scan, g)
                ve.scalar_tensor_tensor(out=ee3[:, :, 1:],
                                        in0=trem_sb[:, :].unsqueeze(1).to_broadcast([P, BT, T]),
                                        scalar=negw[:, c:c + 1], in1=kt[:, :, :],
                                        op0=ALU.mult, op1=ALU.add).then_inc(arg_done, 1)

            def clip_and_scan(g, before_product=None, before_scans=None):
                dve.wait_ge(eu_exp, g + 1)
                ve.tensor_scalar(eu[:, :, :], eu[:, :, :], CLIP_LO, CLIP_HI, ALU.max, ALU.min).then_inc(eu_clip, 1)
                dve.wait_ge(e_exp, g + 1)
                ve.tensor_scalar(ee3[:, :, 1:], ee3[:, :, 1:], CLIP_LO, CLIP_HI, ALU.max, ALU.min).then_inc(e_clip, 1)
                if before_product:
                    before_product()
                dve.wait_ge(e_clip, g + 1)
                wait(dve, sv_scan, g)
                ve.tensor_tensor(ev3[:, :, 1:], ee3[:, :, 1:], vv[:, :, :], ALU.mult).then_inc(ev_done, 1)
                if before_scans:
                    before_scans()
                wait(dve, d_done, g)
                ve.tensor_tensor_scan(ss[:, :], mask_sb[:, :], ee[:, :], 0.0, ALU.mult, ALU.add).then_inc(s_scan, 1)
                dve.wait_ge(ev_done, g + 1)
                wait(dve, y_done, g)
                ve.tensor_tensor_scan(sv[:, :], mask_sb[:, :], ev[:, :], 0.0, ALU.mult, ALU.add).then_inc(sv_scan, 1)

            def one_plus(g):
                dve.wait_ge(r_exp, g + 1)
                ve.tensor_scalar(rt[:, :, :], rt[:, :, :], SIG_CAP, 1.0, ALU.min, ALU.add).then_inc(t_done, 1)

            def denominator(g):
                dve.wait_ge(t_done, g + 1)
                dve.wait_ge(b_done, g + 1)
                wait(dve, rd_done, g)
                ve.tensor_tensor(dd[:, :, :], rt[:, :, :], ss3[:, :, 0:T], ALU.mult).then_inc(d_done, 1)

            def divide(g):
                dve.wait_ge(rd_done, g + 1)
                ve.scalar_tensor_tensor(out=rc[:, :, :], in0=dd[:, :, :], scalar=-2.0, in1=rc[:, :, :],
                                        op0=ALU.add, op1=ALU.mult).then_inc(newton, 1)
                dve.wait_ge(newton, g + 1)
                dve.wait_ge(a_done, g + 1)
                wait(dve, ylo_done, g)
                ve.scalar_tensor_tensor(out=yy[:, :, :], in0=rc[:, :, :], scalar=-1.0, in1=sv3[:, :, 0:T],
                                        op0=ALU.mult, op1=ALU.mult).then_inc(y_done, 1)

            def y_rest(g, c):
                dve.wait_ge(yhi_done, g + 1)
                ve.tensor_tensor(y_lo[:, c % 2, :], flat(yy), y_hi[:, c % 2, :].bitcast(F32),
                                 ALU.subtract).then_inc(ylo_done, 1)

            def statistics(i, s):
                if is_first(i):
                    dve.wait_ge(x0_in[s], 16)
                elif s == 0:
                    dve.wait_ge(x_in, i * 16)
                    dve.wait_ge(normed, i * SUB)
                ve.bn_stats(stats[:, s, :], xin[:, s, :]).then_inc(st_done, 1)

            def aggregate(s):
                ve.bn_aggr(mv[:, s, :], stats[:, s, :]).then_inc(mv_done, 1)

            def normalise(i, s):
                if s == 0:
                    dve.wait_ge(rstd_done, i + 1)
                ve.tensor_scalar(xin[:, s, :], xin[:, s, :], mv[:, s, 0:1], rstd[:, s:s + 1],
                                 ALU.subtract, ALU.mult).then_inc(normed, 1)

            def residual(i):
                wait(dve, wo_done, i * HC + HC)
                wait(dve, bo_added, i + 1)
                for s in range(SUB):
                    ve.tensor_tensor(xres[:, s, :], xres[:, s, :], acc[s][:, :], ALU.add).then_inc(res_done, 1)

            for a in (u["k"], u["r"]):
                ve.memset(a[:, :, 0:T + 2:T + 1], 0.0)
            for a in (ee3, ev3):
                ve.memset(a[:, :, 0:1], 0.0)
            for s in range(SUB):
                statistics(0, s)
            dve.wait_ge(st_done, SUB)
            for s in range(SUB):
                aggregate(s)
            for s in range(SUB):
                normalise(0, s)
            dve.wait_ge(consts_in, 16 * NCONST)
            ve.tensor_scalar(nbr[:, :], col[:, 0, :], -1.0, None, ALU.mult).then_inc(setup, 1)
            ve.tensor_tensor(buk[:, :], col[:, 1, :], col[:, 4, :], ALU.add).then_inc(setup, 1)
            ve.tensor_scalar(ebv[:, :], col[:, 2, :], MIX["v"], None, ALU.mult).then_inc(setup, 1)
            ve.tensor_scalar(negw[:, :], col[:, 3, :], 0.0, -1.0, ALU.max, ALU.mult).then_inc(setup, 1)
            ve.memset(zero[:, :, :], 0.0).then_inc(setup, 1)
            for k in range(KC):
                xt_rest(0, k)
            dve.wait_ge(setup, 5)

            def body(i):
                for c in range(HC):
                    g = i * HC + c
                    back = c > 0 or not is_first(i)
                    ahead = not is_last(i)
                    if back:
                        one_plus(g - 1)
                    if c == HC - 1 and ahead:
                        xt_rest(i + 1, 1)
                        denominator(g - 1)
                        xt_rest(i + 1, 2)
                        divide(g - 1)
                        xt_rest(i + 1, 3)
                        y_rest(g - 1, c - 1)
                        mix("k", i, c, kt, k_mix)
                        decayed(i, c)
                        mix("v", i, c, vv, v_mix)
                        mix("r", i, c, rt, r_mix)
                        clip_and_scan(g)
                        continue
                    if is_first(i):
                        split_rest(4 * (c + 1))
                    if back:
                        denominator(g - 1)
                    if is_last(i) and c == HC - 2:
                        dve.wait_ge(sh.bias_in, 32)
                        dve.wait_ge(proj["v"], i * HC + KC)
                        for j, b in enumerate((1, 2, 0)):
                            ve.tensor_copy(sh.bwide[:, j, :].rearrange("p (k r) -> p k r", k=KC),
                                           sh.bcol[:, b, :].unsqueeze(2).to_broadcast([P, KC, P])
                                           ).then_inc(bwide_done, 1)
                        ve.tensor_tensor_reduce(out=sh.bwide[:, 3, C - KC:], in0=sh.bcol[:, 0, :],
                                                in1=sh.bcol[:, 1, :], scale=1.0, scalar=0.0, op0=ALU.mult,
                                                op1=ALU.add, accum_out=sh.bqk[:, 0:1]).then_inc(dots_done, 1)
                        dve.wait_ge(dots_done, 1)
                        ve.tensor_copy(sh.bwide[:, 3, 0:P], sh.bqk[:, 0:1].to_broadcast([P, P])
                                       ).then_inc(bwide_done, 1)
                    mix("k", i, c, kt, k_mix)
                    decayed(i, c)
                    if is_first(i):
                        split_rest(4 * (c + 1) + 3)
                    if ahead and c in (2, 3):
                        statistics(i + 1, 2 * c - 4)
                        statistics(i + 1, 2 * c - 3)
                        dve.wait_ge(st_done, (i + 1) * SUB + 2 * c - 2)
                    mix("v", i, c, vv, v_mix)
                    if ahead and c in (2, 3):
                        aggregate(2 * c - 4)
                        aggregate(2 * c - 3)
                    if back:
                        divide(g - 1)
                    if ahead and c in (5, 6):
                        normalise(i + 1, 2 * c - 10)
                        normalise(i + 1, 2 * c - 9)
                    mix("r", i, c, rt, r_mix)
                    clip_and_scan(g, (lambda: y_rest(g - 1, (c - 1) % HC)) if back else None,
                                  (lambda: xt_rest(i + 1, 0)) if ahead and c == HC - 2 else None)
                    if c == LAG - 1 and not is_first(i):
                        residual(i - 1)

            def fold_split_rest(m, e):
                dve.wait_ge(sh.fold_high, 2 * KC * (m == "wv") + 2 * e + 1)
                ve.tensor_tensor(sh.fold_lo[m][:, e, :], sh.fold_raw[m][:, e, :], sh.fold_hi[m][:, e, :].bitcast(F32),
                                 ALU.subtract).then_inc(sh.wq_rest, 1)

            over_tiles(dve, body)
            g = NT * HC - 1
            one_plus(g)
            denominator(g)
            dve.wait_ge(k_mix, NT * HC)
            dve.wait_ge(sh.bias_folded, 2)
            for c in range(KC):
                dve.wait_ge(dots_done, c + 1)
                ve.tensor_tensor_reduce(out=sh.bwide[:, 3, P:2 * P], in0=tps[:, c * P:(c + 1) * P], in1=id_sb[:, :],
                                        scale=1.0, scalar=0.0, op0=ALU.mult, op1=ALU.add,
                                        accum_out=sh.qb[:, c:c + 1]).then_inc(dots_done, 1)
            dve.wait_ge(dots_done, 1 + KC)
            ve.tensor_copy(sh.bqk[:, :], sh.bank[1][:, 0:1]).then_inc(sh.bias_left, 1)
            ve.tensor_copy(sh.rk_row[:, :], sh.bank[0][:, :]).then_inc(sh.bias_left, 1)
            fold_split_rest("wq", 0)
            fold_split_rest("wq", 1)
            fold_split_rest("wq", 2)
            divide(g)
            dve.wait_ge(sh.bias_folded, 3)
            ve.tensor_tensor(sh.out_row[:, :], sh.out_row[:, :], sh.bank[2][:, :], ALU.add).then_inc(sh.bias_left, 1)
            y_rest(g, HC - 1)
            fold_split_rest("wq", 3)
            for e in range(2):
                fold_split_rest("wv", e)
            residual(NT - 1)
            for e in range(2, KC):
                fold_split_rest("wv", e)

        @block.gpsimd
        def _(pool):
            gp = nc.gpsimd

            def rstd_of(i):
                wait(pool, mv_done, i * SUB + SUB)
                wait(pool, normed, i * SUB)
                gp.tensor_tensor(rstd[:, :], mv[:, :, 1], eps[:, :], ALU.add).then_inc(veps_done, 1)
                pool.wait_ge(veps_done, i + 1)
                gp.tensor_tensor(rstd[:, :], rstd[:, :], half[:, :], ALU.pow).then_inc(rstd_done, 1)

            def split_rest(n):
                pool.wait_ge(whi_done, n + 1)
                gp.tensor_tensor(piece(n)[2], xres[:, n % 4, :], piece(n)[1].bitcast(F32),
                                 ALU.subtract).then_inc(wlo_done["kvro"[n % 4]], 1)

            def front(g):
                pool.wait_ge(v_mix, g + 1)
                pool.wait_ge(eu_clip, g + 1)
                wait(pool, a_done, g)
                gp.tensor_tensor(euv[:, :, :], eu[:, :, :], vv[:, :, :], ALU.mult).then_inc(euv_done, 1)
                pool.wait_ge(s_scan, g + 1)
                gp.tensor_tensor(ss3[:, :, 0:T], ss3[:, :, 0:T], eu[:, :, :], ALU.add).then_inc(b_done, 1)
                pool.wait_ge(sv_scan, g + 1)
                pool.wait_ge(euv_done, g + 1)
                gp.tensor_tensor(sv3[:, :, 0:T], sv3[:, :, 0:T], euv[:, :, :], ALU.add).then_inc(a_done, 1)

            def back_of(g):
                pool.wait_ge(rc_done, g + 1)
                gp.tensor_tensor(dd[:, :, :], dd[:, :, :], rc[:, :, :], ALU.mult).then_inc(rd_done, 1)

            gp.memset(half[:, :], -0.5).then_inc(consts_set, 1)
            gp.memset(shift[:, :], -LN_SHIFT * math.log(2.0)).then_inc(consts_set, 1)
            gp.memset(eps[:, :], LN_EPS).then_inc(consts_set, 1)
            pool.wait_ge(consts_set, 3)
            rstd_of(0)
            for n in range(4):
                split_rest(n)
            pool.wait_ge(consts_in, 16 * NCONST)

            def body(i):
                for c in range(HC):
                    g = i * HC + c
                    split = is_first(i) and c < HC - 1
                    if split:
                        split_rest(4 * (c + 1) + 1)
                    if c > 0 or not is_first(i):
                        back_of(g - 1)
                    if split:
                        split_rest(4 * (c + 1) + 2)
                    if c == 0 and not is_first(i):
                        pool.wait_ge(res_in, i * 16)
                        for s in range(SUB):
                            last = gp.tensor_tensor(xres[:, s, :], xres[:, s, :], bo_sb[:, :], ALU.add)
                        last.then_inc(bo_added, 1)
                    front(g)
                    if c == 3 and not is_last(i):
                        rstd_of(i + 1)

            def fold_split_rest(m, e):
                pool.wait_ge(sh.fold_high, 2 * KC * (m == "wo") + 2 * e + 2)
                gp.tensor_tensor(sh.fold_lo[m][:, e, :], sh.fold_raw[m][:, e, :], sh.fold_hi[m][:, e, :].bitcast(F32),
                                 ALU.subtract).then_inc(sh.wk_rest, 1)

            over_tiles(pool, body)
            pool.wait_ge(sh.bias_folded, 1)
            fold_split_rest("wk", 0)
            back_of(NT * HC - 1)
            pool.wait_ge(res_in, NT * 16)
            for s in range(SUB):
                last = gp.tensor_tensor(xres[:, s, :], xres[:, s, :], bo_sb[:, :], ALU.add)
            last.then_inc(bo_added, 1)
            for e in range(1, KC):
                fold_split_rest("wk", e)
            pool.wait_ge(sh.bias_folded, 3)
            for e in range(KC):
                fold_split_rest("wo", e)


def cross_pass(nc, sh, x1, ctx_in, ctx_t, fside, x2, ffn):
    with ExitStack() as ctx:
        def sb(name, shape, dt=F32):
            return ctx.enter_context(nc.sbuf_tensor("b_" + name, shape, dt))

        def sem(name):
            return ctx.enter_context(nc.semaphore("b_" + name))

        SCALE = 1.0 / math.sqrt(32.0)
        m_hi, m_lo, l_hi, l_lo, xt_hi, xt_lo = (
            sh.slot("b_" + n, F32R, j) for n, j in (("m_hi", 1), ("m_lo", 3), ("l_hi", 5), ("l_lo", 7),
                                                    ("xt_hi", 10), ("xt_lo", 11)))
        ct, cx = sh.slot("b_ct", F32, 8), sh.slot("b_cx", F32, 9)
        out_row, id_sb, xin, xres, stats, mv, rstd, half, eps = (
            sh.out_row, sh.id_sb, sh.xin, sh.xres, sh.stats, sh.mv, sh.rstd, sh.half, sh.eps)
        qb, rk_row, bqk = sh.qb, sh.rk_row, sh.bqk
        row_product = sb("row_product", [P, C])
        q_hi, q_lo = sh.slot("b_q_hi", F32R, 12), sh.slot("b_q_lo", F32R, 13)
        ct_hi, ct_lo = sb("ct_hi", [P, KC, N], F32R), sb("ct_lo", [P, KC, N], F32R)
        cx_hi, cx_lo = sb("cx_hi", [P, SUB, C], F32R), sb("cx_lo", [P, SUB, C], F32R)
        fs, pr = sb("fs", [P, SUB, T]), sb("pr", [P, SUB, T])
        pt_hi, pt_lo = sb("pt_hi", [P, BT, 2 * T], F32R), sb("pt_lo", [P, BT, 2 * T], F32R)
        pc_hi, pc_lo = sb("pc_hi", [P, KC, N], F32R), sb("pc_lo", [P, KC, N], F32R)
        rq_next, rq, mx, nb, rowsum, rinv = (sb(n, [P, SUB]) for n in ("rq_next", "rq", "mx", "nb", "rowsum",
                                                                      "rinv"))
        bank, acc = sh.bank[:4], sh.bank[4:]

        x_in, res_in, cx_in, ct_in, fs_in = (sem(n) for n in ("x_in", "res_in", "cx_in", "ct_in", "fs_in"))
        stored = sh.x2_stored
        fold_done, fold_left = sh.fold_done, sem("fold_left")
        turned, q_proj, sc_done, pt_done, pc_done, out_done = (
            sem(n) for n in ("turned", "q_proj", "sc_done", "pt_done", "pc_done", "out_done"))
        xhi_done, qhi_done, exp_done, pthi_done, pchi_done, cxhi_done, cthi_done, mlhi_done = (
            sem(n) for n in ("xhi_done", "qhi_done", "exp_done", "pthi_done", "pchi_done", "cxhi_done", "cthi_done",
                             "mlhi_done"))
        xlo_done, qlo_done, sc_left, mx_done, nb_done, rinv_done, ptlo_done, pclo_done, res_done = (
            sem(n) for n in ("xlo_done", "qlo_done", "sc_left", "mx_done", "nb_done", "rinv_done", "ptlo_done",
                             "pclo_done", "res_done"))
        st_done, mv_done, normed, rq_made, rq_moved = (
            sem(n) for n in ("st_done", "mv_done", "normed", "rq_made", "rq_moved"))
        veps_done, rstd_done, bo_added, cxlo_done, ctlo_done = (
            sem(n) for n in ("veps_done", "rstd_done", "bo_added", "cxlo_done", "ctlo_done"))
        fwhi_done = sem("fwhi_done")

        def is_second(i):
            return isinstance(i, int) and i == 1

        def turn_bank(i, k):
            return acc[k] if is_second(i) else bank[2 + k % 2]

        def ct_view(i):
            sel = ctx_t[i:i + 1] if isinstance(i, int) else ctx_t[bass.ds(i, 1)]
            return sel.rearrange("o p k n -> p (o k) n")

        def fs_view(i):
            return tile_of(fside, i)

        def ffn_slots(m):
            return sh.ffn_hi[m], sh.ffn_raw[m], sh.ffn_lo[m]

        NFOLD = 2 * KC
        TAIL = 2
        block = ctx.enter_context(nc.Block())

        @block.sync
        def _(sp):
            sp.dma_start(ct[:, :, :], ct_view(0)).then_inc(ct_in, 16)
            sp.dma_start(fs[:, :, :], fs_view(0)).then_inc(fs_in, 16)
            sp.dma_start(cx[:, :, :], tile_of(ctx_in, 0)).then_inc(cx_in, 16)
            sp.wait_ge(sh.x1_stored, 16 * NT)
            sp.dma_start(xres[:, :, :], tile_of(x1, 0)).then_inc(res_in, 16)
            sp.wait_ge(turned, KC)
            sp.wait_ge(rq_made, SUB)
            sp.dma_start(xin[:, :, :], tile_of(x1, 1)).then_inc(x_in, 16)
            sp.wait_ge(turned, 2 * KC)
            sp.wait_ge(rq_made, 2 * SUB)
            sp.dma_start(xin[:, :, :], tile_of(x1, 2)).then_inc(x_in, 16)
            sp.wait_ge(ctlo_done, KC)
            sp.dma_start(ct[:, :, :], ct_view(1)).then_inc(ct_in, 16)
            sp.wait_ge(fold_left, NFOLD)
            for m in "rkv":
                sp.dma_start(sh.ffn_raw[m][:, :, :], ffn[m]).then_inc(sh.ffn_in, 16)
            sp.dma_start(sh.mu_sb[:, :, :], ffn["mu"]).then_inc(sh.ffn_in, 16)

            def body(i):
                more = not is_last(i)
                if more:
                    sp.wait_ge(cxlo_done, (i + 1) * SUB)
                    sp.dma_start(cx[:, :, :], tile_of(ctx_in, i + 1)).then_inc(cx_in, 16)
                    sp.wait_ge(sc_left, i * SUB + SUB)
                    sp.dma_start(fs[:, :, :], fs_view(i + 1)).then_inc(fs_in, 16)
                if not isinstance(i, int) or i <= NT - 3:
                    sp.wait_ge(ctlo_done, (i + 2) * KC)
                    sp.dma_start(ct[:, :, :], ct_view(i + 2)).then_inc(ct_in, 16)
                    sp.wait_ge(rq_made, i * SUB + 3 * SUB)
                    sp.wait_ge(turned, i * KC + 3 * KC)
                    if isinstance(i, int) and i == NT - 3:
                        sp.dma_start(xin[:, :, :], tile_of(x2, 0)).then_inc(sh.x2_in, 16)
                    else:
                        sp.dma_start(xin[:, :, :], tile_of(x1, i + 3)).then_inc(x_in, 16)
                if is_last(i):
                    sp.wait_ge(sh.ffn_turned, KC)
                    sp.dma_start(xin[:, :, :], tile_of(x2, 1)).then_inc(sh.x2_in, 16)
                sp.wait_ge(res_done, i * SUB + SUB)
                sp.dma_start(tile_of(x2, i), xres[:, :, :]).then_inc(stored, 16)
                if more:
                    sp.wait_ge(stored, i * 16 + 16)
                    sp.dma_start(xres[:, :, :], tile_of(x1, i + 1)).then_inc(res_in, 16)

            over_tiles(sp, body, 3)

        @block.tensor
        def _(pe):
            te = nc.tensor

            def cut(a, k, j):
                return a[:, k, j * P:(j + 1) * P]

            def turn(i, k):
                wait(pe, normed, i * SUB + SUB)
                if is_second(i):
                    pe.wait_ge(fold_left, KC + k + 1)
                elif k >= 2:
                    wait(pe, xlo_done, i * KC + k - 1)
                elif not is_first(i):
                    wait(pe, ptlo_done, (i - 2) * BT + k + 1)
                    wait(pe, xlo_done, (i - 1) * KC + k + 3)
                for s in range(SUB):
                    last = te.transpose(turn_bank(i, k)[:, s * P:(s + 1) * P], xin[:, s, k * P:(k + 1) * P],
                                        id_sb[:, :])
                last.then_inc(turned, 1)

            def receptance_ffn(s):
                pe.wait_ge(sh.r_rest, KC)
                pe.wait_ge(sh.r_split, KC)
                three(te, bank[s][:, :],
                      [((cut(sh.mr_hi, k, s), cut(sh.mr_lo, k, s)), (sh.ffn_hi["r"][:, k, :], sh.ffn_lo["r"][:, k, :]))
                       for k in range(KC)]).then_inc(sh.r_proj, 1)

            def turn_ffn(k):
                pe.wait_ge(normed, NT * SUB + SUB)
                if k < 2:
                    pe.wait_ge(ptlo_done, NT * BT - 1 + k)
                else:
                    pe.wait_ge(sh.xt_left, k - 1)
                for s in range(SUB):
                    last = te.transpose(bank[2 + k % 2][:, s * P:(s + 1) * P], xin[:, s, k * P:(k + 1) * P],
                                        id_sb[:, :])
                last.then_inc(sh.ffn_turned, 1)

            def query(i, c):
                early = isinstance(i, int) and i < 2

                def split(k):
                    pe.wait_ge(xlo_done, i * KC + k + 1)

                if c == 0 and not early:
                    wait(pe, xlo_done, i * KC + KC)
                if c >= 2:
                    wait(pe, qlo_done, i * KC + c - 1)
                elif not is_first(i):
                    wait(pe, sc_left, (i - 1) * SUB + c + 1)
                else:
                    wait(pe, fold_left, KC)
                three(te, bank[c % 2][:, :],
                      [((cut(m_hi, k, c), cut(m_lo, k, c)), (xt_hi[:, k, :], xt_lo[:, k, :]))
                       for k in range(KC)], split if c == 0 and early else None).then_inc(q_proj, 1)

            def scores(i, s):
                def split(k):
                    if k in (0, KC - 1):
                        pe.wait_ge(qlo_done, KC if k else KC - 1)

                b = s // 2
                if s == 0:
                    if not is_first(i):
                        wait(pe, qlo_done, i * KC + KC)
                    wait(pe, ctlo_done, i * KC + KC)
                if s < 2:
                    wait(pe, pclo_done, (i - 1) * KC + 3 + s)
                elif not is_first(i) and not is_last(i):
                    wait(pe, xlo_done, (i + 1) * KC + s + 1)
                keys = slice(b * T, (b + 1) * T)
                three(te, bank[s][:, 0:T],
                      [((cut(q_hi, k, s), cut(q_lo, k, s)), (ct_hi[:, k, keys], ct_lo[:, k, keys]))
                       for k in range(KC)], split if s == 0 and is_first(i) else None).then_inc(sc_done, 1)

            def turn_probs(i, b):
                wait(pe, exp_done, i * SUB + 2 * b + 2)
                wait(pe, sc_left, i * SUB + 3 + b)
                if not is_last(i):
                    wait(pe, xlo_done, (i + 1) * KC + 3 + b)
                for kk in range(2):
                    for h in range(2):
                        last = te.transpose(bank[2 + b][:, kk * T + h * P:kk * T + (h + 1) * P],
                                            pr[:, 2 * b + h, kk * P:(kk + 1) * P], id_sb[:, :])
                last.then_inc(pt_done, 1)

            def context(i, c):
                if c == 0:
                    wait(pe, ptlo_done, i * BT + BT)
                    wait(pe, cxlo_done, i * SUB + SUB)
                if c >= 2:
                    wait(pe, pclo_done, i * KC + c - 1)
                elif is_last(i):
                    wait(pe, sc_left, i * SUB + c + 1)
                else:
                    wait(pe, qlo_done, (i + 1) * KC + 3 + c)
                for b in range(BT):
                    last = three(te, bank[c % 2][:, b * T:(b + 1) * T],
                                 [((cut(cx_hi, 2 * b + kk, c), cut(cx_lo, 2 * b + kk, c)),
                                   (pt_hi[:, b, kk * T:(kk + 1) * T], pt_lo[:, b, kk * T:(kk + 1) * T]))
                                  for kk in range(2)])
                last.then_inc(pc_done, 1)

            def output(i, c):
                wait(pe, pclo_done, i * KC + c + 1)
                if c == 0:
                    wait(pe, res_done, i * SUB)
                    if is_first(i):
                        pe.wait_ge(fold_left, NFOLD)
                for s in range(SUB):
                    for a, b in ((pc_hi, l_hi), (pc_hi, l_lo), (pc_lo, l_hi)):
                        last = te.matmul(acc[s][:, :], cut(a, c, s), b[:, c, :],
                                         start=(c == 0 and a is pc_hi and b is l_hi),
                                         stop=(c == KC - 1 and a is pc_lo))
                if c == KC - 1:
                    last.then_inc(out_done, 1)

            fold(te, sh, "wv", "wo", acc, range(KC - 1))
            pe.wait_ge(fold_left, KC)
            turn(0, 0)
            turn(0, 1)
            fold(te, sh, "wv", "wo", acc, (KC - 1,)).then_inc(fold_done, 1)
            turn(0, 2)
            turn(0, 3)
            for c in range(KC):
                query(0, c)

            def body(i):
                two_ahead = not isinstance(i, int) or i < NT - TAIL
                for s in range(SUB):
                    if is_first(i) and s == 2:
                        for k in range(KC):
                            turn(1, k)
                    scores(i, s)
                if not is_last(i):
                    query(i + 1, 0)
                    query(i + 1, 1)
                turn_probs(i, 0)
                turn_probs(i, 1)
                if not is_last(i):
                    query(i + 1, 2)
                    query(i + 1, 3)
                context(i, 0)
                context(i, 1)
                if is_last(i):
                    turn_ffn(0)
                    turn_ffn(1)
                for c in range(KC):
                    if is_last(i) and c in (1, 2):
                        turn_ffn(c + 1)
                    output(i, c)
                    if c < 2:
                        context(i, c + 2)
                    if two_ahead:
                        turn(i + 2, c)

            over_tiles(pe, body, TAIL)
            receptance_ffn(0)
            receptance_ffn(1)

        @block.scalar
        def _(act):
            sc = nc.scalar

            def x_high(i, k):
                wait(act, turned, i * KC + k + 1)
                sc.activation(xt_hi[:, k, :], turn_bank(i, k)[:, :], ACT.Copy).then_inc(xhi_done, 1)

            def q_high(i, c):
                wait(act, q_proj, i * KC + c + 1)
                sc.activation(q_hi[:, c, :], bank[c % 2][:, :], ACT.Identity, bias=qb[:, c:c + 1]).then_inc(qhi_done, 1)

            def context_high(i, k):
                wait(act, ct_in, i * 16 + 16)
                wait(act, sc_done, i * SUB)
                sc.activation(ct_hi[:, k, :], ct[:, k, :], ACT.Copy).then_inc(cthi_done, 1)

            def context_high2(i, s):
                wait(act, cx_in, i * 16 + 16)
                wait(act, pc_done, i * KC)
                sc.activation(cx_hi[:, s, :], cx[:, s, :], ACT.Copy).then_inc(cxhi_done, 1)

            def ffn_high(m, k):
                act.wait_ge(sh.ffn_in, 16 * 4)
                if m != "r":
                    act.wait_ge(q_proj, NT * KC)
                sc.activation(ffn_slots(m)[0][:, k, :], ffn_slots(m)[1][:, k, :], ACT.Copy).then_inc(fwhi_done, 1)

            def exponent(i, s):
                wait(act, nb_done, i * SUB + s + 1)
                if s == 0:
                    wait(act, rinv_done, i)
                sc.activation(pr[:, s, :], pr[:, s, :], ACT.Exp, scale=SCALE, bias=nb[:, s:s + 1],
                              accum_out=rowsum[:, s:s + 1]).then_inc(exp_done, 1)

            def probs_high(i, b):
                wait(act, pt_done, i * BT + b + 1)
                sc.activation(pt_hi[:, b, :], bank[2 + b][:, :], ACT.Copy).then_inc(pthi_done, 1)

            def pc_high(i, c):
                wait(act, pc_done, i * KC + c + 1)
                sc.activation(pc_hi[:, c, :], bank[c % 2][:, :], ACT.Copy).then_inc(pchi_done, 1)

            def leave_ffn(k):
                act.wait_ge(sh.ffn_turned, k + 1)
                act.wait_ge(ctlo_done, NT * KC)
                act.wait_ge(cxlo_done, NT * SUB)
                sc.activation(sh.xt[:, k, :, 1:], bank[2 + k % 2][:, :].rearrange("p (b t) -> p b t", b=BT),
                              ACT.Copy).then_inc(sh.xt_left, 1)

            def mixed_high_ffn(k):
                act.wait_ge(sh.r_mixed, k + 1)
                act.wait_ge(sc_done, NT * SUB)
                sc.activation(sh.mr_hi[:, k, :], sh.mixed["r"][:, k, :], ACT.Copy).then_inc(sh.r_high, 1)

            def fold_high(n):
                act.wait_ge(fold_done, n // KC + 1)
                dst = (m_hi, l_hi)[n // KC][:, n % KC, :]
                sc.activation(dst, sh.bank[n][:, :], ACT.Copy).then_inc(mlhi_done, 1)

            for n in range(KC):
                fold_high(n)
            for k in range(KC):
                context_high(0, k)
            for k in range(KC):
                x_high(0, k)
            for n in range(KC):
                fold_high(KC + n)
            for c in range(KC):
                q_high(0, c)
                context_high2(0, c)
            for k in range(KC):
                x_high(1, k)

            def body(i):
                ahead = not is_last(i)
                two_ahead = not isinstance(i, int) or i < NT - TAIL
                for s in range(SUB):
                    exponent(i, s)
                if ahead:
                    q_high(i + 1, 0)
                    q_high(i + 1, 1)
                probs_high(i, 0)
                probs_high(i, 1)
                if ahead:
                    context_high(i + 1, 0)
                    q_high(i + 1, 2)
                    context_high(i + 1, 1)
                    context_high(i + 1, 2)
                    q_high(i + 1, 3)
                    context_high(i + 1, 3)
                for c in range(KC):
                    pc_high(i, c)
                    if not ahead and c == 1:
                        leave_ffn(0)
                    if c >= 2 and two_ahead:
                        x_high(i + 2, c - 2)
                    if ahead and not two_ahead:
                        for m in "rkv":
                            ffn_high(m, c)
                    if not ahead and c:
                        leave_ffn(c)
                        mixed_high_ffn(c - 1)
                if two_ahead:
                    x_high(i + 2, 2)
                    x_high(i + 2, 3)
                if ahead:
                    for s in range(SUB):
                        context_high2(i + 1, s)
                if not ahead:
                    mixed_high_ffn(KC - 1)

            over_tiles(act, body, TAIL)

        @block.vector
        def _(dve):
            ve = nc.vector

            def rest(out, src, high, done):
                ve.tensor_tensor(out, src, high.bitcast(F32), ALU.subtract).then_inc(done, 1)

            def x_rest(i, k):
                wait(dve, xhi_done, i * KC + k + 1)
                rest(xt_lo[:, k, :], turn_bank(i, k)[:, :], xt_hi[:, k, :], xlo_done)

            def q_rest(i, c):
                wait(dve, qhi_done, i * KC + c + 1)
                ve.scalar_tensor_tensor(out=q_lo[:, c, :], in0=bank[c % 2][:, :], scalar=qb[:, c:c + 1],
                                        in1=q_hi[:, c, :].bitcast(F32), op0=ALU.add,
                                        op1=ALU.subtract).then_inc(qlo_done, 1)

            def score(i, s):
                g = i * SUB + s
                wait(dve, sc_done, g + 1)
                if s == 0:
                    wait(dve, fs_in, i * 16 + 16)
                    wait(dve, rq_moved, i + 1)
                    wait(dve, pt_done, i * BT)
                ve.scalar_tensor_tensor(out=pr[:, s, :], in0=bank[s][:, 0:T], scalar=rq[:, s:s + 1],
                                        in1=fs[:, s, :], op0=ALU.add, op1=ALU.add).then_inc(sc_left, 1)
                wait(dve, sc_left, g + 1)
                wait(dve, nb_done, g)
                ve.reduce_max(mx[:, s:s + 1], pr[:, s, :], AX.X).then_inc(mx_done, 1)
                wait(dve, mx_done, g + 1)
                ve.tensor_scalar(nb[:, s:s + 1], mx[:, s:s + 1], -SCALE, None, ALU.mult).then_inc(nb_done, 1)

            def probs_rest(i, b):
                wait(dve, pthi_done, i * BT + b + 1)
                rest(pt_lo[:, b, :], bank[2 + b][:, :], pt_hi[:, b, :], ptlo_done)

            def pc_rest(i, c):
                wait(dve, pchi_done, i * KC + c + 1)
                rest(pc_lo[:, c, :], bank[c % 2][:, :], pc_hi[:, c, :], pclo_done)

            def inverse(i):
                wait(dve, exp_done, i * SUB + SUB)
                wait(dve, res_done, i * SUB)
                ve.reciprocal(rinv[:, :], rowsum[:, :]).then_inc(rinv_done, 1)

            def residual(i):
                wait(dve, out_done, i + 1)
                wait(dve, bo_added, i + 1)
                wait(dve, rinv_done, i + 1)
                for s in range(SUB):
                    ve.scalar_tensor_tensor(out=xres[:, s, :], in0=acc[s][:, :], scalar=rinv[:, s:s + 1],
                                            in1=xres[:, s, :], op0=ALU.mult, op1=ALU.add).then_inc(res_done, 1)

            def statistics(i, subs=range(SUB)):
                if 0 not in subs:
                    pass
                elif is_first(i):
                    dve.wait_ge(sh.x1_in, 16)
                elif isinstance(i, int) and i == NT:
                    dve.wait_ge(sh.x2_in, 16)
                else:
                    wait(dve, x_in, i * 16)
                for s in subs:
                    ve.bn_stats(stats[:, s, :], xin[:, s, :]).then_inc(st_done, 1)

            def aggregate():
                for s in range(SUB):
                    ve.bn_aggr(mv[:, s, :], stats[:, s, :]).then_inc(mv_done, 1)

            def normalise(i):
                wait(dve, rstd_done, i + 1)
                for s in range(SUB):
                    ve.tensor_scalar(xin[:, s, :], xin[:, s, :], mv[:, s, 0:1], rstd[:, s:s + 1],
                                     ALU.subtract, ALU.mult).then_inc(normed, 1)

            def row_products(i, subs=range(SUB)):
                for s in subs:
                    wait(dve, normed, i * SUB + s + 1)
                    wait(dve, rq_made, i * SUB + s)
                    wait(dve, rq_moved, i)
                    ve.tensor_tensor_reduce(out=row_product[:, :], in0=xin[:, s, :], in1=rk_row[:, :], scale=1.0,
                                            scalar=bqk[:, 0:1], op0=ALU.mult, op1=ALU.add,
                                            accum_out=rq_next[:, s:s + 1]).then_inc(rq_made, 1)

            def move_rq(i):
                wait(dve, rq_made, i * SUB + SUB)
                if not is_first(i):
                    wait(dve, sc_left, i * SUB)
                ve.tensor_copy(rq[:, :], rq_next[:, :]).then_inc(rq_moved, 1)

            def mix_ffn(k):
                as_seqs = lambda a: a.rearrange("p (b t) -> p b t", b=BT)
                dve.wait_ge(sh.xt_left, k + 1)
                dve.wait_ge(sh.margin, 1)
                dve.wait_ge(q_proj, NT * KC)
                ve.tensor_tensor(as_seqs(sh.diff[:, k, :]), sh.xt[:, k, :, 1:], sh.xt[:, k, :, 0:T],
                                 ALU.subtract).then_inc(sh.diffed, 1)
                dve.wait_ge(sh.diffed, k + 1)
                dve.wait_ge(sh.ffn_in, 16 * 4)
                ve.scalar_tensor_tensor(out=as_seqs(sh.mixed["r"][:, k, :]), in0=as_seqs(sh.diff[:, k, :]),
                                        scalar=sh.mu_sb[:, 0, k:k + 1], in1=sh.xt[:, k, :, 0:T],
                                        op0=ALU.mult, op1=ALU.add).then_inc(sh.r_mixed, 1)

            def mixed_rest_ffn(k):
                dve.wait_ge(sh.r_high, k + 1)
                ve.tensor_tensor(sh.mr_lo[:, k, :], sh.mixed["r"][:, k, :], sh.mr_hi[:, k, :].bitcast(F32),
                                 ALU.subtract).then_inc(sh.r_rest, 1)

            def fold_rest(n):
                dve.wait_ge(mlhi_done, n + 1)
                hi, lo = ((m_hi, m_lo), (l_hi, l_lo))[n // KC]
                rest(lo[:, n % KC, :], sh.bank[n][:, :], hi[:, n % KC, :], fold_left)

            statistics(0)
            dve.wait_ge(st_done, SUB)
            aggregate()
            for n in range(KC):
                fold_rest(n)
            normalise(0)
            row_products(0)
            for k in range(KC):
                x_rest(0, k)
            move_rq(0)
            for n in range(KC - 1):
                fold_rest(KC + n)
            q_rest(0, 0)
            fold_rest(2 * KC - 1)
            q_rest(0, 1)
            statistics(1)
            dve.wait_ge(st_done, 2 * SUB)
            aggregate()
            q_rest(0, 2)
            q_rest(0, 3)
            normalise(1)
            row_products(1, (0, 1))

            def body(i):
                ahead = not is_last(i)
                two_ahead = not isinstance(i, int) or i < NT - TAIL
                for s in range(SUB):
                    score(i, s)
                    if is_first(i) and s == 0:
                        x_rest(1, 0)
                        x_rest(1, 1)
                        row_products(1, (2, 3))
                        x_rest(1, 2)
                        x_rest(1, 3)
                if ahead:
                    move_rq(i + 1)
                    statistics(i + 2, (0, 1))
                    q_rest(i + 1, 0)
                    statistics(i + 2, (2, 3))
                    dve.wait_ge(st_done, i * SUB + 3 * SUB)
                    q_rest(i + 1, 1)
                    aggregate()
                inverse(i)
                probs_rest(i, 0)
                probs_rest(i, 1)
                if ahead:
                    q_rest(i + 1, 2)
                    q_rest(i + 1, 3)
                for c in range(KC):
                    pc_rest(i, c)
                    if c == 0 and ahead:
                        normalise(i + 2)
                    if c == 1 and two_ahead:
                        row_products(i + 2)
                    if c >= 2 and two_ahead:
                        x_rest(i + 2, c - 2)
                    if not ahead and c:
                        if c == 1:
                            mix_ffn(0)
                        mix_ffn(c)
                        mixed_rest_ffn(c - 1)
                if two_ahead:
                    x_rest(i + 2, 2)
                    x_rest(i + 2, 3)
                if not ahead:
                    mixed_rest_ffn(KC - 1)
                residual(i)

            over_tiles(dve, body, TAIL)
            dve.wait_ge(sh.x2_in, 32)
            for s in range(SUB):
                ve.bn_stats(stats[:, s, :], xin[:, s, :]).then_inc(sh.ffn_stats, 1)

        @block.gpsimd
        def _(pool):
            gp = nc.gpsimd

            def rstd_of(i):
                wait(pool, mv_done, i * SUB + SUB)
                wait(pool, normed, i * SUB)
                gp.tensor_tensor(rstd[:, :], mv[:, :, 1], eps[:, :], ALU.add).then_inc(veps_done, 1)
                wait(pool, veps_done, i + 1)
                gp.tensor_tensor(rstd[:, :], rstd[:, :], half[:, :], ALU.pow).then_inc(rstd_done, 1)

            def context_rest(i, k):
                wait(pool, cthi_done, i * KC + k + 1)
                gp.tensor_tensor(ct_lo[:, k, :], ct[:, k, :], ct_hi[:, k, :].bitcast(F32),
                                 ALU.subtract).then_inc(ctlo_done, 1)

            def context_rest2(i, s):
                wait(pool, cxhi_done, i * SUB + s + 1)
                gp.tensor_tensor(cx_lo[:, s, :], cx[:, s, :], cx_hi[:, s, :].bitcast(F32),
                                 ALU.subtract).then_inc(cxlo_done, 1)

            def ffn_rest(n, m, k):
                pool.wait_ge(fwhi_done, n + 1)
                hi, raw_m, lo = ffn_slots(m)
                last = gp.tensor_tensor(lo[:, k, :], raw_m[:, k, :], hi[:, k, :].bitcast(F32), ALU.subtract)
                if m == "r":
                    last.then_inc(sh.r_split, 1)

            def add_bias(i):
                wait(pool, res_in, i * 16 + 16)
                for s in range(SUB):
                    last = gp.tensor_tensor(xres[:, s, :], xres[:, s, :], out_row[:, :], ALU.add)
                last.then_inc(bo_added, 1)

            rstd_of(0)
            for k in range(KC):
                context_rest(0, k)
            context_rest2(0, 0)
            context_rest2(0, 1)
            rstd_of(1)
            context_rest2(0, 2)
            context_rest2(0, 3)
            pool.wait_ge(fold_left, NFOLD)

            def body(i):
                if not is_last(i):
                    rstd_of(i + 2)
                    for k in range(KC):
                        context_rest(i + 1, k)
                add_bias(i)
                if not is_last(i):
                    for s in range(SUB):
                        context_rest2(i + 1, s)
                    if isinstance(i, int) and i == NT - TAIL:
                        for k in range(KC):
                            for n, m in enumerate("rkv"):
                                ffn_rest(3 * k + n, m, k)
                        pool.wait_ge(ctlo_done, NT * KC)
                        pool.wait_ge(cxlo_done, NT * SUB)
                        gp.memset(sh.xt[:, :, :, 0:1], 0.0).then_inc(sh.margin, 1)

            over_tiles(pool, body, TAIL)


def ffn_pass(nc, sh, x2, x3):
    with ExitStack() as ctx:
        def sb(name, shape, dt=F32):
            return ctx.enter_context(nc.sbuf_tensor("c_" + name, shape, dt))

        def sem(name):
            return ctx.enter_context(nc.semaphore("c_" + name))

        WM = "rkv"
        w_hi, w_lo = sh.ffn_hi, sh.ffn_lo
        mu_sb, id_sb, xin, xres, stats, mv, rstd, half, eps = (
            sh.mu_sb, sh.id_sb, sh.xin, sh.xres, sh.stats, sh.mv, sh.rstd, sh.half, sh.eps)
        xt, diff, mixed = sh.xt, sh.diff, sh.mixed
        m_hi = {"r": sh.mr_hi, "k": sb("mixed_k_hi", [P, KC, N], F32R)}
        m_lo = {"r": sh.mr_lo, "k": sb("mixed_k_lo", [P, KC, N], F32R)}
        gate, grec = sb("gate", [P, SUB, C]), sb("grec", [P, SUB, C])
        ka = sb("ka", [P, 2, N])
        k_hi, k_lo = sb("k_hi", [P, KC, N], F32R), sb("k_lo", [P, KC, N], F32R)
        seqs = lambda a: a.rearrange("p (b t) -> p b t", b=BT)

        bank, acc = sh.bank[:4], sh.bank[4:]

        x_in, res_in, stored = sh.x2_in, sem("res_in"), sem("stored")
        turned, r_proj, k_proj, v_done = sh.ffn_turned, sh.r_proj, sem("k_proj"), sem("v_done")
        xt_left = sh.xt_left
        e_exp, ln_done, rc_done, relu_done, square_done, khi_done, klo_done = (
            sem(n) for n in ("e_exp", "ln_done", "rc_done", "relu_done", "square_done", "khi_done", "klo_done"))
        diffed = sh.diffed
        mix_done = {"r": sh.r_mixed, "k": sem("mix_done_k")}
        mhi_done = {"r": sh.r_high, "k": sem("mhi_done_k")}
        mlo_done = {"r": sh.r_rest, "k": sem("mlo_done_k")}
        capped, rd_done, newton, gated, res_done, odd_res = (
            sem(n) for n in ("capped", "rd_done", "newton", "gated", "res_done", "odd_res"))
        st_done = sh.ffn_stats
        mv_done, normed, veps_done, rstd_done = (sem(n) for n in ("mv_done", "normed", "veps_done", "rstd_done"))

        TAIL = 2
        block = ctx.enter_context(nc.Block())

        @block.sync
        def _(sp):
            sp.wait_ge(sh.x2_stored, 16 * NT)
            sp.dma_start(xres[:, :, :], tile_of(x2, 0)).then_inc(res_in, 16)

            def body(i):
                if not isinstance(i, int) or i < NT - TAIL:
                    sp.wait_ge(turned, i * KC + 2 * KC)
                    sp.dma_start(xin[:, :, :], tile_of(x2, i + 2)).then_inc(x_in, 16)
                if is_last(i):
                    for s in range(SUB):
                        if s % 2:
                            sp.wait_ge(odd_res, s // 2 + 1)
                        else:
                            sp.wait_ge(res_done, i * SUB + s // 2 + 1)
                        sp.dma_start(tile_of(x3, i)[:, s:s + 1, :], xres[:, s:s + 1, :]).then_inc(stored, 16)
                    sp.wait_ge(stored, (NT - 1 + SUB) * 16)
                else:
                    sp.wait_ge(res_done, i * SUB + SUB)
                    sp.dma_start(tile_of(x3, i), xres[:, :, :]).then_inc(stored, 16)
                    sp.wait_ge(stored, i * 16 + 16)
                    sp.dma_start(xres[:, :, :], tile_of(x2, i + 1)).then_inc(res_in, 16)

            over_tiles(sp, body, TAIL)

        @block.tensor
        def _(pe):
            te = nc.tensor

            def cut(a, k, j):
                return a[:, k, j * P:(j + 1) * P]

            def turn(i, k):
                wait(pe, normed, i * SUB)
                wait(pe, xt_left, i * KC + k - 1)
                for s in range(SUB):
                    last = te.transpose(bank[2 + k % 2][:, s * P:(s + 1) * P], xin[:, s, k * P:(k + 1) * P],
                                        id_sb[:, :])
                last.then_inc(turned, 1)

            def receptance(i, s):
                if s == 0:
                    wait(pe, mlo_done["r"], i * KC + KC)
                if s >= 2:
                    wait(pe, capped, i * SUB + s - 1)
                else:
                    wait(pe, relu_done, (i - 1) * KC + 3 + s)
                three(te, bank[s % 2][:, :],
                      [((cut(m_hi["r"], k, s), cut(m_lo["r"], k, s)), (w_hi["r"][:, k, :], w_lo["r"][:, k, :]))
                       for k in range(KC)]).then_inc(r_proj, 1)

            def key(i, c):
                def split(k):
                    pe.wait_ge(mlo_done["k"], i * KC + k + 1)

                if c >= 2:
                    wait(pe, relu_done, i * KC + c - 1)
                else:
                    wait(pe, capped, i * SUB + 3 + c)
                three(te, bank[c % 2][:, :],
                      [((cut(w_hi["k"], k, c), cut(w_lo["k"], k, c)), (m_hi["k"][:, k, :], m_lo["k"][:, k, :]))
                       for k in range(KC)], split if c == 0 else None).then_inc(k_proj, 1)

            def value(i, c, subs=range(SUB)):
                wait(pe, klo_done, i * KC + c + 1)
                if c == 0:
                    wait(pe, gated, i * SUB)
                for s in subs:
                    for a, b in ((k_hi, w_hi["v"]), (k_hi, w_lo["v"]), (k_lo, w_hi["v"])):
                        last = te.matmul(acc[s][:, :], cut(a, c, s), b[:, c, :],
                                         start=(c == 0 and a is k_hi and b is w_hi["v"]),
                                         stop=(c == KC - 1 and a is k_lo))
                if c == KC - 1:
                    last.then_inc(v_done, 1)

            def body(i):
                for s in range(2 if is_first(i) else 0, SUB):
                    receptance(i, s)
                for c in range(KC):
                    key(i, c)
                    if not is_last(i):
                        turn(i + 1, c)
                if is_last(i):
                    value(i, 0)
                    for s in range(SUB):
                        for c in range(1, KC):
                            value(i, c, (s,))
                    return
                for c in range(KC):
                    value(i, c)

            over_tiles(pe, body, TAIL)

        @block.scalar
        def _(act):
            sc = nc.scalar

            def leave(i, k):
                wait(act, turned, i * KC + k + 1)
                for m in "rk":
                    wait(act, mix_done[m], (i - 1) * KC + k + 1)
                sc.activation(xt[:, k, :, 1:], seqs(bank[2 + k % 2][:, :]), ACT.Copy).then_inc(xt_left, 1)

            def mixed_high(m, i, k):
                wait(act, mix_done[m], i * KC + k + 1)
                if k == 0:
                    wait(act, {"r": r_proj, "k": k_proj}[m], i * KC)
                sc.activation(m_hi[m][:, k, :], mixed[m][:, k, :], ACT.Copy).then_inc(mhi_done[m], 1)

            def exp_r(i, s):
                wait(act, capped, i * SUB + s + 1)
                sc.activation(gate[:, s, :], gate[:, s, :], ACT.Exp, scale=-1.0).then_inc(e_exp, 1)

            def first_reciprocal(i, s):
                wait(act, e_exp, i * SUB + s + 1)
                wait(act, res_done, (i - 1) * SUB + s + 1)
                sc.activation(grec[:, s, :], gate[:, s, :], ACT.Ln, bias=1.0).then_inc(ln_done, 1)
                wait(act, ln_done, i * SUB + s + 1)
                sc.activation(grec[:, s, :], grec[:, s, :], ACT.Exp, scale=-1.0).then_inc(rc_done, 1)

            def relu_square(i, c):
                g = i * KC + c
                wait(act, k_proj, g + 1)
                wait(act, klo_done, g - 1)
                sc.activation(ka[:, c % 2, :], bank[c % 2][:, :], ACT.Relu).then_inc(relu_done, 1)
                wait(act, relu_done, g + 1)
                sc.activation(ka[:, c % 2, :], ka[:, c % 2, :], ACT.Square).then_inc(square_done, 1)
                wait(act, square_done, g + 1)
                if c == 0:
                    wait(act, v_done, i)
                sc.activation(k_hi[:, c, :], ka[:, c % 2, :], ACT.Copy).then_inc(khi_done, 1)

            for k in range(KC):
                mixed_high("k", 0, k)

            def body(i):
                for s in range(SUB):
                    exp_r(i, s)
                    if s:
                        first_reciprocal(i, s - 1)
                for c in range(KC):
                    relu_square(i, c)
                    if not is_last(i):
                        leave(i + 1, c)
                    if c == 0:
                        first_reciprocal(i, SUB - 1)
                if not is_last(i):
                    for m in "rk":
                        for k in range(KC):
                            mixed_high(m, i + 1, k)

            over_tiles(act, body, TAIL)

        @block.vector
        def _(dve):
            ve = nc.vector

            def statistics(i):
                wait(dve, x_in, i * 16 + 16)
                for s in range(SUB):
                    ve.bn_stats(stats[:, s, :], xin[:, s, :]).then_inc(st_done, 1)

            def aggregate():
                for s in range(SUB):
                    ve.bn_aggr(mv[:, s, :], stats[:, s, :]).then_inc(mv_done, 1)

            def normalise(i):
                wait(dve, rstd_done, i)
                for s in range(SUB):
                    ve.tensor_scalar(xin[:, s, :], xin[:, s, :], mv[:, s, 0:1], rstd[:, s:s + 1],
                                     ALU.subtract, ALU.mult).then_inc(normed, 1)

            def mix(m, i, k):
                wait(dve, diffed, i * KC + k + 1)
                wait(dve, mhi_done[m], (i - 1) * KC + k + 1)
                wait(dve, mlo_done[m], (i - 1) * KC + k + 1)
                ve.scalar_tensor_tensor(out=seqs(mixed[m][:, k, :]), in0=seqs(diff[:, k, :]),
                                        scalar=mu_sb[:, "rk".index(m), k:k + 1], in1=xt[:, k, :, 0:T],
                                        op0=ALU.mult, op1=ALU.add).then_inc(mix_done[m], 1)

            def mixed_rest(m, i, k):
                wait(dve, mhi_done[m], i * KC + k + 1)
                ve.tensor_tensor(m_lo[m][:, k, :], mixed[m][:, k, :], m_hi[m][:, k, :].bitcast(F32),
                                 ALU.subtract).then_inc(mlo_done[m], 1)

            def cap(i, s):
                wait(dve, r_proj, i * SUB + s + 1)
                ve.tensor_scalar(gate[:, s, :], bank[s % 2][:, :], -math.log(SIG_CAP), None,
                                 ALU.max).then_inc(capped, 1)

            def k_rest(i, c):
                wait(dve, khi_done, i * KC + c + 1)
                ve.tensor_tensor(k_lo[:, c, :], ka[:, c % 2, :], k_hi[:, c, :].bitcast(F32),
                                 ALU.subtract).then_inc(klo_done, 1)

            def refine(i, s):
                wait(dve, rc_done, i * SUB + s + 1)
                ve.scalar_tensor_tensor(out=gate[:, s, :], in0=gate[:, s, :], scalar=1.0, in1=grec[:, s, :],
                                        op0=ALU.add, op1=ALU.mult).then_inc(rd_done, 1)
                wait(dve, rd_done, i * SUB + s + 1)
                ve.scalar_tensor_tensor(out=grec[:, s, :], in0=gate[:, s, :], scalar=-2.0, in1=grec[:, s, :],
                                        op0=ALU.add, op1=ALU.mult).then_inc(newton, 1)

            def residual(i):
                wait(dve, v_done, i + 1)
                wait(dve, newton, i * SUB + SUB)
                for s in range(SUB):
                    if is_last(i) and s:
                        dve.wait_ge(v_done, NT + s)
                    ve.scalar_tensor_tensor(out=grec[:, s, :], in0=acc[s][:, :], scalar=-1.0, in1=grec[:, s, :],
                                            op0=ALU.mult, op1=ALU.mult).then_inc(gated, 1)

            cap(0, 0)
            cap(0, 1)
            dve.wait_ge(st_done, SUB)
            aggregate()
            for k in range(KC):
                mix("k", 0, k)
            normalise(1)

            def body(i):
                ahead = not is_last(i)
                for s in range(SUB):
                    if s >= 2 or not is_first(i):
                        cap(i, s)
                    if s == 1 and ahead and not is_first(i):
                        aggregate()
                    if s == 2 and ahead and not is_first(i):
                        normalise(i + 1)
                    if s >= 2:
                        refine(i, s - 2)
                for c in range(KC):
                    k_rest(i, c)
                    if ahead:
                        mix("r", i + 1, c)
                        mix("k", i + 1, c)
                    if c < 2:
                        refine(i, c + 2)
                if ahead:
                    for k in range(KC):
                        mixed_rest("r", i + 1, k)
                if not isinstance(i, int) or i < NT - TAIL:
                    statistics(i + 2)
                    dve.wait_ge(st_done, i * SUB + 2 * SUB)
                residual(i)

            over_tiles(dve, body, TAIL)
            dve.wait_ge(res_in, NT * 16)
            for s in (1, 3):
                dve.wait_ge(gated, (NT - 1) * SUB + s + 1)
                ve.tensor_tensor(xres[:, s, :], xres[:, s, :], grec[:, s, :], ALU.add).then_inc(odd_res, 1)

        @block.gpsimd
        def _(pool):
            gp = nc.gpsimd

            def rstd_of(i):
                wait(pool, mv_done, i * SUB)
                wait(pool, normed, (i - 1) * SUB)
                gp.tensor_tensor(rstd[:, :], mv[:, :, 1], eps[:, :], ALU.add).then_inc(veps_done, 1)
                wait(pool, veps_done, i)
                gp.tensor_tensor(rstd[:, :], rstd[:, :], half[:, :], ALU.pow).then_inc(rstd_done, 1)

            def difference(i, k):
                wait(pool, xt_left, i * KC + k + 1)
                wait(pool, mix_done["k"], (i - 1) * KC + k + 1)
                gp.tensor_tensor(seqs(diff[:, k, :]), xt[:, k, :, 1:], xt[:, k, :, 0:T],
                                 ALU.subtract).then_inc(diffed, 1)

            def mixed_rest(m, i, k):
                wait(pool, mhi_done[m], i * KC + k + 1)
                gp.tensor_tensor(m_lo[m][:, k, :], mixed[m][:, k, :], m_hi[m][:, k, :].bitcast(F32),
                                 ALU.subtract).then_inc(mlo_done[m], 1)

            def add(i, subs=range(SUB)):
                wait(pool, res_in, i * 16 + 16)
                for s in subs:
                    wait(pool, gated, i * SUB + s + 1)
                    gp.tensor_tensor(xres[:, s, :], xres[:, s, :], grec[:, s, :], ALU.add).then_inc(res_done, 1)

            rstd_of(1)
            for k in range(KC):
                mixed_rest("k", 0, k)

            def body(i):
                if not is_last(i) and not is_first(i):
                    rstd_of(i + 1)
                if not is_first(i):
                    add(i - 1)
                if not is_last(i):
                    for c in range(KC):
                        difference(i + 1, c)
                    for k in range(KC):
                        mixed_rest("k", i + 1, k)

            over_tiles(pool, body, TAIL)
            add(NT - 1, (0, 2))


def decoder(nc, a, out):
    x1 = nc.dram_tensor("x_after_attention", (B, T, C), F32, kind="Internal").ap()
    x2 = nc.dram_tensor("x_after_cross", (B, T, C), F32, kind="Internal").ap()
    with ExitStack() as ctx:
        sh = Shared(nc, ctx)
        attention_pass(nc, sh, a["x"], {m: a["w_" + m] for m in "kvr"}, a["wo_t"], a["cols"], a["bo_b"], a["trem"],
                       a["scanmask"], a["ident"], x1,
                       dict(wq=a["xwq"], wk=a["xwk"], wv=a["xwv"], wo=a["xwo"], biases=a["xbias"], bo=a["xbo_b"]))
        cross_pass(nc, sh, x1, a["ctx"], a["ctx_t"], a["fside"], x2,
                   dict(r=a["fr"], k=a["fk"], v=a["fv"], mu=a["mu"]))
        ffn_pass(nc, sh, x2, out)


def layouts(inp):
    import numpy as np

    def chunks_of(w, n):
        a = np.asarray(w).reshape(n, P, w.shape[1] // P, P)
        return np.ascontiguousarray(a.transpose(0, 3, 2, 1)).reshape(n, P, -1)

    def rows(w):
        return np.ascontiguousarray(np.asarray(w).reshape(KC, P, C).transpose(1, 0, 2))

    def columns(names, n):
        return np.ascontiguousarray(np.stack([np.asarray(inp[m]).reshape(n, P).T for m in names], 1))

    def on_all(v):
        return np.ascontiguousarray(np.broadcast_to(np.asarray(v), (P, len(v))))

    out = {"x": np.asarray(inp["x"]), "ctx": np.asarray(inp["ctx_1024"]), "fside": np.asarray(inp["fside_BxSxS2_0"])}
    out["ctx_t"] = np.ascontiguousarray(
        out["ctx"].reshape(NT, BT, T, KC, P).transpose(0, 4, 3, 1, 2)).reshape(NT, P, KC, N)
    for m in "kvr":
        out["w_" + m] = chunks_of(inp[f"L0_attn_W{m}"], HC)
    out["wo_t"] = np.ascontiguousarray(np.asarray(inp["L0_attn_Wo"]).T).reshape(HC, P, C)
    out["cols"] = columns(["L0_attn_" + n for n in ("br", "bk", "bv", "time_decay", "U")], HC)
    out["bo_b"] = on_all(inp["L0_attn_bo"])
    for m in "qkv":
        out["xw" + m] = rows(inp[f"L0_xattn_W{m}"])
    out["xwo"] = rows(np.asarray(inp["L0_xattn_Wo"]).T)
    out["xbias"] = columns(["L0_xattn_bq", "L0_xattn_bk", "L0_xattn_bv"], KC)
    out["xbo_b"] = on_all(inp["L0_xattn_bo"])
    for m in "rkv":
        out["f" + m] = rows(np.asarray(inp[f"L0_ffn_W_{m}"]).T)
    out["mu"] = columns(["L0_ffn_mu_r", "L0_ffn_mu_k"], KC)
    out["trem"] = np.ascontiguousarray(np.broadcast_to(np.arange(T - 1, -1, -1, dtype=np.float32), (P, T)))
    mask = np.ones((P, BT, T + 1), np.float32)
    mask[:, :, 0] = 0
    out["scanmask"] = mask.reshape(P, -1)
    out["ident"] = np.eye(P, dtype=np.float32)
    return out


def kernel(**inputs):
    import concourse.bacc as bacc
    from concourse.bass_utils import run_bass_kernel_spmd

    nc = bacc.Bacc("TRN2", target_bir_lowering=False, num_devices=1)
    arrays, args = {}, {}
    for name, a in layouts(inputs).items():
        arrays[f"in_{name}"] = a
        args[name] = nc.dram_tensor(f"in_{name}", a.shape, mybir.dt.from_np(a.dtype), kind="ExternalInput").ap()
    out = nc.dram_tensor("out_x", (B, T, C), F32, kind="ExternalOutput").ap()
    decoder(nc, args, out)
    r = run_bass_kernel_spmd(nc, [arrays], core_ids=[0])
    return r.results[0]["out_x"]
```
